# Optimizing a Trainium2 kernel written in Bass

```python
import numpy as np
import jax
import jax.numpy as jnp

def _softmax(x, axis=-1):
    return jax.nn.softmax(x, axis=axis)

def _gelu(x):
    return jax.nn.gelu(x, approximate=True)

def _silu(x):
    return jax.nn.silu(x)

def _sigmoid(x):
    return jax.nn.sigmoid(x)

def _layernorm(x, axis=-1, eps=1e-05):
    m = jnp.mean(x, axis=axis, keepdims=True)
    v = jnp.var(x, axis=axis, keepdims=True)
    return (x - m) / jnp.sqrt(v + eps)

def _scatter_add(tgt, idx, src, axis=0):
    return tgt.at[idx].add(src)

def _segment_sum(src, seg, n):
    return jax.ops.segment_sum(src, seg, n)
kernel_name = 'mk_sandwich_d1_jaxref_r8_ee4014'

def setup_inputs(seed: int=0):
    np.random.seed(seed)
    _w = jnp.asarray

    def _L0_attn_setup():
        import jax, jax.numpy as jnp
        import numpy as np
        DIM = 128
        HEADS = 16
        HEAD_DIM = DIM // HEADS

        def _xavier(key, shape):
            fan_out, fan_in = shape
            limit = float(np.sqrt(6.0 / (fan_in + fan_out)))
            return jax.random.uniform(key, shape, jnp.float32, -limit, limit)
        key = jax.random.key(seed)
        kx, kv, kk, kq = jax.random.split(key, 4)
        x = jax.random.normal(kx, (4, 256, DIM), jnp.float32)
        Wv = _xavier(kv, (DIM, DIM))
        Wk = _xavier(kk, (DIM, DIM))
        Wq = _xavier(kq, (DIM, DIM))
        return {'x': x, 'Wq': Wq, 'Wk': Wk, 'Wv': Wv}
    _L0_attn_in = _L0_attn_setup()

    def _L0_ffn_setup():
        import jax, jax.numpy as jnp
        import numpy as np
        B, S, D, H, M, E, K = (4, 128, 128, 16, 2, 8, 2)
        KD = D // H
        F = 2 * D
        EPS = 1e-06

        def _ln(x, g, b):
            m = jnp.mean(x, axis=-1, keepdims=True)
            v = jnp.mean(jnp.square(x - m), axis=-1, keepdims=True)
            return (x - m) * jax.lax.rsqrt(v + EPS) * g + b
        key = jax.random.key(seed)
        ks = jax.random.split(key, 12)
        r = lambda i, shape: jax.random.normal(ks[i], shape, jnp.float32) * 0.02
        return {'x': jax.random.normal(ks[0], (B, S, D), jnp.float32), 'ln1_g': jnp.ones((D,), jnp.float32), 'ln1_b': jnp.zeros((D,), jnp.float32), 'ln2_g': jnp.ones((D,), jnp.float32), 'ln2_b': jnp.zeros((D,), jnp.float32), 'mha_wq': r(1, (M, D, H, KD)), 'mha_bq': jnp.zeros((M, H, KD), jnp.float32), 'mha_wk': r(2, (M, D, H, KD)), 'mha_bk': jnp.zeros((M, H, KD), jnp.float32), 'mha_wv': r(3, (M, D, H, KD)), 'mha_bv': jnp.zeros((M, H, KD), jnp.float32), 'mha_wo': r(4, (M, H, KD, D)), 'mha_bo': jnp.zeros((M, D), jnp.float32), 'mha_rw': r(5, (D, M)), 'mha_rb': jnp.zeros((M,), jnp.float32), 'ffn_rw': r(6, (D, E)), 'ffn_rb': jnp.zeros((E,), jnp.float32), 'fw1': r(7, (E, D, F)), 'fw2': r(8, (E, F, D))}
    _L0_ffn_in = _L0_ffn_setup()
    _d = {'L0_attn_x': _L0_attn_in['x'], 'L0_attn_Wq': _L0_attn_in['Wq'], 'L0_attn_Wk': _L0_attn_in['Wk'], 'L0_attn_Wv': _L0_attn_in['Wv'], 'L0_ffn_ln1_g': _L0_ffn_in['ln1_g'], 'L0_ffn_ln1_b': _L0_ffn_in['ln1_b'], 'L0_ffn_ln2_g': _L0_ffn_in['ln2_g'], 'L0_ffn_ln2_b': _L0_ffn_in['ln2_b'], 'L0_ffn_mha_wq': _L0_ffn_in['mha_wq'], 'L0_ffn_mha_bq': _L0_ffn_in['mha_bq'], 'L0_ffn_mha_wk': _L0_ffn_in['mha_wk'], 'L0_ffn_mha_bk': _L0_ffn_in['mha_bk'], 'L0_ffn_mha_wv': _L0_ffn_in['mha_wv'], 'L0_ffn_mha_bv': _L0_ffn_in['mha_bv'], 'L0_ffn_mha_wo': _L0_ffn_in['mha_wo'], 'L0_ffn_mha_bo': _L0_ffn_in['mha_bo'], 'L0_ffn_mha_rw': _L0_ffn_in['mha_rw'], 'L0_ffn_mha_rb': _L0_ffn_in['mha_rb'], 'L0_ffn_ffn_rw': _L0_ffn_in['ffn_rw'], 'L0_ffn_ffn_rb': _L0_ffn_in['ffn_rb'], 'L0_ffn_fw1': _L0_ffn_in['fw1'], 'L0_ffn_fw2': _L0_ffn_in['fw2']}
    _x0 = _d['L0_attn_x']
    _d['L0_attn_x'] = jax.random.normal(jax.random.fold_in(jax.random.key(seed), 1), (16, 256, 128), dtype=_x0.dtype)
    del _x0
    return _d

def reference(L0_attn_x, L0_attn_Wq, L0_attn_Wk, L0_attn_Wv, L0_ffn_ln1_g, L0_ffn_ln1_b, L0_ffn_ln2_g, L0_ffn_ln2_b, L0_ffn_mha_wq, L0_ffn_mha_bq, L0_ffn_mha_wk, L0_ffn_mha_bk, L0_ffn_mha_wv, L0_ffn_mha_bv, L0_ffn_mha_wo, L0_ffn_mha_bo, L0_ffn_mha_rw, L0_ffn_mha_rb, L0_ffn_ffn_rw, L0_ffn_ffn_rb, L0_ffn_fw1, L0_ffn_fw2):

    def _L0_attn_ref(x, Wq, Wk, Wv):
        import jax, jax.numpy as jnp
        import numpy as np
        DIM = 128
        HEADS = 16
        HEAD_DIM = DIM // HEADS

        def _xavier(key, shape):
            fan_out, fan_in = shape
            limit = float(np.sqrt(6.0 / (fan_in + fan_out)))
            return jax.random.uniform(key, shape, jnp.float32, -limit, limit)
        B, S, D = x.shape
        H, Hd = (HEADS, HEAD_DIM)
        q = (x @ Wq.T).reshape(B, S, H, Hd)
        k = (x @ Wk.T).reshape(B, S, H, Hd)
        v = (x @ Wv.T).reshape(B, S, H, Hd)
        energy = jnp.einsum('bqhd,bkhd->bhqk', q, k)
        attn = jax.nn.softmax(energy / jnp.sqrt(jnp.float32(D)), axis=-1)
        out = jnp.einsum('bhqk,bkhd->bqhd', attn, v).reshape(B, S, D)
        return out

    def _L0_ffn_ref(x, ln1_g, ln1_b, ln2_g, ln2_b, mha_wq, mha_bq, mha_wk, mha_bk, mha_wv, mha_bv, mha_wo, mha_bo, mha_rw, mha_rb, ffn_rw, ffn_rb, fw1, fw2):
        import jax, jax.numpy as jnp
        import numpy as np
        B, S, D, H, M, E, K = (4, 128, 128, 16, 2, 8, 2)
        KD = D // H
        F = 2 * D
        EPS = 1e-06

        def _ln(x, g, b):
            m = jnp.mean(x, axis=-1, keepdims=True)
            v = jnp.mean(jnp.square(x - m), axis=-1, keepdims=True)
            return (x - m) * jax.lax.rsqrt(v + EPS) * g + b
        n1 = _ln(x, ln1_g, ln1_b)
        mha_probs = jax.nn.softmax(jnp.mean(n1, axis=1) @ mha_rw + mha_rb, axis=-1)
        q = jnp.einsum('btd,mdhk->mbhtk', n1, mha_wq) + mha_bq[:, None, :, None, :]
        kk = jnp.einsum('btd,mdhk->mbhtk', n1, mha_wk) + mha_bk[:, None, :, None, :]
        v = jnp.einsum('btd,mdhk->mbhtk', n1, mha_wv) + mha_bv[:, None, :, None, :]
        scores = jnp.einsum('mbhtk,mbhsk->mbhts', q, kk) / jnp.sqrt(jnp.float32(KD))
        attn = jax.nn.softmax(scores, axis=-1)
        ctx = jnp.einsum('mbhts,mbhsk->mbthk', attn, v)
        mha_out = jnp.einsum('mbthk,mhkd->mbtd', ctx, mha_wo) + mha_bo[:, None, None, :]
        x = x + jnp.einsum('mbtd,bm->btd', mha_out, mha_probs)
        n2 = _ln(x, ln2_g, ln2_b)
        ffn_probs = jax.nn.softmax(jnp.mean(n2, axis=1) @ ffn_rw + ffn_rb, axis=-1)
        topk_p, topk_i = jax.lax.top_k(ffn_probs, K)
        topk_p = topk_p / jnp.sum(topk_p, axis=-1, keepdims=True)
        sw1 = fw1[topk_i]
        sw2 = fw2[topk_i]
        h = jax.nn.gelu(jnp.einsum('btd,bkdf->bktf', n2, sw1), approximate=False)
        eo = jnp.einsum('bktf,bkfd->bktd', h, sw2)
        return x + jnp.einsum('bktd,bk->btd', eo, topk_p)
    x = L0_attn_x
    x = x + _layernorm(_L0_attn_ref(_layernorm(x, axis=-1), L0_attn_Wq, L0_attn_Wk, L0_attn_Wv), axis=-1)
    x = x + _layernorm(_L0_ffn_ref(_layernorm(x, axis=-1), L0_ffn_ln1_g, L0_ffn_ln1_b, L0_ffn_ln2_g, L0_ffn_ln2_b, L0_ffn_mha_wq, L0_ffn_mha_bq, L0_ffn_mha_wk, L0_ffn_mha_bk, L0_ffn_mha_wv, L0_ffn_mha_bv, L0_ffn_mha_wo, L0_ffn_mha_bo, L0_ffn_mha_rw, L0_ffn_mha_rb, L0_ffn_ffn_rw, L0_ffn_ffn_rb, L0_ffn_fw1, L0_ffn_fw2), axis=-1)
    return x

_drawn_inputs = setup_inputs


def setup_inputs(seed=0):
    import zlib

    import numpy as np

    out = dict(_drawn_inputs(seed))
    spreads = {'L0_ffn_ln1_g': (1.0, 0.6),
     'L0_ffn_ln1_b': (0.0, 0.8),
     'L0_ffn_ln2_g': (1.0, 0.6),
     'L0_ffn_ln2_b': (0.0, 0.8),
     'L0_ffn_mha_bq': (0.0, 0.8),
     'L0_ffn_mha_bk': (0.0, 0.8),
     'L0_ffn_mha_bv': (0.0, 0.8),
     'L0_ffn_mha_bo': (0.0, 0.28),
     'L0_ffn_mha_rb': (0.0, 0.8),
     'L0_ffn_ffn_rb': (0.0, 0.701)}
    factors = {'L0_ffn_mha_wq': 8.0,
     'L0_ffn_mha_wk': 8.0,
     'L0_ffn_mha_wv': 5.63,
     'L0_ffn_mha_wo': 4.498,
     'L0_ffn_mha_rw': 8.0,
     'L0_ffn_ffn_rw': 6.65,
     'L0_ffn_fw1': 5.054,
     'L0_ffn_fw2': 4.964}
    for name, (base, spread) in spreads.items():
        noise = np.random.default_rng([zlib.crc32(name.encode()), seed]).standard_normal(out[name].shape)
        drawn = base * np.exp(spread * noise) if base else spread * noise
        out[name] = jnp.asarray(drawn.astype(out[name].dtype))
    for name, factor in factors.items():
        out[name] = (out[name] * factor).astype(out[name].dtype)
    return out
```

```python
from contextlib import ExitStack

import concourse.bass as bass
from concourse import mybir

ALU = mybir.AluOpType
ACT = mybir.ActivationFunctionType
F32 = mybir.dt.float32
BF16 = mybir.dt.bfloat16
U32 = mybir.dt.uint32
AX_X = mybir.AxisListType.X

NB, T, D = 16, 256, 128
H, KD = 16, 8
QT = T // 128
F, NE, TOPK, NM = 256, 8, 2, 2
FC = F // 128
EPS_OUTER, EPS_INNER = 1e-5, 1e-6
HALF = H // 2
VW = 32
SHIFT = 126
Q_PARTS = (0, 1, 2, 0, 1, 0)
K_PARTS = (0, 0, 0, 1, 1, 2)

KINDS = ("A", "B0", "B1")
FIRST_STEP, LAST_STEP = -4, 16
LOOP_STEPS = (1, 12)

INSTANCES = [("A", 0), ("A", 1), ("A", 2)]
for _k in range(NB):
    INSTANCES += [("B0", _k), ("B1", _k)] + ([("A", _k + 3)] if _k + 3 < NB else [])
PLACE = {inst: n for n, inst in enumerate(INSTANCES)}

TENSOR_WORK = {
    "B0": [(1, "shift1", "B0", 0, "Y"), (2, "mix", "B", -1, "X"), (4, "project", "B0", 1, "Y"), (6, "turn1", "A", 2, "X"),
           (7, "route", "A", 1, "Y"), (8, "values", "A", 3, "Y"), (10, "shift0", "B1", 0, "Y"), (14, "turn0", "B0", 0, "X")],
    "B1": [(1, "shift1", "B1", 0, "Y"), (4, "project", "B1", 1, "Y"), (6, "turn1", "B0", 0, "X"),
           (8, "values", "B0", 1, "Y"), (9, "norm2", "B", -1, "X"), (10, "shift0", "A", 3, "Y"), (11, "context", "B0", 0, "X"),
           (14, "turn0", "B1", 0, "X")],
    "A": [(1, "shift1", "A", 3, "Y"), (2, "norm_x", "A", 4, "X"), (5, "project", "A", 4, "Y"), (6, "turn1", "B1", 0, "X"),
          (8, "values", "B1", 1, "Y"), (10, "shift0", "B0", 1, "Y"), (11, "context", "B1", 0, "X"),
          (12, "norm1", "A", 2, "Y"), (14, "turn0", "A", 3, "X")],
}
SLOTS = {"B0": (("B0", 0), ("B1", 0)), "B1": (("B1", 0), ("A", 3)), "A": (("A", 3), ("B0", 1))}


def known(k):
    return isinstance(k, int)


def real(k, off):
    return not known(k) or 0 <= k + off < NB


def place(kind, k, off):
    if known(k):
        return PLACE[(kind, k + off)]
    return 3 * k + 3 * off + {"A": -4, "B0": 3, "B1": 4}[kind]


def ring3(kind, k, off):
    return PLACE[(kind, k + off)] % 3 if known(k) else {"A": 2, "B0": 0, "B1": 1}[kind]


def turn3(kind, k, off):
    return PLACE[(kind, k + off)] // 3 if known(k) else k + off + {"A": -2, "B0": 1, "B1": 1}[kind]


def before(kind, k, off):
    if not known(k):
        return {"A": ("B1", off - 3), "B0": ("A", off + 2), "B1": ("B0", off)}[kind]
    n = PLACE[(kind, k + off)]
    return (INSTANCES[n - 1][0], INSTANCES[n - 1][1] - k) if n else None


def wait(eng, sem, value):
    if not (known(value) and value <= 0):
        eng.wait_ge(sem, value)


def alone(eng, passed):
    eng.sem_inc(passed, 1)


def run_steps(eng, step):
    for k in range(FIRST_STEP, LOOP_STEPS[0]):
        step(k)
    with eng.Fori(*LOOP_STEPS) as k:
        step(k)
    for k in range(LOOP_STEPS[1], LAST_STEP + 1):
        step(k)


def sandwich_kernel(nc, x, w_proj, w_out, cols, rows, ffn_rw, ffn_rb, fw1, fw2, out):
    ctx = ExitStack()
    with ctx:
        def sb(name, shape, dt=F32):
            return ctx.enter_context(nc.sbuf_tensor(name, shape, dt))

        def sem(name):
            return ctx.enter_context(nc.semaphore(name))

        xs = sb("xs", [128, NB * T])
        ys = sb("ys", [128, NB * T])
        n2t = sb("n2t", [128, NB * T])
        n2sum = sb("n2sum", [128, NB])
        mixp = sb("mixp", [128, NB * NM])
        wp = sb("wp", [128, 9, 128])
        wo = sb("wo", [128, NM, 128])
        col = sb("col", [128, 12])
        qbias = sb("qbias", [128, NM])
        row = sb("row", [1, NM * 128])
        rbb = sb("rbb", [128, NM])
        frw = sb("frw", [128, NE])
        frb = sb("frb", [NB, NE])
        ident = sb("ident", [128, 128])
        identb = sb("identb", [128, 128], BF16)
        ones = sb("ones", [1, 128])
        onerow = sb("onerow", [2, H * T], BF16)
        BQ, BK, BV, G1, B1, G2, B2, RW = 0, 2, 4, 6, 7, 8, 9, 10

        qs = [sb(f"qs{i}", [128, H, T], BF16) for i in range(3)]
        ks = [sb(f"ks{i}", [128, H, T], BF16) for i in range(3)]
        vext = [sb(f"vext{i}", [128, QT * H, VW]) for i in range(3)]
        probs = sb("probs", [128, H, QT * T])
        qk = sb("qk", [128, 2 * T])
        parts = sb("parts", [128, 3, 2 * T], BF16)
        rest = sb("rest", [128, 2 * T])
        rowmax = sb("rowmax", [128, 2, QT, HALF])
        shift = sb("shift", [128, 2, QT, 2 * HALF], BF16)
        shiftrow = sb("shiftrow", [2 * HALF, 2, T], BF16)
        heads_out = sb("heads_out", [128, 2, 512])
        inv = sb("inv", [128, 2, QT, HALF])
        context = sb("context", [128, QT, 128])
        ct = [sb(f"ct{m}", [128, T]) for m in range(NM)]
        nta = sb("nta", [128, T])
        n1t = sb("n1t", [128, T])
        n1sum = sb("n1sum", [128, 1])
        n1sumb = sb("n1sumb", [128, 128])
        u0 = sb("u0", [128, T])
        u1 = sb("u1", [128, T])
        u2 = sb("u2", [128, T])
        t1 = sb("t1", [128, T])
        st = {s: (sb(f"st{s}", [128, QT, 6]), sb(f"mv{s}", [128, QT, 2]), sb(f"rs{s}", [128, QT])) for s in "xayzf"}
        var_eps = {s: sb(f"var_eps{s}", [128, QT]) for s in "xaynzf"}
        minus_half = sb("minus_half", [128, QT])
        r2 = sb("r2", [128, 2 * QT])
        r3 = sb("r3", [128, QT])
        lg = sb("lg", [128, 10])

        s_ps = [ctx.enter_context(nc.psum_tensor(f"s_ps{i}", [128, 512], F32)) for i in range(2)]
        e_ps = [ctx.enter_context(nc.psum_tensor(f"e_ps{i}", [128, 512], F32)) for i in range(2)]
        o_ps = [ctx.enter_context(nc.psum_tensor(f"o_ps{i}", [128, 512], F32)) for i in range(2)]
        misc = {b: ctx.enter_context(nc.psum_tensor(f"misc{b}", [128, 512], F32)) for b in "XY"}

        scratch = nc.dram_tensor("part_scratch", (3, H, KD, 3, 2 * T), BF16, kind="Internal").ap()

        inv_std = {s: sem(f"inv_std_{s}") for s in "xaynzf"}
        const_in = sem("const_in")
        x_in = sem("x_in")
        passed = {e: sem(f"passed_{e}") for e in ("dve", "pool", "sp")}
        zeroed = sem("zeroed")
        ones_in = sem("ones_in")
        pool_const = sem("pool_const")
        xn = sem("xn")
        xt_ps = sem("xt_ps")
        xt_done = sem("xt_done")
        qk_ps = sem("qk_ps")
        qk_out = sem("qk_out")
        split = sem("split")
        parts_out = sem("parts_out")
        stacked = [sem(f"stacked{i}") for i in range(3)]
        v_ps = sem("v_ps")
        v_out = sem("v_out")
        s_ready = sem("s_ready")
        s_max = sem("s_max")
        shift_made = sem("shift_made")
        shift_ps = sem("shift_ps")
        shift_out = sem("shift_out")
        shift_in = [sem(f"shift_in{i}") for i in range(2)]
        e_ready = sem("e_ready")
        e_done = sem("e_done")
        pv = sem("pv")
        o_saved = sem("o_saved")
        o_ps_t = sem("o_ps_t")
        ctx_done = sem("ctx_done")
        an = sem("an")
        n1_ps = sem("n1_ps")
        n1_out = sem("n1_out")
        n1sum_b = sem("n1sum_b")
        route_ps = sem("route_ps")
        route_v = sem("route_v")
        route_e = sem("route_e")
        ct_ps = sem("ct_ps")
        ct_out = sem("ct_out")
        mix_ps = sem("mix_ps")
        zn = sem("zn")
        n2_ps = sem("n2_ps")
        n2_out = sem("n2_out")

        NX, NA, NZ, NR = 7, 20, 9, 6

        fr = sb("fr", [NB, 48])
        top = sb("top", [NB, 8])
        topi = sb("topi", [NB, 8], U32)
        taken_p = sb("taken_p", [128, NB * TOPK])
        taken_i = sb("taken_i", [1, NB * 8], U32)
        w1s = [sb(f"w1s{i}", [128, TOPK, F]) for i in range(2)]
        w2l = [sb(f"w2l{i}", [128, TOPK, FC, D]) for i in range(2)]
        w2s = [sb(f"w2s{i}", [128, TOPK, FC, D]) for i in range(2)]
        hidden = [sb(f"hidden{i}", [128, TOPK, FC * T]) for i in range(2)]
        z = sb("z", [128, T])
        normed = sb("normed", [128, T])
        result = [sb(f"result{i}", [128, T]) for i in range(2)]
        p_scratch = nc.dram_tensor("p_scratch", (NB, TOPK), F32, kind="Internal").ap()
        i_scratch = nc.dram_tensor("i_scratch", (NB, 8), U32, kind="Internal").ap()
        fr_ps = sem("fr_ps")
        fr_v = sem("fr_v")
        fr_e = sem("fr_e")
        routed = sem("routed")
        w_in = [sem(f"w_in{i}") for i in range(2)]
        w2_scaled = sem("w2_scaled")
        h_ps = sem("h_ps")
        h_act = sem("h_act")
        eo_ps = sem("eo_ps")
        fz = sem("fz")
        stored = [sem(f"stored{i}") for i in range(2)]
        NF = 9

        block = ctx.enter_context(nc.Block())

        @block.sync
        def _(sp):
            sp.dma_start(xs[:, :].rearrange("p (b q d) -> p b q d", b=NB, q=QT)[:, 0:1],
                         x.rearrange("b (q p) d -> p b q d", p=128)[:, 0:1]).then_inc(x_in, 16)
            for dst, src in ((wp[:, :, :].rearrange("p c n -> p (c n)"), w_proj), (col[:, :], cols), (wo[:, :, :], w_out.rearrange("m p n -> p m n")),
                             (row[:, :], rows[0:1, 0:NM * 128]), (frw[:, :], ffn_rw),
                             (rbb[:, :], rows[0:1, NM * 128:NM * 128 + NM].to_broadcast([128, NM])),
                             (frb[:, :], ffn_rb.to_broadcast([NB, NE]))):
                sp.dma_start(dst, src).then_inc(const_in, 16)
            sp.dma_start(xs[:, :].rearrange("p (b q d) -> p b q d", b=NB, q=QT)[:, 1:NB],
                         x.rearrange("b (q p) d -> p b q d", p=128)[:, 1:NB]).then_inc(x_in, 16)

            sp.wait_ge(zeroed, 9)
            sp.wait_ge(pool_const, 9)
            for i in range(3):
                sp.dma_start(ks[i][SHIFT:SHIFT + 2, :, :], onerow[:, :].rearrange("p (h n) -> p h n", h=H)).then_inc(ones_in, 16)

            def shift_rows(k, kind, off, half):
                i = place(kind, k, off)
                wait(sp, shift_out, 2 * i + half + 1)
                for part in range(2):
                    sp.dma_start(qs[ring3(kind, k, off)][SHIFT + part:SHIFT + part + 1, half * HALF:(half + 1) * HALF, :],
                                 shiftrow[part * HALF:(part + 1) * HALF, half, :]).then_inc(shift_in[half], 16)

            def store_parts(k, kind, off):
                i, r = place(kind, k, off), ring3(kind, k, off)
                wait(sp, split, 3 * i + 3)
                alone(sp, passed["sp"])
                wait(sp, stacked[r], 192 * turn3(kind, k, off))
                sp.dma_start(scratch[r].rearrange("h d p n -> (h d) (p n)"),
                             parts[:, :, :].rearrange("q p n -> q (p n)")).then_inc(parts_out, 16)

            def stack_heads(k, kind, off):
                i, r = place(kind, k, off), ring3(kind, k, off)
                wait(sp, parts_out, 16 * (i + 1))
                alone(sp, passed["sp"])
                wait(sp, e_ready, 16 * (i - 2))
                for c in range(6):
                    for dst, p, t in ((qs, Q_PARTS, 0), (ks, K_PARTS, T)):
                        sp.dma_start(dst[r][KD * c:KD * (c + 1), :, :],
                                     scratch[r, :, :, p[c], t:t + T].rearrange("h d n -> d h n")).then_inc(stacked[r], 16)

            def step(k):
                for slot in ("B0", "B1", "A"):
                    (kind, off), (mkind, moff) = SLOTS[slot]
                    if real(k, off):
                        shift_rows(k, kind, off, 1)
                    if real(k, off + 1):
                        store_parts(k, kind, off + 1)
                    if real(k, moff):
                        shift_rows(k, mkind, moff, 0)
                    if real(k, off + 1):
                        stack_heads(k, kind, off + 1)

            run_steps(sp, step)

            sp.wait_ge(fr_v, 11)
            sp.dma_start(p_scratch, fr[:, 40:40 + TOPK]).then_inc(routed, 16)
            sp.dma_start(i_scratch, topi[:, :]).then_inc(routed, 16)
            sp.wait_ge(routed, 32)
            sp.dma_start(taken_p[:, :], p_scratch.rearrange("(o b) e -> o (b e)", o=1).to_broadcast([128, NB * TOPK])).then_inc(routed, 16)
            sp.dma_start(taken_i[:, :], i_scratch.rearrange("(o b) e -> o (b e)", o=1)).then_inc(routed, 16)
            sp.wait_ge(routed, 64)

            def load_experts(b, par):
                wait(sp, eo_ps, b - 1)
                alone(sp, passed["sp"])
                for e in range(TOPK):
                    r = sp.value_load(taken_i[0:1, bass.ds(b * 8 + e, 1)], min_val=0, max_val=NE - 1)
                    sp.dma_start(w1s[par][:, e, :], fw1[bass.ds(r, 1), :, :].rearrange("o p f -> p (o f)")).then_inc(w_in[par], 16)
                    sp.dma_start(w2l[par][:, e, :, :], fw2[bass.ds(r, 1), :, :].rearrange("o (c p) n -> p (o c) n", p=128)).then_inc(w_in[par], 16)

            def store_result(b, par):
                sp.wait_ge(fz, NF * b + 9)
                sp.dma_start(out[bass.ds(b, 1), :, :].rearrange("o (q p) d -> p (o q) d", p=128),
                             result[par][:, :].rearrange("p (q d) -> p q d", q=QT)).then_inc(stored[par], 16)

            load_experts(0, 0)
            load_experts(1, 1)
            with sp.Fori(0, NB // 2 - 1) as g:
                for par in range(2):
                    load_experts(2 * g + par + 2, par)
                    store_result(2 * g + par, par)
            for par in range(2):
                store_result(NB - 2 + par, par)
                sp.wait_ge(stored[par], 16 * (NB // 2))

        @block.gpsimd
        def _(pool):
            pool.memset(ident[:, :], 0.0).then_inc(pool_const, 1)
            pool.memset(identb[:, :], 0.0).then_inc(pool_const, 1)
            pool.memset(ones[:, :], 1.0).then_inc(pool_const, 1)
            pool.wait_ge(pool_const, 3)
            for m in (ident, identb):
                pool.affine_select(out=m[:, :], in_=m[:, :], compare_op=ALU.not_equal, fill=1.0, base=0,
                                   pattern=[[-1, 128]], channel_multiplier=1).then_inc(pool_const, 1)
            pool.memset(onerow[:, :], 1.0).then_inc(pool_const, 1)
            pool.memset(minus_half[:, :], -0.5).then_inc(pool_const, 1)
            pool.wait_ge(zeroed, 9)
            for i in range(3):
                pool.memset(vext[i][:, :, KD:KD + 1], 1.0).then_inc(pool_const, 1)
            pool.wait_ge(const_in, 16 * 7)
            pool.tensor_scalar(qbias[:, :], col[:, BQ:BQ + NM], KD ** -0.5, None, ALU.mult).then_inc(pool_const, 1)

            pool.wait_ge(pool_const, 11)

            def split_parts(k, kind, off, part):
                i = place(kind, k, off)
                if part == 0:
                    wait(pool, qk_out, 3 * i + 3)
                    wait(pool, split, 3 * i)
                    pool.tensor_tensor(rest[:, :], qk[:, :], parts[:, 0, :], ALU.subtract).then_inc(split, 1)
                elif part == 1:
                    pool.wait_ge(split, 3 * i + 1)
                    wait(pool, parts_out, 16 * i)
                    alone(pool, passed["pool"])
                    pool.tensor_copy(parts[:, 1, :], rest[:, :]).then_inc(split, 1)
                else:
                    pool.wait_ge(split, 3 * i + 2)
                    pool.tensor_tensor(parts[:, 2, :], rest[:, :], parts[:, 1, :], ALU.subtract).then_inc(split, 1)

            STD = {"x": (xn, NX, 5), "a": (an, NA, 5), "y": (an, NA, 13), "n": (an, NA, 18), "z": (zn, NZ, 7), "f": (fz, NF, 6)}

            def invert_std(k, s, off):
                b = k + off
                sem_, per, done = STD[s]
                pool.wait_ge(sem_, per * b + done)
                wait(pool, inv_std[s], b)
                pool.tensor_tensor(r3[:, :] if s == "n" else st[s][2][:, :], var_eps[s][:, :], minus_half[:, :], ALU.pow).then_inc(inv_std[s], 1)

            def spread_sum(k, kind, off):
                b = k + off
                wait(pool, n1_out, b + 1)
                wait(pool, route_ps, b)
                alone(pool, passed["pool"])
                pool.tensor_copy(n1sumb[:, :], n1sum[:, 0:1].to_broadcast([128, 128])).then_inc(n1sum_b, 1)

            def step(k):
                for what, *args in WORK:
                    if real(k, args[1]):
                        what(k, *args)

            WORK = [(split_parts, "B0", 1, 0), (invert_std, "z", -1), (split_parts, "B0", 1, 1), (split_parts, "B0", 1, 2), (invert_std, "a", 2),
                    (invert_std, "y", 2), (split_parts, "B1", 1, 0), (invert_std, "n", 2), (split_parts, "B1", 1, 1), (split_parts, "B1", 1, 2),
                    (invert_std, "x", 4), (split_parts, "A", 4, 0), (split_parts, "A", 4, 1), (split_parts, "A", 4, 2), (spread_sum, "A", 2)]
            run_steps(pool, step)

            with pool.Fori(0, NB) as b:
                invert_std(b, "f", 0)

        @block.tensor
        def _(pe):
            pe.wait_ge(const_in, 16 * 7)
            pe.wait_ge(pool_const, 11)
            pe.wait_ge(zeroed, 9)
            pe.wait_ge(ones_in, 16 * 3)
            at = {"X": None, "Y": None}

            def read(stage, kind, k, off):
                b = k + off
                if stage in ("mix", "norm2"):
                    return {"mix": (zn, NZ * b + 2), "norm2": (n2_out, b + 1)}[stage]
                i = place(kind, k, off)
                return {"shift0": (shift_out, 2 * i + 1), "shift1": (shift_out, 2 * i + 2), "project": (qk_out, 3 * i + 2),
                        "turn0": (ctx_done, 4 * i + 2), "turn1": (ctx_done, 4 * i + 4), "route": (route_v, NR * b + 1),
                        "values": (v_out, i + 1), "context": (ct_out, 2 * b + KINDS.index(kind)),
                        "norm_x": (xt_done, b + 1), "norm1": (n1_out, b + 1)}[stage]

            def take(bank, stage, kind, k, off):
                if at[bank]:
                    pe.wait_ge(*read(at[bank][0], at[bank][1], k, at[bank][2]))
                at[bank] = (stage, kind, off)
                return misc[bank]

            def turn_tiles(dst, src, done):
                for q in range(QT):
                    last = pe.transpose(dst[:, q * 128:(q + 1) * 128], src[:, q * 128:(q + 1) * 128], ident[:, :])
                last.then_inc(done, 1)

            def work(k, stage, kind, off, bank):
                b = k + off
                i = place(kind, k, off) if kind != "B" else None
                m = KINDS.index(kind) - 1 if kind != "B" else None
                if stage in ("shift0", "shift1"):
                    half = int(stage[-1])
                    pe.wait_ge(shift_made, 4 * i + 2 * half + 2)
                    ps = take(bank, stage, kind, k, off)[:, :].bitcast(BF16)
                    for q in range(QT):
                        last = pe.transpose(ps[0:2 * HALF, q * 128:(q + 1) * 128], shift[:, half, q, :], identb[:, :])
                    last.then_inc(shift_ps, 1)
                elif stage in ("turn0", "turn1"):
                    half = int(stage[-1])
                    pe.wait_ge(o_saved, 2 * i + half + 1)
                    ps = take(bank, stage, kind, k, off)
                    for q in range(QT):
                        for s in range(2):
                            last = pe.transpose(ps[:, q * 256 + s * 128:q * 256 + (s + 1) * 128],
                                                heads_out[:, half, s * 256 + q * 128:s * 256 + (q + 1) * 128], ident[:, :])
                    last.then_inc(o_ps_t, 1)
                elif stage == "project":
                    if kind == "A":
                        pe.wait_ge(xt_done, b + 1)
                    else:
                        pe.wait_ge(n1_out, b + 1)
                    ps = take(bank, stage, kind, k, off)
                    for j in range(2):
                        last = pe.matmul(ps[:, j * T:(j + 1) * T], wp[:, 3 * (m + 1) + j, :], (nta if kind == "A" else n1t)[:, :],
                                         start=True, stop=True)
                    last.then_inc(qk_ps, 1)
                elif stage == "values":
                    ps = take(bank, stage, kind, k, off)
                    for q in range(QT):
                        last = pe.matmul(ps[:, q * 128:(q + 1) * 128], (nta if kind == "A" else n1t)[:, q * 128:(q + 1) * 128],
                                         wp[:, 3 * (m + 1) + 2, :], start=True, stop=True)
                    last.then_inc(v_ps, 1)
                elif stage == "norm_x":
                    pe.wait_ge(xn, NX * b + 7)
                    turn_tiles(take(bank, stage, kind, k, off), u0, xt_ps)
                elif stage == "norm1":
                    pe.wait_ge(an, NA * b + 20)
                    turn_tiles(take(bank, stage, kind, k, off), u1, n1_ps)
                elif stage == "norm2":
                    pe.wait_ge(zn, NZ * b + 9)
                    turn_tiles(take(bank, stage, kind, k, off), u2, n2_ps)
                elif stage == "route":
                    pe.wait_ge(n1sum_b, b + 1)
                    ps = take(bank, stage, kind, k, off)
                    pe.matmul(ps[:, 0:NM], n1sumb[:, :], col[:, RW:RW + NM], start=True, stop=True).then_inc(route_ps, 1)
                elif stage == "context":
                    pe.wait_ge(ctx_done, 4 * i + 4)
                    ps = take(bank, stage, kind, k, off)
                    for q in range(QT):
                        last = pe.transpose(ps[:, q * 128:(q + 1) * 128], context[:, q, :], ident[:, :])
                    last.then_inc(ct_ps, 1)
                elif stage == "mix":
                    pe.wait_ge(ct_out, 2 * b + 2)
                    ps = take(bank, stage, kind, k, off)
                    for e in range(NM):
                        for q in range(QT):
                            o = ps[:, e * T + q * 128:e * T + (q + 1) * 128]
                            pe.matmul(o, ct[e][:, q * 128:(q + 1) * 128], wo[:, e, :], start=True, stop=False)
                            last = pe.matmul(o, ones[:, :], row[:, e * 128:(e + 1) * 128], start=False, stop=True)
                    last.then_inc(mix_ps, 1)

            def scores(k, kind, off, h):
                i, r = place(kind, k, off), ring3(kind, k, off)
                if h == 0:
                    pe.wait_ge(stacked[r], 192 * (turn3(kind, k, off) + 1))
                wait(pe, s_max, 16 * i + h - 1)
                for q in range(QT):
                    last = pe.matmul(s_ps[h % 2][:, q * T:(q + 1) * T], qs[r][0:SHIFT, h, q * 128:(q + 1) * 128],
                                     ks[r][0:SHIFT, h, :], start=True, stop=True)
                last.then_inc(s_ready, 1)

            def shifted_scores(k, kind, off, h):
                i, r = place(kind, k, off), ring3(kind, k, off)
                if h % HALF == 0:
                    pe.wait_ge(shift_in[h // HALF], 32 * (i + 1))
                wait(pe, e_done, 16 * i + h - 1)
                for q in range(QT):
                    last = pe.matmul(e_ps[h % 2][:, q * T:(q + 1) * T], ks[r][:, h, q * 128:(q + 1) * 128],
                                     qs[r][:, h, :], start=True, stop=True)
                last.then_inc(e_ready, 1)

            def probs_v(k, kind, off, quad, q):
                i, r = place(kind, k, off), ring3(kind, k, off)
                if q == 0:
                    pe.wait_ge(e_done, 16 * i + 4 * quad + 4)
                    if quad == 0:
                        pe.wait_ge(v_out, i + 1)
                    if quad % 2 == 0:
                        wait(pe, o_saved, 2 * i + quad // 2 - 1)
                o = o_ps[quad // 2]
                for g in range(4):
                    h = 4 * quad + g
                    last = pe.matmul(o[VW * g:VW * (g + 1), (quad % 2) * T:(quad % 2 + 1) * T], vext[r][:, q * H + h, :],
                                     probs[:, h, q * T:(q + 1) * T], start=(q == 0), stop=(q == QT - 1))
                if q == QT - 1:
                    last.then_inc(pv, 1)

            def step(k):
                for bank in at:
                    if at[bank]:
                        at[bank] = at[bank][:2] + (at[bank][2] - 1,)
                for slot, last in (("B0", ("A", 2)), ("B1", ("B0", 0)), ("A", ("B1", 0))):
                    (kind, off), (mkind, moff) = SLOTS[slot]
                    for h in range(H):
                        if real(k, moff):
                            scores(k, mkind, moff, h)
                        if real(k, off):
                            shifted_scores(k, kind, off, h)
                        if h in (1, 3) and real(k, last[1]):
                            probs_v(k, *last, 3, h // 2)
                        if h % 2 and h >= 5 and real(k, off):
                            probs_v(k, kind, off, (h - 5) // 4, (h - 5) // 2 % 2)
                        for when, stage, skind, soff, bank in TENSOR_WORK[slot]:
                            if when == h and real(k, soff):
                                work(k, stage, skind, soff, bank)

            run_steps(pe, step)

            pe.wait_ge(n2_out, NB)
            pe.wait_ge(zn, NZ * NB)
            pe.matmul(misc["X"][0:NB, 0:NE], n2sum[:, :], frw[:, :], start=True, stop=True).then_inc(fr_ps, 1)

            def up(b, par, half_count):
                pe.wait_ge(w_in[par], 64 * half_count)
                wait(pe, h_act, 2 * b - 2)
                for e in range(TOPK):
                    for c in range(FC):
                        last = pe.matmul((s_ps, e_ps)[par][e][:, c * T:(c + 1) * T], w1s[par][:, e, c * 128:(c + 1) * 128],
                                         n2t[:, bass.ds(b * T, T)], start=True, stop=True)
                    last.then_inc(h_ps, 1)

            def down(b, par):
                pe.wait_ge(h_act, 2 * b + 2)
                pe.wait_ge(w2_scaled, 2 * b + 2)
                wait(pe, fz, NF * (b - 2) + 1)
                for q in range(QT):
                    for e in range(TOPK):
                        for c in range(FC):
                            last = pe.matmul(o_ps[par][:, q * 128:(q + 1) * 128],
                                             hidden[par][:, e, c * T + q * 128:c * T + (q + 1) * 128], w2s[par][:, e, c, :],
                                             start=(e == 0 and c == 0), stop=(e == TOPK - 1 and c == FC - 1))
                last.then_inc(eo_ps, 1)

            up(0, 0, 1)
            up(1, 1, 1)
            down(0, 0)
            up(2, 0, 2)
            down(1, 1)
            with pe.Fori(1, NB // 2 - 1) as g:
                up(2 * g + 1, 1, g + 1)
                down(2 * g, 0)
                up(2 * g + 2, 0, g + 2)
                down(2 * g + 1, 1)
            up(NB - 1, 1, NB // 2)
            down(NB - 2, 0)
            down(NB - 1, 1)

        @block.scalar
        def _(act):
            act.wait_ge(const_in, 16 * 7)
            act.wait_ge(pool_const, 11)
            act.wait_ge(zeroed, 9)

            def exps(k, kind, off, h):
                i = place(kind, k, off)
                if h % 4 == 0:
                    wait(act, pv, 4 * i + h // 4 - 3)
                act.wait_ge(e_ready, 16 * i + h + 1)
                act.activation(probs[:, h, :], e_ps[h % 2][:, :], ACT.Exp).then_inc(e_done, 1)

            def save_heads(k, kind, off, half):
                i = place(kind, k, off)
                act.wait_ge(pv, 4 * i + 2 * half + 2)
                wait(act, o_ps_t, 2 * i + half - 1)
                act.activation(heads_out[:, half, :], o_ps[half][:, :], ACT.Copy).then_inc(o_saved, 1)

            def save_shift(k, kind, off, half):
                i = place(kind, k, off)
                act.wait_ge(shift_ps, 2 * i + half + 1)
                wait(act, shift_in[half], 32 * i)
                ps = misc["Y"][:, :].bitcast(BF16)
                act.activation(shiftrow[:, half, :], ps[0:2 * HALF, 0:T], ACT.Copy).then_inc(shift_out, 1)

            def save_qk(k, kind, off):
                i, m = place(kind, k, off), KINDS.index(kind) - 1
                act.wait_ge(qk_ps, i + 1)
                wait(act, split, 3 * i - 2)
                if kind == "A":
                    act.activation(qk[:, 0:T], misc["Y"][:, 0:T], ACT.Copy, scale=D ** -0.5).then_inc(qk_out, 1)
                    act.activation(qk[:, T:2 * T], misc["Y"][:, T:2 * T], ACT.Copy).then_inc(qk_out, 1)
                else:
                    act.activation(qk[:, 0:T], misc["Y"][:, 0:T], ACT.Identity, bias=qbias[:, m:m + 1], scale=KD ** -0.5).then_inc(qk_out, 1)
                    act.activation(qk[:, T:2 * T], misc["Y"][:, T:2 * T], ACT.Identity, bias=col[:, BK + m:BK + m + 1]).then_inc(qk_out, 1)
                act.wait_ge(qk_out, 3 * i + 2)
                wait(act, parts_out, 16 * i)
                act.activation(parts[:, 0, :], qk[:, :], ACT.Copy).then_inc(qk_out, 1)

            def save_v(k, kind, off):
                i, r = place(kind, k, off), ring3(kind, k, off)
                act.wait_ge(v_ps, i + 1)
                wait(act, pv, 4 * (i - 2))
                act.activation(vext[r][:, :, 0:KD], misc["Y"][:, 0:T].rearrange("p (c d) -> p c d", d=KD), ACT.Copy).then_inc(v_out, 1)

            def save_norm_x(k, off):
                b = k + off
                act.wait_ge(xt_ps, b + 1)
                if real(k, off - 1):
                    act.wait_ge(v_ps, place("A", k, off - 1) + 1)
                act.activation(nta[:, :], misc["X"][:, 0:T], ACT.Copy).then_inc(xt_done, 1)

            def save_norm1(k, off):
                b = k + off
                act.wait_ge(n1_ps, b + 1)
                if real(k, off - 1):
                    act.wait_ge(v_ps, place("B1", k, off - 1) + 1)
                    act.wait_ge(n1sum_b, b)
                act.activation(n1t[:, :], misc["Y"][:, 0:T], ACT.Identity, bias=col[:, B1:B1 + 1], scale=col[:, G1:G1 + 1],
                               accum_out=n1sum[:, 0:1]).then_inc(n1_out, 1)

            def save_norm2(k, off):
                b = k + off
                act.wait_ge(n2_ps, b + 1)
                act.activation(n2t[:, bass.ds(b * T, T)], misc["X"][:, 0:T], ACT.Identity, bias=col[:, B2:B2 + 1],
                               scale=col[:, G2:G2 + 1], accum_out=n2sum[:, bass.ds(b, 1)]).then_inc(n2_out, 1)

            def save_context(k, kind, off):
                b, m = k + off, KINDS.index(kind) - 1
                act.wait_ge(ct_ps, 2 * b + m + 1)
                wait(act, mix_ps, b)
                act.activation(ct[m][:, :], misc["X"][:, 0:T], ACT.Identity, bias=col[:, BV + m:BV + m + 1]).then_inc(ct_out, 1)

            def route_exp(k, off):
                b = k + off
                act.wait_ge(route_v, NR * b + 3)
                act.activation(lg[:, 6:8], lg[:, 4:6], ACT.Exp).then_inc(route_e, 1)

            WORK = {
                "B0": [(2, save_shift, "B0", 0, 1), (4, save_heads, "A", 2, 1), (5, save_qk, "B0", 1), (9, save_v, "A", 3),
                       (11, save_shift, "B1", 0, 0), (12, route_exp, 1), (12, save_heads, "B0", 0, 0)],
                "B1": [(2, save_shift, "B1", 0, 1), (4, save_heads, "B0", 0, 1), (5, save_qk, "B1", 1), (9, save_v, "B0", 1),
                       (10, save_norm2, -1), (11, save_shift, "A", 3, 0), (12, save_context, "B0", 0), (12, save_heads, "B1", 0, 0)],
                "A": [(2, save_shift, "A", 3, 1), (3, save_norm_x, 4), (4, save_heads, "B1", 0, 1), (6, save_qk, "A", 4), (9, save_v, "B1", 1),
                      (11, save_shift, "B0", 1, 0), (12, save_context, "B1", 0), (12, save_heads, "A", 3, 0), (13, save_norm1, 2)],
            }

            def step(k):
                for slot in ("B0", "B1", "A"):
                    (kind, off), _m = SLOTS[slot]
                    for h in range(H):
                        if real(k, off):
                            exps(k, kind, off, h)
                        for when, what, *args in WORK[slot]:
                            if when == h and real(k, args[1] if isinstance(args[0], str) else args[0]):
                                what(k, *args)

            run_steps(act, step)

            act.wait_ge(fr_v, 3)
            act.activation(fr[:, 24:32], fr[:, 16:24], ACT.Exp).then_inc(fr_e, 1)

            def gelus(b, par):
                wait(act, eo_ps, b - 1)
                for e in range(TOPK):
                    act.wait_ge(h_ps, 2 * b + e + 1)
                    act.activation(hidden[par][:, e, :], (s_ps, e_ps)[par][e][:, :], ACT.Gelu).then_inc(h_act, 1)

            for par in range(2):
                gelus(par, par)
            with act.Fori(1, NB // 2) as g:
                for par in range(2):
                    gelus(2 * g + par, par)

        @block.vector
        def _(dve):
            for i in range(3):
                dve.memset(vext[i][:, :, :], 0.0).then_inc(zeroed, 1)
            for s in ks + qs:
                dve.memset(s[:, :, :].bitcast(U32), 0).then_inc(zeroed, 1)
            dve.wait_ge(const_in, 16 * 7)

            def maxima(k, kind, off, h):
                i = place(kind, k, off)
                if h % HALF == 0:
                    wait(dve, shift_made, 4 * i + 2 * (h // HALF) - 2)
                dve.wait_ge(s_ready, 16 * i + h + 1)
                dve.tensor_reduce(rowmax[:, h // HALF, :, h % HALF:h % HALF + 1], s_ps[h % 2][:, :].rearrange("p (q n) -> p q n", q=QT),
                                  AX_X, ALU.max).then_inc(s_max, 1)

            def make_shift(k, kind, off, half):
                i = place(kind, k, off)
                dve.wait_ge(s_max, 16 * i + HALF * (half + 1))
                wait(dve, shift_ps, 2 * i + half - 1)
                hi, lo = shift[:, half, :, 0:HALF], shift[:, half, :, HALF:2 * HALF]
                dve.tensor_scalar(hi, rowmax[:, half, :, :], -1.0, None, ALU.mult).then_inc(shift_made, 1)
                dve.wait_ge(shift_made, 4 * i + 2 * half + 1)
                dve.scalar_tensor_tensor(out=lo, in0=rowmax[:, half, :, :], scalar=-1.0, in1=hi, op0=ALU.mult,
                                         op1=ALU.subtract).then_inc(shift_made, 1)

            def invert_sums(k, kind, off, half):
                i = place(kind, k, off)
                dve.wait_ge(o_ps_t, 2 * i + half + 1)
                wait(dve, ctx_done, 4 * i + 2 * half - 2)
                sums = misc["X"][:, :].rearrange("p (q s c) -> p q s c", q=QT, c=VW)[:, :, :, KD]
                dve.reciprocal(inv[:, half, :, :], sums).then_inc(ctx_done, 1)

            def normalise(k, kind, off, half):
                i = place(kind, k, off)
                dve.wait_ge(ctx_done, 4 * i + 2 * half + 1)
                if (last := before(kind, k, off)) and half == 0:
                    b = k + last[1]
                    if last[0] == "A":
                        dve.wait_ge(an, NA * b + 7)
                    else:
                        dve.wait_ge(ct_ps, 2 * b + KINDS.index(last[0]))
                heads = misc["X"][:, :].rearrange("p (q s c) -> p q s c", q=QT, c=VW)[:, :, :, 0:KD]
                dst = context[:, :, half * 64:(half + 1) * 64].rearrange("p q (s d) -> p q s d", d=KD)
                dve.tensor_tensor(dst, heads, inv[:, half, :, :].unsqueeze(3).to_broadcast([128, QT, HALF, KD]),
                                  ALU.mult).then_inc(ctx_done, 1)

            def stats(sem_, base, done, src, s):
                wait(dve, sem_, base + done)
                alone(dve, passed["dve"])
                for q in range(QT):
                    dve.bn_stats(st[s][0][:, q, :], src(q)).then_inc(sem_, 1)

            def aggregate(sem_, base, done, s):
                dve.wait_ge(sem_, base + done)
                alone(dve, passed["dve"])
                for q in range(QT):
                    dve.bn_aggr(st[s][1][:, q, :], st[s][0][:, q, :]).then_inc(sem_, 1)

            def add_eps(sem_, base, done, s, eps):
                dve.wait_ge(sem_, base + done)
                dve.tensor_scalar(var_eps[s][:, :], st[s][1][:, :, 1], eps, None, ALU.add).then_inc(sem_, 1)

            def scale_to(sem_, b, s, dst, src):
                dve.wait_ge(inv_std[s], b + 1)
                for q in range(QT):
                    dve.tensor_scalar(dst(q), src(q), st[s][1][:, q, 0:1], st[s][2][:, q:q + 1], ALU.subtract, ALU.mult).then_inc(sem_, 1)

            def tile_of(buf):
                return lambda q: buf[:, q * 128:(q + 1) * 128]

            def tile_at(buf, b):
                return lambda q: buf[:, bass.ds(b * T + q * 128, 128)]

            def norm_x(k, off, part):
                b = k + off
                if part == 0:
                    if known(k):
                        dve.wait_ge(x_in, 32 if b else 16)
                    stats(xn, NX * b, 0, tile_at(xs, b), "x")
                elif part == 1:
                    aggregate(xn, NX * b, 2, "x")
                elif part == 2:
                    add_eps(xn, NX * b, 4, "x", EPS_OUTER)
                else:
                    wait(dve, xt_ps, b)
                    scale_to(xn, b, "x", tile_of(u0), tile_at(xs, b))

            def first_block(k, off, part):
                b = k + off
                base = NA * b
                if part == 0:
                    dve.wait_ge(ctx_done, 4 * place("A", k, off) + 4)
                    stats(an, base, 0, lambda q: context[:, q, :], "a")
                elif part == 1:
                    aggregate(an, base, 2, "a")
                elif part == 2:
                    add_eps(an, base, 4, "a", EPS_OUTER)
                elif part == 3:
                    scale_to(an, b, "a", tile_of(t1), lambda q: context[:, q, :])
                elif part == 4:
                    dve.wait_ge(an, base + 7)
                    x_b = xs[:, bass.ds(b * T, T)]
                    dve.tensor_tensor(x_b, t1[:, :], x_b, ALU.add).then_inc(an, 1)
                elif part == 5:
                    stats(an, base, 8, tile_at(xs, b), "y")
                elif part == 6:
                    aggregate(an, base, 10, "y")
                elif part == 7:
                    add_eps(an, base, 12, "y", EPS_OUTER)
                elif part == 8:
                    scale_to(an, b, "y", tile_at(ys, b), tile_at(xs, b))
                elif part == 9:
                    dve.wait_ge(an, base + 15)
                    dve.tensor_tensor(r2[:, 0:QT], st["y"][1][:, :, 1], st["y"][2][:, :], ALU.mult).then_inc(an, 1)
                elif part == 10:
                    dve.wait_ge(an, base + 16)
                    dve.tensor_tensor(r2[:, QT:2 * QT], r2[:, 0:QT], st["y"][2][:, :], ALU.mult).then_inc(an, 1)
                elif part == 11:
                    dve.wait_ge(an, base + 17)
                    dve.tensor_scalar(var_eps["n"][:, :], r2[:, QT:2 * QT], EPS_INNER, None, ALU.add).then_inc(an, 1)
                else:
                    dve.wait_ge(inv_std["n"], b + 1)
                    wait(dve, n1_ps, b)
                    for q in range(QT):
                        dve.tensor_scalar(tile_of(u1)(q), tile_at(ys, b)(q), r3[:, q:q + 1], None, ALU.mult).then_inc(an, 1)

            def second_block(k, off, part):
                b = k + off
                base = NZ * b
                if part < 2:
                    if part == 0:
                        dve.wait_ge(mix_ps, b + 1)
                        dve.wait_ge(an, NA * b + 15)
                        dve.wait_ge(route_v, NR * b + 6)
                    else:
                        dve.wait_ge(zn, base + 1)
                    y_b = ys[:, bass.ds(b * T, T)]
                    dve.scalar_tensor_tensor(out=y_b, in0=misc["X"][:, part * T:(part + 1) * T], scalar=mixp[:, bass.ds(b * NM + part, 1)],
                                             in1=y_b, op0=ALU.mult, op1=ALU.add).then_inc(zn, 1)
                elif part == 2:
                    stats(zn, base, 2, tile_at(ys, b), "z")
                elif part == 3:
                    aggregate(zn, base, 4, "z")
                elif part == 4:
                    add_eps(zn, base, 6, "z", EPS_INNER)
                else:
                    wait(dve, n2_ps, b)
                    scale_to(zn, b, "z", tile_of(u2), tile_at(ys, b))

            def route(k, off, part):
                b = k + off
                dve.wait_ge(*((route_ps, b + 1) if part == 0 else (route_v, NR * b + part)))
                if part == 0:
                    wait(dve, route_v, NR * b)
                    op = dve.scalar_tensor_tensor(out=lg[:, 0:2], in0=misc["Y"][:, 0:NM], scalar=1.0 / T, in1=rbb[:, :], op0=ALU.mult, op1=ALU.add)
                elif part == 1:
                    op = dve.tensor_reduce(lg[:, 2:3], lg[:, 0:2], AX_X, ALU.max)
                elif part == 2:
                    wait(dve, route_e, b)
                    op = dve.tensor_scalar(lg[:, 4:6], lg[:, 0:2], lg[:, 2:3], None, ALU.subtract)
                elif part == 3:
                    dve.wait_ge(route_e, b + 1)
                    op = dve.tensor_reduce(lg[:, 8:9], lg[:, 6:8], AX_X, ALU.add)
                elif part == 4:
                    op = dve.reciprocal(lg[:, 9:10], lg[:, 8:9])
                else:
                    op = dve.tensor_scalar(mixp[:, bass.ds(b * NM, NM)], lg[:, 6:8], lg[:, 9:10], None, ALU.mult)
                op.then_inc(route_v, 1)

            WORK = {
                "B0": [(0, normalise, "A", 2, 0), (7, invert_sums, "A", 2, 1), (8, normalise, "A", 2, 1), (8, make_shift, "B1", 0, 0),
                       (15, make_shift, "B1", 0, 1), (15, invert_sums, "B0", 0, 0)]
                + [(h, second_block, -1, n) for n, h in enumerate((3, 4, 5, 6, 7, 10))]
                + [(h, first_block, 2, n) for n, h in enumerate((9, 10, 11, 13, 14))]
                + [(8 + n, route, 1, n) for n in range(3)] + [(13 + n, route, 1, 3 + n) for n in range(3)],
                "B1": [(0, normalise, "B0", 0, 0), (7, invert_sums, "B0", 0, 1), (8, normalise, "B0", 0, 1), (8, make_shift, "A", 3, 0),
                       (15, make_shift, "A", 3, 1), (15, invert_sums, "B1", 0, 0)]
                + [(h, first_block, 2, 5 + n) for n, h in enumerate((1, 2, 3, 5, 6, 7, 8, 11))]
                + [(h, norm_x, 4, n) for n, h in enumerate((9, 10, 11, 14))],
                "A": [(0, normalise, "B1", 0, 0), (7, invert_sums, "B1", 0, 1), (8, normalise, "B1", 0, 1), (8, make_shift, "B0", 1, 0),
                      (15, make_shift, "B0", 1, 1), (15, invert_sums, "A", 3, 0)],
            }

            def step(k):
                for slot in ("B0", "B1", "A"):
                    _e, (mkind, moff) = SLOTS[slot]
                    for h in range(H):
                        if real(k, moff):
                            maxima(k, mkind, moff, h)
                        for when, what, *args in WORK[slot]:
                            if when == h and real(k, args[1] if isinstance(args[0], str) else args[0]):
                                what(k, *args)

            run_steps(dve, step)

            dve.wait_ge(fr_ps, 1)
            dve.scalar_tensor_tensor(out=fr[:, 0:8], in0=misc["X"][0:NB, 0:NE], scalar=1.0 / T, in1=frb[:, :], op0=ALU.mult,
                                     op1=ALU.add).then_inc(fr_v, 1)
            dve.wait_ge(fr_v, 1)
            dve.tensor_reduce(fr[:, 8:9], fr[:, 0:8], AX_X, ALU.max).then_inc(fr_v, 1)
            dve.wait_ge(fr_v, 2)
            dve.tensor_scalar(fr[:, 16:24], fr[:, 0:8], fr[:, 8:9], None, ALU.subtract).then_inc(fr_v, 1)
            dve.wait_ge(fr_e, 1)
            dve.tensor_reduce(fr[:, 9:10], fr[:, 24:32], AX_X, ALU.add).then_inc(fr_v, 1)
            dve.wait_ge(fr_v, 4)
            dve.reciprocal(fr[:, 10:11], fr[:, 9:10]).then_inc(fr_v, 1)
            dve.wait_ge(fr_v, 5)
            dve.tensor_scalar(fr[:, 32:40], fr[:, 24:32], fr[:, 10:11], None, ALU.mult).then_inc(fr_v, 1)
            dve.wait_ge(fr_v, 6)
            dve.max(top[:, :], fr[:, 32:40]).then_inc(fr_v, 1)
            dve.wait_ge(fr_v, 7)
            dve.max_index(topi[:, :], top[:, :], fr[:, 32:40]).then_inc(fr_v, 1)
            dve.tensor_reduce(fr[:, 11:12], top[:, 0:TOPK], AX_X, ALU.add).then_inc(fr_v, 1)
            dve.wait_ge(fr_v, 9)
            dve.reciprocal(fr[:, 12:13], fr[:, 11:12]).then_inc(fr_v, 1)
            dve.wait_ge(fr_v, 10)
            dve.tensor_scalar(fr[:, 40:42], top[:, 0:TOPK], fr[:, 12:13], None, ALU.mult).then_inc(fr_v, 1)
            dve.wait_ge(routed, 64)

            def scale_experts(b, par, half_count):
                dve.wait_ge(w_in[par], 64 * half_count)
                wait(dve, eo_ps, b - 1)
                for e in range(TOPK):
                    dve.tensor_scalar(w2s[par][:, e, :, :], w2l[par][:, e, :, :], taken_p[:, bass.ds(b * TOPK + e, 1)], None,
                                      ALU.mult).then_inc(w2_scaled, 1)

            def finish(b, par, half_count):
                base = NF * b
                dve.wait_ge(eo_ps, b + 1)
                wait(dve, fz, base)
                dve.tensor_tensor(z[:, :], o_ps[par][:, 0:T], ys[:, bass.ds(b * T, T)], ALU.add).then_inc(fz, 1)
                stats(fz, base, 1, tile_of(z), "f")
                aggregate(fz, base, 3, "f")
                add_eps(fz, base, 5, "f", EPS_OUTER)
                scale_to(fz, b, "f", tile_of(normed), tile_of(z))
                dve.wait_ge(fz, base + 8)
                wait(dve, stored[par], 16 * (half_count - 1))
                dve.tensor_tensor(result[par][:, :], normed[:, :], xs[:, bass.ds(b * T, T)], ALU.add).then_inc(fz, 1)

            scale_experts(0, 0, 1)
            scale_experts(1, 1, 1)
            finish(0, 0, 1)
            scale_experts(2, 0, 2)
            finish(1, 1, 1)
            with dve.Fori(1, NB // 2 - 1) as g:
                scale_experts(2 * g + 1, 1, g + 1)
                finish(2 * g, 0, g + 1)
                scale_experts(2 * g + 2, 0, g + 2)
                finish(2 * g + 1, 1, g + 1)
            scale_experts(NB - 1, 1, NB // 2)
            finish(NB - 2, 0, NB // 2)
            finish(NB - 1, 1, NB // 2)


def kernel(L0_attn_x, L0_attn_Wq, L0_attn_Wk, L0_attn_Wv, L0_ffn_ln1_g, L0_ffn_ln1_b, L0_ffn_ln2_g, L0_ffn_ln2_b,
           L0_ffn_mha_wq, L0_ffn_mha_bq, L0_ffn_mha_wk, L0_ffn_mha_bk, L0_ffn_mha_wv, L0_ffn_mha_bv, L0_ffn_mha_wo,
           L0_ffn_mha_bo, L0_ffn_mha_rw, L0_ffn_mha_rb, L0_ffn_ffn_rw, L0_ffn_ffn_rb, L0_ffn_fw1, L0_ffn_fw2):
    import numpy as np
    import concourse.bacc as bacc
    from concourse.bass_utils import run_bass_kernel_spmd

    def flat(w):
        return np.asarray(w).reshape(D, D)

    wq, wk, wv, wo = (np.asarray(w) for w in (L0_ffn_mha_wq, L0_ffn_mha_wk, L0_ffn_mha_wv, L0_ffn_mha_wo))
    w_proj = np.concatenate([np.asarray(w).T for w in (L0_attn_Wq, L0_attn_Wk, L0_attn_Wv)]
                            + [flat(w[m]) for m in range(NM) for w in (wq, wk, wv)], axis=1)
    cols = np.concatenate([np.asarray(v).reshape(NM, D).T for v in (L0_ffn_mha_bq, L0_ffn_mha_bk, L0_ffn_mha_bv)]
                          + [np.asarray(v).reshape(D, 1) for v in (L0_ffn_ln1_g, L0_ffn_ln1_b, L0_ffn_ln2_g, L0_ffn_ln2_b)]
                          + [np.asarray(L0_ffn_mha_rw)], axis=1)
    rows = np.concatenate([np.asarray(L0_ffn_mha_bo).reshape(1, NM * D), np.asarray(L0_ffn_mha_rb).reshape(1, NM)], axis=1)
    arrays = {
        "x": np.asarray(L0_attn_x), "w_proj": w_proj, "w_out": wo.reshape(NM, D, D), "cols": cols, "rows": rows,
        "ffn_rw": np.asarray(L0_ffn_ffn_rw), "ffn_rb": np.asarray(L0_ffn_ffn_rb).reshape(1, NE),
        "fw1": np.asarray(L0_ffn_fw1), "fw2": np.asarray(L0_ffn_fw2),
    }
    arrays = {name: np.ascontiguousarray(a) for name, a in arrays.items()}
    nc = bacc.Bacc("TRN2", target_bir_lowering=False, num_devices=1)
    args = [nc.dram_tensor(name, a.shape, F32, kind="ExternalInput").ap() for name, a in arrays.items()]
    out = nc.dram_tensor("out", (NB, T, D), F32, kind="ExternalOutput").ap()
    sandwich_kernel(nc, *args, out)
    return run_bass_kernel_spmd(nc, [arrays], core_ids=[0]).results[0]["out"]
```

```python
from contextlib import ExitStack

import concourse.bass as bass
from concourse import mybir

ALU = mybir.AluOpType
ACT = mybir.ActivationFunctionType
F32 = mybir.dt.float32
BF16 = mybir.dt.bfloat16
U32 = mybir.dt.uint32
AX_X = mybir.AxisListType.X

NB, T, D = 16, 256, 128
H, KD = 16, 8
QT = T // 128
F, NE, TOPK, NM = 256, 8, 2, 2
FC = F // 128
EPS_OUTER, EPS_INNER = 1e-5, 1e-6
HALF = H // 2
VW = 32
SHIFT = 126
RUNS = ((0, 1), (1, 2), (3, 3))

KINDS = ("A", "B0", "B1")
LAST_STEP = 16
LOOP_STEPS = (1, 12)

INSTANCES = [("A", 0), ("A", 1), ("A", 2)]
for _k in range(NB):
    INSTANCES += [("B0", _k), ("B1", _k)] + ([("A", _k + 3)] if _k + 3 < NB else [])
PLACE = {inst: n for n, inst in enumerate(INSTANCES)}

START = (("project A", None, None, None), ("maxima A0", None, ("A", 0), None), ("attend A0", ("A", 0), ("A", 1), None),
         ("attend A1", ("A", 1), ("A", 2), ("A", 0)), ("attend A2", ("A", 2), None, ("A", 1)), ("turn to B", None, None, None),
         ("maxima B0", None, ("B0", 0), None))
SLOTS = (("B0", ("B0", 0), ("B1", 0), ("A", 2)), ("B1", ("B1", 0), ("A", 3), ("B0", 0)), ("A", ("A", 3), ("B0", 1), ("B1", 0)))

TENSOR_WORK = {
    "project A": [(0, "norm_x", "A", 0, "X"), (0, "project", "A", 0, "Y"), (0, "values", "A", 0, "Y"), (0, "norm_x", "A", 1, "X"),
                  (0, "project", "A", 1, "Y"), (0, "values", "A", 1, "Y"), (0, "norm_x", "A", 2, "X")],
    "maxima A0": [(2, "project", "A", 2, "Y"), (5, "values", "A", 2, "Y"), (10, "shift0", "A", 0, "Y")],
    "attend A0": [(1, "shift1", "A", 0, "Y"), (7, "norm_x", "A", 3, "X"), (10, "shift0", "A", 1, "Y"), (14, "turn0", "A", 0, "X")],
    "attend A1": [(1, "shift1", "A", 1, "Y"), (6, "turn1", "A", 0, "X"), (10, "shift0", "A", 2, "Y"), (14, "turn0", "A", 1, "X")],
    "attend A2": [(1, "shift1", "A", 2, "Y"), (4, "norm1", "A", 0, "Y"), (6, "project", "B0", 0, "Y"), (7, "turn1", "A", 1, "X"),
                  (8, "values", "B0", 0, "Y"), (14, "project", "B1", 0, "Y"), (14, "turn0", "A", 2, "X")],
    "turn to B": [(0, "values", "B1", 0, "Y"), (0, "route", "A", 0, "Y"), (0, "norm1", "A", 1, "Y"), (0, "project", "A", 3, "Y")],
    "maxima B0": [(10, "shift0", "B0", 0, "Y")],
    "B0": [(1, "shift1", "B0", 0, "Y"), (2, "mix", "B", -1, "X"), (4, "project", "B0", 1, "Y"), (6, "turn1", "A", 2, "X"),
           (7, "route", "A", 1, "Y"), (8, "values", "A", 3, "Y"), (10, "shift0", "B1", 0, "Y"), (14, "turn0", "B0", 0, "X")],
    "B1": [(1, "shift1", "B1", 0, "Y"), (4, "project", "B1", 1, "Y"), (6, "turn1", "B0", 0, "X"),
           (8, "values", "B0", 1, "Y"), (9, "norm2", "B", -1, "X"), (10, "shift0", "A", 3, "Y"), (11, "context", "B0", 0, "X"),
           (14, "turn0", "B1", 0, "X")],
    "A": [(1, "shift1", "A", 3, "Y"), (2, "norm_x", "A", 4, "X"), (5, "project", "A", 4, "Y"), (6, "turn1", "B1", 0, "X"),
          (8, "values", "B1", 1, "Y"), (10, "shift0", "B0", 1, "Y"), (11, "context", "B1", 0, "X"),
          (12, "norm1", "A", 2, "Y"), (14, "turn0", "A", 3, "X")],
}


def known(k):
    return isinstance(k, int)


def real(k, off):
    return not known(k) or 0 <= k + off < NB


def place(kind, k, off):
    if known(k):
        return PLACE[(kind, k + off)]
    return 3 * k + 3 * off + {"A": -4, "B0": 3, "B1": 4}[kind]


def ring3(kind, k, off):
    return PLACE[(kind, k + off)] % 3 if known(k) else {"A": 2, "B0": 0, "B1": 1}[kind]


def turn3(kind, k, off):
    return PLACE[(kind, k + off)] // 3 if known(k) else k + off + {"A": -2, "B0": 1, "B1": 1}[kind]


def before(kind, k, off):
    if not known(k):
        return {"A": ("B1", off - 3), "B0": ("A", off + 2), "B1": ("B0", off)}[kind]
    n = PLACE[(kind, k + off)]
    return (INSTANCES[n - 1][0], INSTANCES[n - 1][1] - k) if n else None


def wait(eng, sem, value):
    if not (known(value) and value <= 0):
        eng.wait_ge(sem, value)


def alone(eng, passed):
    eng.sem_inc(passed, 1)


def heads_of(attend, maxima):
    return range(H if attend or maxima else 1)


def run_steps(eng, step):
    for k in range(LOOP_STEPS[0]):
        step(k)
    with eng.Fori(*LOOP_STEPS) as k:
        step(k)
    for k in range(LOOP_STEPS[1], LAST_STEP + 1):
        step(k)


def sandwich_kernel(nc, x, w_proj, w_out, cols, rows, ffn_rw, ffn_rb, fw1, fw2, out):
    ctx = ExitStack()
    with ctx:
        def sb(name, shape, dt=F32):
            return ctx.enter_context(nc.sbuf_tensor(name, shape, dt))

        def sem(name):
            return ctx.enter_context(nc.semaphore(name))

        xs = sb("xs", [128, NB * T])
        ys = sb("ys", [128, NB * T])
        n2t = sb("n2t", [128, NB * T])
        n2sum = sb("n2sum", [128, NB])
        mixp = sb("mixp", [128, NB * NM])
        wp = sb("wp", [128, 9, 128])
        wo = sb("wo", [128, NM, 128])
        col = sb("col", [128, 12])
        qbias = sb("qbias", [128, NM])
        row = sb("row", [1, NM * 128])
        rbb = sb("rbb", [128, NM])
        frw = sb("frw", [128, NE])
        frb = sb("frb", [NB, NE])
        ident = sb("ident", [128, 128])
        identb = sb("identb", [128, 128], BF16)
        ones = sb("ones", [1, 128])
        onerow = sb("onerow", [2, H * T], BF16)
        BQ, BK, BV, G1, B1, G2, B2, RW = 0, 2, 4, 6, 7, 8, 9, 10

        qs = [sb(f"qs{i}", [128, H, T], BF16) for i in range(3)]
        ks = [sb(f"ks{i}", [128, H, T], BF16) for i in range(3)]
        vext = [sb(f"vext{i}", [128, QT * H, VW]) for i in range(3)]
        probs = sb("probs", [128, H, QT * T])
        qk = sb("qk", [128, 2 * T])
        parts = sb("parts", [128, 6, T], BF16)
        rest = sb("rest", [128, 2 * T])
        rowmax = sb("rowmax", [128, 2, QT, HALF])
        shift = sb("shift", [128, 2, QT, 2 * HALF], BF16)
        shiftrow = sb("shiftrow", [2 * HALF, 2, T], BF16)
        heads_out = sb("heads_out", [128, 2, 512])
        inv = sb("inv", [128, 2, QT, HALF])
        context = sb("context", [128, QT, 128])
        ct = [sb(f"ct{m}", [128, T]) for m in range(NM)]
        nta = sb("nta", [128, T])
        n1t = sb("n1t", [128, T])
        n1sum = sb("n1sum", [128, 1])
        n1sumb = sb("n1sumb", [128, 128])
        u0 = sb("u0", [128, T])
        u1 = sb("u1", [128, T])
        u2 = sb("u2", [128, T])
        t1 = sb("t1", [128, T])
        st = {s: (sb(f"st{s}", [128, QT, 6]), sb(f"mv{s}", [128, QT, 2]), sb(f"rs{s}", [128, QT])) for s in (*"xayz", "f0", "f1")}
        var_eps = {s: sb(f"var_eps{s}", [128, QT]) for s in (*"xaynz", "f0", "f1")}
        minus_half = sb("minus_half", [128, QT])
        r2 = sb("r2", [128, 2 * QT])
        r3 = sb("r3", [128, QT])
        lg = sb("lg", [128, 10])

        s_ps = [ctx.enter_context(nc.psum_tensor(f"s_ps{i}", [128, 512], F32)) for i in range(2)]
        e_ps = [ctx.enter_context(nc.psum_tensor(f"e_ps{i}", [128, 512], F32)) for i in range(2)]
        o_ps = [ctx.enter_context(nc.psum_tensor(f"o_ps{i}", [128, 512], F32)) for i in range(2)]
        misc = {b: ctx.enter_context(nc.psum_tensor(f"misc{b}", [128, 512], F32)) for b in "XY"}

        scratch = nc.dram_tensor("part_scratch", (3, 6, KD, H, T), BF16, kind="Internal").ap()

        def part(p):
            return parts[:, p:6 - p:5 - 2 * p, :]

        def both(buf):
            return buf[:, :].rearrange("p (j n) -> p j n", j=2)

        inv_std = {s: sem(f"inv_std_{s}") for s in "xaynzf"}
        const_in = sem("const_in")
        wp_a_in = sem("wp_a_in")
        x_in = [sem(f"x_in{i}") for i in range(3)]
        passed = {e: sem(f"passed_{e}") for e in ("dve", "pool", "sp")}
        zeroed = sem("zeroed")
        ones_in = sem("ones_in")
        pool_const = sem("pool_const")
        xn = sem("xn")
        xt_ps = sem("xt_ps")
        xt_done = sem("xt_done")
        qk_ps = sem("qk_ps")
        qk_out = sem("qk_out")
        onerow_set = sem("onerow_set")
        qbias_set = sem("qbias_set")
        split = sem("split")
        parts_out = sem("parts_out")
        stacked = [sem(f"stacked{i}") for i in range(3)]
        v_ps = sem("v_ps")
        v_out = sem("v_out")
        s_ready = sem("s_ready")
        s_max = sem("s_max")
        shift_made = sem("shift_made")
        shift_ps = sem("shift_ps")
        shift_out = sem("shift_out")
        shift_in = [sem(f"shift_in{i}") for i in range(2)]
        e_ready = sem("e_ready")
        e_done = sem("e_done")
        pv = sem("pv")
        o_saved = sem("o_saved")
        o_ps_t = sem("o_ps_t")
        ctx_done = sem("ctx_done")
        an = sem("an")
        n1_ps = sem("n1_ps")
        n1_out = sem("n1_out")
        n1sum_b = sem("n1sum_b")
        route_ps = sem("route_ps")
        route_v = sem("route_v")
        route_e = sem("route_e")
        ct_ps = sem("ct_ps")
        ct_out = sem("ct_out")
        mix_ps = sem("mix_ps")
        zn = sem("zn")
        n2_ps = sem("n2_ps")
        n2_out = sem("n2_out")

        NX, NA, NZ, NR = 7, 20, 9, 6

        fr = sb("fr", [NB, 48])
        top = sb("top", [NB, 8])
        topi = sb("topi", [NB, 8], U32)
        taken_p = sb("taken_p", [128, NB * TOPK])
        taken_i = sb("taken_i", [1, NB * 8], U32)
        w1 = sb("w1", [128, NE, F])
        w2 = sb("w2", [128, NE, FC * D])
        hidden = [probs[:, i * TOPK:(i + 1) * TOPK, :] for i in range(2)]
        w1s = [probs[:, 2 * TOPK + i, :].rearrange("p (e f) -> p e f", e=TOPK) for i in range(2)]
        w2s = [probs[:, 3 * TOPK + i, :].rearrange("p (e n) -> p e n", e=TOPK) for i in range(2)]
        z = [sb(f"z{i}", [128, T]) for i in range(2)]
        normed = [sb(f"normed{i}", [128, T]) for i in range(2)]
        result = [sb(f"result{i}", [128, T]) for i in range(2)]
        p_scratch = nc.dram_tensor("p_scratch", (NB, TOPK), F32, kind="Internal").ap()
        i_scratch = nc.dram_tensor("i_scratch", (NB, 8), U32, kind="Internal").ap()
        fr_ps = sem("fr_ps")
        fr_v = sem("fr_v")
        fr_e = sem("fr_e")
        routed = sem("routed")
        w_in = sem("w_in")
        w1_picked = sem("w1_picked")
        w2_scaled = sem("w2_scaled")
        h_ps = sem("h_ps")
        h_act = sem("h_act")
        eo_ps = sem("eo_ps")
        fz = sem("fz")
        fn = sem("fn")
        finished = sem("finished")
        stored = [sem(f"stored{i}") for i in range(2)]
        NF = 6

        block = ctx.enter_context(nc.Block())

        @block.sync
        def _(sp):
            def load_x(i, first, last):
                sp.dma_start(xs[:, :].rearrange("p (b q d) -> p b q d", b=NB, q=QT)[:, first:last],
                             x.rearrange("b (q p) d -> p b q d", p=128)[:, first:last]).then_inc(x_in[i], 16)

            load_x(0, 0, 1)
            sp.dma_start(wp[:, 0:3, :].rearrange("p c n -> p (c n)"), w_proj[:, 0:3 * D]).then_inc(wp_a_in, 16)
            load_x(1, 1, 3)
            for dst, src in ((col[:, :], cols), (wp[:, 3:9, :].rearrange("p c n -> p (c n)"), w_proj[:, 3 * D:9 * D]),
                             (wo[:, :, :], w_out.rearrange("m p n -> p m n")),
                             (row[:, :], rows[0:1, 0:NM * 128]), (frw[:, :], ffn_rw),
                             (rbb[:, :], rows[0:1, NM * 128:NM * 128 + NM].to_broadcast([128, NM])),
                             (frb[:, :], ffn_rb.to_broadcast([NB, NE]))):
                sp.dma_start(dst, src).then_inc(const_in, 16)
            load_x(2, 3, NB)

            def ones_rows(i):
                sp.dma_start(ks[i][SHIFT:SHIFT + 2, :, :], onerow[:, :].rearrange("p (h n) -> p h n", h=H)).then_inc(ones_in, 16)

            def shift_rows(k, kind, off, half):
                i = place(kind, k, off)
                wait(sp, shift_out, 2 * i + half + 1)
                for part in range(2):
                    sp.dma_start(qs[ring3(kind, k, off)][SHIFT + part:SHIFT + part + 1, half * HALF:(half + 1) * HALF, :],
                                 shiftrow[part * HALF:(part + 1) * HALF, half, :]).then_inc(shift_in[half], 16)

            def store_parts(k, kind, off):
                i, r = place(kind, k, off), ring3(kind, k, off)
                wait(sp, split, 3 * i + 3)
                alone(sp, passed["sp"])
                wait(sp, stacked[r], 96 * turn3(kind, k, off))
                sp.dma_start(scratch[r].rearrange("c d h n -> (d h) c n"), parts[:, :, :]).then_inc(parts_out, 16)

            def stack_heads(k, kind, off):
                i, r = place(kind, k, off), ring3(kind, k, off)
                wait(sp, parts_out, 16 * (i + 1))
                alone(sp, passed["sp"])
                wait(sp, e_ready, 16 * (i - 2))
                for c, n in RUNS:
                    for dst, first in ((qs, 0), (ks, 6 - n)):
                        sp.dma_start(dst[r][KD * c:KD * (c + n), :, :],
                                     scratch[r, first:first + n].rearrange("c d h n -> (c d) h n")).then_inc(stacked[r], 16)

            def step(k):
                for _slot, (kind, off), (mkind, moff), _last in SLOTS:
                    if real(k, off):
                        shift_rows(k, kind, off, 1)
                    if real(k, off + 1):
                        store_parts(k, kind, off + 1)
                    if real(k, moff):
                        shift_rows(k, mkind, moff, 0)
                    if real(k, off + 1):
                        stack_heads(k, kind, off + 1)

            for b in range(3):
                store_parts(0, "A", b)
                sp.wait_ge(zeroed, 2 * b + 2)
                stack_heads(0, "A", b)
                if b == 1:
                    sp.wait_ge(onerow_set, 1)
                    ones_rows(0)
                    ones_rows(1)
            ones_rows(2)
            shift_rows(0, "A", 0, 0)
            for b in range(2):
                shift_rows(0, "A", b, 1)
                shift_rows(0, "A", b + 1, 0)
            shift_rows(0, "A", 2, 1)
            sp.dma_start(w1[:, :, :], fw1.rearrange("e p f -> p e f")).then_inc(w_in, 16)
            sp.dma_start(w2[:, :, :].rearrange("p e (c n) -> p e c n", c=FC), fw2.rearrange("e (c p) n -> p e c n", p=128)).then_inc(w_in, 16)
            for kind, b in (("B0", 0), ("B1", 0), ("A", 3)):
                store_parts(0, kind, b)
                stack_heads(0, kind, b)
            shift_rows(0, "B0", 0, 0)
            run_steps(sp, step)

            sp.wait_ge(fr_v, 11)
            sp.dma_start(p_scratch, fr[:, 40:40 + TOPK]).then_inc(routed, 16)
            sp.dma_start(i_scratch, topi[:, :]).then_inc(routed, 16)
            sp.wait_ge(routed, 32)
            sp.dma_start(taken_p[:, :], p_scratch.rearrange("(o b) e -> o (b e)", o=1).to_broadcast([128, NB * TOPK])).then_inc(routed, 16)
            sp.dma_start(taken_i[:, :], i_scratch.rearrange("(o b) e -> o (b e)", o=1)).then_inc(routed, 16)
            sp.wait_ge(routed, 64)

            def store_result(b, par):
                sp.wait_ge(finished, b + 1)
                sp.dma_start(out[bass.ds(b, 1), :, :].rearrange("o (q p) d -> p (o q) d", p=128),
                             result[par][:, :].rearrange("p (q d) -> p q d", q=QT)).then_inc(stored[par], 16)

            with sp.Fori(0, NB // 2) as g:
                for par in range(2):
                    store_result(2 * g + par, par)
            for par in range(2):
                sp.wait_ge(stored[par], 16 * (NB // 2))

        @block.gpsimd
        def _(pool):
            pool.memset(ident[:, :], 0.0).then_inc(pool_const, 1)
            pool.memset(identb[:, :], 0.0).then_inc(pool_const, 1)
            pool.memset(ones[:, :], 1.0).then_inc(pool_const, 1)
            pool.wait_ge(pool_const, 3)
            for m in (ident, identb):
                pool.affine_select(out=m[:, :], in_=m[:, :], compare_op=ALU.not_equal, fill=1.0, base=0,
                                   pattern=[[-1, 128]], channel_multiplier=1).then_inc(pool_const, 1)
            pool.memset(minus_half[:, :], -0.5).then_inc(pool_const, 1)
            for i in range(3):
                pool.memset(vext[i][:, :, :], 0.0).then_inc(pool_const, 1)
            pool.wait_ge(pool_const, 9)
            for i in range(3):
                pool.memset(vext[i][:, :, KD:KD + 1], 1.0).then_inc(pool_const, 1)

            def split_parts(k, kind, off, step):
                i = place(kind, k, off)
                if step == 0:
                    wait(pool, qk_out, 3 * i + 3)
                    wait(pool, split, 3 * i)
                    pool.tensor_tensor(both(rest), both(qk), part(0), ALU.subtract).then_inc(split, 1)
                elif step == 1:
                    pool.wait_ge(split, 3 * i + 1)
                    wait(pool, parts_out, 16 * i)
                    alone(pool, passed["pool"])
                    pool.tensor_copy(part(1), both(rest)).then_inc(split, 1)
                else:
                    pool.wait_ge(split, 3 * i + 2)
                    pool.tensor_tensor(part(2), both(rest), part(1), ALU.subtract).then_inc(split, 1)

            STD = {"x": (xn, NX, 5), "a": (an, NA, 5), "y": (an, NA, 13), "n": (an, NA, 18), "z": (zn, NZ, 7)}

            def invert_std(k, s, off):
                b = k + off
                sem_, per, done = STD[s]
                pool.wait_ge(sem_, per * b + done)
                wait(pool, inv_std[s], b)
                pool.tensor_tensor(r3[:, :] if s == "n" else st[s][2][:, :], var_eps[s][:, :], minus_half[:, :], ALU.pow).then_inc(inv_std[s], 1)

            def spread_sum(k, kind, off):
                b = k + off
                wait(pool, n1_out, b + 1)
                wait(pool, route_ps, b)
                alone(pool, passed["pool"])
                pool.tensor_copy(n1sumb[:, :], n1sum[:, 0:1].to_broadcast([128, 128])).then_inc(n1sum_b, 1)

            def step(k):
                for what, *args in WORK:
                    if real(k, args[1]):
                        what(k, *args)

            WORK = [(split_parts, "B0", 1, 0), (invert_std, "z", -1), (split_parts, "B0", 1, 1), (split_parts, "B0", 1, 2), (invert_std, "a", 2),
                    (invert_std, "y", 2), (split_parts, "B1", 1, 0), (invert_std, "n", 2), (split_parts, "B1", 1, 1), (split_parts, "B1", 1, 2),
                    (invert_std, "x", 4), (split_parts, "A", 4, 0), (split_parts, "A", 4, 1), (split_parts, "A", 4, 2), (spread_sum, "A", 2)]
            def start(*work):
                for what, *args in work:
                    what(0, *args)

            start((invert_std, "x", 0), (invert_std, "x", 1), *((split_parts, "A", 0, n) for n in range(3)))
            pool.memset(onerow[:, :], 1.0).then_inc(onerow_set, 1)
            pool.wait_ge(const_in, 16 * 7)
            pool.tensor_scalar(qbias[:, :], col[:, BQ:BQ + NM], KD ** -0.5, None, ALU.mult).then_inc(qbias_set, 1)
            start((invert_std, "x", 2), *((split_parts, "A", b, n) for b in (1, 2) for n in range(3)), (invert_std, "x", 3),
                  (invert_std, "a", 0), (invert_std, "y", 0), (invert_std, "n", 0), (split_parts, "B0", 0, 0), (spread_sum, "A", 0),
                  (split_parts, "B0", 0, 1), (split_parts, "B0", 0, 2), (invert_std, "a", 1), (invert_std, "y", 1), (invert_std, "n", 1),
                  *((split_parts, "B1", 0, n) for n in range(3)), (spread_sum, "A", 1), *((split_parts, "A", 3, n) for n in range(3)))
            run_steps(pool, step)

            def last_std(b, par):
                pool.wait_ge(fz, NF * (b + 1))
                pool.tensor_tensor(st[f"f{par}"][2][:, :], var_eps[f"f{par}"][:, :], minus_half[:, :], ALU.pow).then_inc(inv_std["f"], 1)

            def add_result(b, par, half_count):
                pool.wait_ge(fn, 2 * b + 2)
                wait(pool, stored[par], 16 * (half_count - 1))
                alone(pool, passed["pool"])
                pool.tensor_tensor(result[par][:, :], normed[par][:, :], xs[:, bass.ds(b * T, T)], ALU.add).then_inc(finished, 1)

            last_std(0, 0)
            add_result(0, 0, 1)
            last_std(1, 1)
            with pool.Fori(1, NB // 2) as g:
                add_result(2 * g - 1, 1, g)
                last_std(2 * g, 0)
                add_result(2 * g, 0, g + 1)
                last_std(2 * g + 1, 1)
            add_result(NB - 1, 1, NB // 2)

        @block.tensor
        def _(pe):
            pe.wait_ge(pool_const, 5)
            pe.wait_ge(wp_a_in, 16)
            at = {"X": None, "Y": None}

            def read(stage, kind, k, off):
                b = k + off
                if stage in ("mix", "norm2"):
                    return {"mix": (zn, NZ * b + 2), "norm2": (n2_out, b + 1)}[stage]
                i = place(kind, k, off)
                return {"shift0": (shift_out, 2 * i + 1), "shift1": (shift_out, 2 * i + 2), "project": (qk_out, 3 * i + 2),
                        "turn0": (ctx_done, 4 * i + 2), "turn1": (ctx_done, 4 * i + 4), "route": (route_v, NR * b + 1),
                        "values": (v_out, i + 1), "context": (ct_out, 2 * b + KINDS.index(kind)),
                        "norm_x": (xt_done, b + 1), "norm1": (n1_out, b + 1)}[stage]

            def take(bank, stage, kind, k, off):
                if at[bank]:
                    pe.wait_ge(*read(at[bank][0], at[bank][1], k, at[bank][2]))
                at[bank] = (stage, kind, off)
                return misc[bank]

            def turn_tiles(dst, src, done):
                for q in range(QT):
                    last = pe.transpose(dst[:, q * 128:(q + 1) * 128], src[:, q * 128:(q + 1) * 128], ident[:, :])
                last.then_inc(done, 1)

            def work(k, stage, kind, off, bank):
                b = k + off
                i = place(kind, k, off) if kind != "B" else None
                m = KINDS.index(kind) - 1 if kind != "B" else None
                if stage in ("shift0", "shift1"):
                    half = int(stage[-1])
                    pe.wait_ge(shift_made, 4 * i + 2 * half + 2)
                    ps = take(bank, stage, kind, k, off)[:, :].bitcast(BF16)
                    for q in range(QT):
                        last = pe.transpose(ps[0:2 * HALF, q * 128:(q + 1) * 128], shift[:, half, q, :], identb[:, :])
                    last.then_inc(shift_ps, 1)
                elif stage in ("turn0", "turn1"):
                    half = int(stage[-1])
                    pe.wait_ge(o_saved, 2 * i + half + 1)
                    ps = take(bank, stage, kind, k, off)
                    for q in range(QT):
                        for s in range(2):
                            last = pe.transpose(ps[:, q * 256 + s * 128:q * 256 + (s + 1) * 128],
                                                heads_out[:, half, s * 256 + q * 128:s * 256 + (q + 1) * 128], ident[:, :])
                    last.then_inc(o_ps_t, 1)
                elif stage == "project":
                    if kind == "A":
                        pe.wait_ge(xt_done, b + 1)
                    else:
                        pe.wait_ge(n1_out, b + 1)
                    ps = take(bank, stage, kind, k, off)
                    for j in range(2):
                        last = pe.matmul(ps[:, j * T:(j + 1) * T], wp[:, 3 * (m + 1) + j, :], (nta if kind == "A" else n1t)[:, :],
                                         start=True, stop=True)
                    last.then_inc(qk_ps, 1)
                elif stage == "values":
                    ps = take(bank, stage, kind, k, off)
                    for q in range(QT):
                        last = pe.matmul(ps[:, q * 128:(q + 1) * 128], (nta if kind == "A" else n1t)[:, q * 128:(q + 1) * 128],
                                         wp[:, 3 * (m + 1) + 2, :], start=True, stop=True)
                    last.then_inc(v_ps, 1)
                elif stage == "norm_x":
                    pe.wait_ge(xn, NX * b + 7)
                    turn_tiles(take(bank, stage, kind, k, off), u0, xt_ps)
                elif stage == "norm1":
                    pe.wait_ge(an, NA * b + 20)
                    turn_tiles(take(bank, stage, kind, k, off), u1, n1_ps)
                elif stage == "norm2":
                    pe.wait_ge(zn, NZ * b + 9)
                    turn_tiles(take(bank, stage, kind, k, off), u2, n2_ps)
                elif stage == "route":
                    pe.wait_ge(n1sum_b, b + 1)
                    ps = take(bank, stage, kind, k, off)
                    pe.matmul(ps[:, 0:NM], n1sumb[:, :], col[:, RW:RW + NM], start=True, stop=True).then_inc(route_ps, 1)
                elif stage == "context":
                    pe.wait_ge(ctx_done, 4 * i + 4)
                    ps = take(bank, stage, kind, k, off)
                    for q in range(QT):
                        last = pe.transpose(ps[:, q * 128:(q + 1) * 128], context[:, q, :], ident[:, :])
                    last.then_inc(ct_ps, 1)
                elif stage == "mix":
                    pe.wait_ge(ct_out, 2 * b + 2)
                    ps = take(bank, stage, kind, k, off)
                    for e in range(NM):
                        for q in range(QT):
                            o = ps[:, e * T + q * 128:e * T + (q + 1) * 128]
                            pe.matmul(o, ct[e][:, q * 128:(q + 1) * 128], wo[:, e, :], start=True, stop=False)
                            last = pe.matmul(o, ones[:, :], row[:, e * 128:(e + 1) * 128], start=False, stop=True)
                    last.then_inc(mix_ps, 1)

            def scores(k, kind, off, h):
                i, r = place(kind, k, off), ring3(kind, k, off)
                if h == 0:
                    pe.wait_ge(stacked[r], 96 * (turn3(kind, k, off) + 1))
                wait(pe, s_max, 16 * i + h - 1)
                for q in range(QT):
                    last = pe.matmul(s_ps[h % 2][:, q * T:(q + 1) * T], qs[r][0:SHIFT, h, q * 128:(q + 1) * 128],
                                     ks[r][0:SHIFT, h, :], start=True, stop=True)
                last.then_inc(s_ready, 1)

            def shifted_scores(k, kind, off, h):
                i, r = place(kind, k, off), ring3(kind, k, off)
                if h % HALF == 0:
                    pe.wait_ge(shift_in[h // HALF], 32 * (i + 1))
                wait(pe, e_done, 16 * i + h - 1)
                for q in range(QT):
                    last = pe.matmul(e_ps[h % 2][:, q * T:(q + 1) * T], ks[r][:, h, q * 128:(q + 1) * 128],
                                     qs[r][:, h, :], start=True, stop=True)
                last.then_inc(e_ready, 1)

            def probs_v(k, kind, off, quad, q):
                i, r = place(kind, k, off), ring3(kind, k, off)
                if q == 0:
                    pe.wait_ge(e_done, 16 * i + 4 * quad + 4)
                    if quad == 0:
                        pe.wait_ge(v_out, i + 1)
                    if quad % 2 == 0:
                        wait(pe, o_saved, 2 * i + quad // 2 - 1)
                o = o_ps[quad // 2]
                for g in range(4):
                    h = 4 * quad + g
                    last = pe.matmul(o[VW * g:VW * (g + 1), (quad % 2) * T:(quad % 2 + 1) * T], vext[r][:, q * H + h, :],
                                     probs[:, h, q * T:(q + 1) * T], start=(q == 0), stop=(q == QT - 1))
                if q == QT - 1:
                    last.then_inc(pv, 1)

            def step(k):
                for slot in SLOTS:
                    run_slot(k, *slot)
                for bank in at:
                    if at[bank]:
                        at[bank] = at[bank][:2] + (at[bank][2] - 1,)

            def run_slot(k, name, attend, maxima, last):
                for h in heads_of(attend, maxima):
                    if maxima and real(k, maxima[1]):
                        scores(k, *maxima, h)
                    if attend and real(k, attend[1]):
                        shifted_scores(k, *attend, h)
                    if h in (1, 3) and last and real(k, last[1]):
                        probs_v(k, *last, 3, h // 2)
                    if h % 2 and h >= 5 and attend and real(k, attend[1]):
                        probs_v(k, *attend, (h - 5) // 4, (h - 5) // 2 % 2)
                    for when, stage, kind, off, bank in TENSOR_WORK[name]:
                        if when == h and real(k, off):
                            work(k, stage, kind, off, bank)

            for slot in START:
                if slot[0] == "maxima A0":
                    pe.wait_ge(zeroed, 6)
                if slot[0] == "attend A0":
                    pe.wait_ge(ones_in, 16 * 3)
                    pe.wait_ge(const_in, 16 * 7)
                run_slot(0, *slot)
            run_steps(pe, step)

            pe.wait_ge(n2_out, NB)
            pe.wait_ge(zn, NZ * NB)
            pe.matmul(misc["X"][0:NB, 0:NE], n2sum[:, :], frw[:, :], start=True, stop=True).then_inc(fr_ps, 1)

            def up(b, par):
                wait(pe, h_act, 2 * b - 2)
                for e in range(TOPK):
                    pe.wait_ge(w1_picked, 2 * b + e + 1)
                    for c in range(FC):
                        last = pe.matmul((s_ps, e_ps)[par][e][:, c * T:(c + 1) * T],
                                         w1s[par][:, e, c * 128:(c + 1) * 128],
                                         n2t[:, bass.ds(b * T, T)], start=True, stop=True)
                    last.then_inc(h_ps, 1)

            def down(b, par):
                pe.wait_ge(h_act, 2 * b + 2)
                pe.wait_ge(w2_scaled, 2 * b + 2)
                wait(pe, fz, NF * (b - 2) + 1)
                for q in range(QT):
                    for e in range(TOPK):
                        for c in range(FC):
                            last = pe.matmul(o_ps[par][:, q * 128:(q + 1) * 128],
                                             hidden[par][:, e, c * T + q * 128:c * T + (q + 1) * 128], w2s[par][:, e, c * D:(c + 1) * D],
                                             start=(e == 0 and c == 0), stop=(e == TOPK - 1 and c == FC - 1))
                last.then_inc(eo_ps, 1)

            up(0, 0)
            up(1, 1)
            down(0, 0)
            up(2, 0)
            down(1, 1)
            with pe.Fori(1, NB // 2 - 1) as g:
                up(2 * g + 1, 1)
                down(2 * g, 0)
                up(2 * g + 2, 0)
                down(2 * g + 1, 1)
            up(NB - 1, 1)
            down(NB - 2, 0)
            down(NB - 1, 1)

        @block.scalar
        def _(act):

            def exps(k, kind, off, h):
                i = place(kind, k, off)
                if h % 4 == 0:
                    wait(act, pv, 4 * i + h // 4 - 3)
                act.wait_ge(e_ready, 16 * i + h + 1)
                act.activation(probs[:, h, :], e_ps[h % 2][:, :], ACT.Exp).then_inc(e_done, 1)

            def save_heads(k, kind, off, half):
                i = place(kind, k, off)
                act.wait_ge(pv, 4 * i + 2 * half + 2)
                wait(act, o_ps_t, 2 * i + half - 1)
                act.activation(heads_out[:, half, :], o_ps[half][:, :], ACT.Copy).then_inc(o_saved, 1)

            def save_shift(k, kind, off, half):
                i = place(kind, k, off)
                act.wait_ge(shift_ps, 2 * i + half + 1)
                wait(act, shift_in[half], 32 * i)
                ps = misc["Y"][:, :].bitcast(BF16)
                act.activation(shiftrow[:, half, :], ps[0:2 * HALF, 0:T], ACT.Copy).then_inc(shift_out, 1)

            def save_qk(k, kind, off):
                i, m = place(kind, k, off), KINDS.index(kind) - 1
                act.wait_ge(qk_ps, i + 1)
                wait(act, split, 3 * i - 2)
                if kind == "A":
                    act.activation(qk[:, 0:T], misc["Y"][:, 0:T], ACT.Copy, scale=D ** -0.5).then_inc(qk_out, 1)
                    act.activation(qk[:, T:2 * T], misc["Y"][:, T:2 * T], ACT.Copy).then_inc(qk_out, 1)
                else:
                    act.activation(qk[:, 0:T], misc["Y"][:, 0:T], ACT.Identity, bias=qbias[:, m:m + 1], scale=KD ** -0.5).then_inc(qk_out, 1)
                    act.activation(qk[:, T:2 * T], misc["Y"][:, T:2 * T], ACT.Identity, bias=col[:, BK + m:BK + m + 1]).then_inc(qk_out, 1)
                act.wait_ge(qk_out, 3 * i + 2)
                wait(act, parts_out, 16 * i)
                act.activation(part(0), both(qk), ACT.Copy).then_inc(qk_out, 1)

            def save_v(k, kind, off):
                i, r = place(kind, k, off), ring3(kind, k, off)
                act.wait_ge(v_ps, i + 1)
                wait(act, pv, 4 * (i - 2))
                act.activation(vext[r][:, :, 0:KD], misc["Y"][:, 0:T].rearrange("p (c d) -> p c d", d=KD), ACT.Copy).then_inc(v_out, 1)

            def save_norm_x(k, off):
                b = k + off
                act.wait_ge(xt_ps, b + 1)
                if real(k, off - 1):
                    act.wait_ge(v_ps, place("A", k, off - 1) + 1)
                act.activation(nta[:, :], misc["X"][:, 0:T], ACT.Copy).then_inc(xt_done, 1)

            def save_norm1(k, off):
                b = k + off
                act.wait_ge(n1_ps, b + 1)
                if real(k, off - 1):
                    act.wait_ge(v_ps, place("B1", k, off - 1) + 1)
                    act.wait_ge(n1sum_b, b)
                act.activation(n1t[:, :], misc["Y"][:, 0:T], ACT.Identity, bias=col[:, B1:B1 + 1], scale=col[:, G1:G1 + 1],
                               accum_out=n1sum[:, 0:1]).then_inc(n1_out, 1)

            def save_norm2(k, off):
                b = k + off
                act.wait_ge(n2_ps, b + 1)
                act.activation(n2t[:, bass.ds(b * T, T)], misc["X"][:, 0:T], ACT.Identity, bias=col[:, B2:B2 + 1],
                               scale=col[:, G2:G2 + 1], accum_out=n2sum[:, bass.ds(b, 1)]).then_inc(n2_out, 1)

            def save_context(k, kind, off):
                b, m = k + off, KINDS.index(kind) - 1
                act.wait_ge(ct_ps, 2 * b + m + 1)
                wait(act, mix_ps, b)
                act.activation(ct[m][:, :], misc["X"][:, 0:T], ACT.Identity, bias=col[:, BV + m:BV + m + 1]).then_inc(ct_out, 1)

            def route_exp(k, off):
                b = k + off
                act.wait_ge(route_v, NR * b + 3)
                act.activation(lg[:, 6:8], lg[:, 4:6], ACT.Exp).then_inc(route_e, 1)

            WORK = {
                "project A": [(0, save_norm_x, 0), (0, save_qk, "A", 0), (0, save_v, "A", 0), (0, save_norm_x, 1), (0, save_qk, "A", 1),
                              (0, save_v, "A", 1), (0, save_norm_x, 2)],
                "maxima A0": [(3, save_qk, "A", 2), (6, save_v, "A", 2), (11, save_shift, "A", 0, 0)],
                "attend A0": [(2, save_shift, "A", 0, 1), (8, save_norm_x, 3), (11, save_shift, "A", 1, 0), (12, save_heads, "A", 0, 0)],
                "attend A1": [(2, save_shift, "A", 1, 1), (4, save_heads, "A", 0, 1), (11, save_shift, "A", 2, 0), (12, save_heads, "A", 1, 0)],
                "attend A2": [(2, save_shift, "A", 2, 1), (4, save_heads, "A", 1, 1), (5, save_norm1, 0), (7, save_qk, "B0", 0), (9, save_v, "B0", 0),
                              (12, save_heads, "A", 2, 0), (15, save_qk, "B1", 0)],
                "turn to B": [(0, save_v, "B1", 0), (0, route_exp, 0), (0, save_norm1, 1), (0, save_qk, "A", 3)],
                "maxima B0": [(11, save_shift, "B0", 0, 0)],
                "B0": [(2, save_shift, "B0", 0, 1), (4, save_heads, "A", 2, 1), (5, save_qk, "B0", 1), (9, save_v, "A", 3),
                       (11, save_shift, "B1", 0, 0), (12, route_exp, 1), (12, save_heads, "B0", 0, 0)],
                "B1": [(2, save_shift, "B1", 0, 1), (4, save_heads, "B0", 0, 1), (5, save_qk, "B1", 1), (9, save_v, "B0", 1),
                       (10, save_norm2, -1), (11, save_shift, "A", 3, 0), (12, save_context, "B0", 0), (12, save_heads, "B1", 0, 0)],
                "A": [(2, save_shift, "A", 3, 1), (3, save_norm_x, 4), (4, save_heads, "B1", 0, 1), (6, save_qk, "A", 4), (9, save_v, "B1", 1),
                      (11, save_shift, "B0", 1, 0), (12, save_context, "B1", 0), (12, save_heads, "A", 3, 0), (13, save_norm1, 2)],
            }

            def step(k):
                for slot in SLOTS:
                    run_slot(k, *slot)

            def run_slot(k, name, attend, maxima, _last):
                for h in heads_of(attend, maxima):
                    if attend and real(k, attend[1]):
                        exps(k, *attend, h)
                    for when, what, *args in WORK[name]:
                        if when == h and real(k, args[1] if isinstance(args[0], str) else args[0]):
                            what(k, *args)

            for slot in START:
                if slot[0] == "project A":
                    act.wait_ge(pool_const, 12)
                if slot[0] == "attend A2":
                    act.wait_ge(const_in, 16 * 7)
                    act.wait_ge(qbias_set, 1)
                run_slot(0, *slot)
            run_steps(act, step)

            act.wait_ge(fr_v, 3)
            act.activation(fr[:, 24:32], fr[:, 16:24], ACT.Exp).then_inc(fr_e, 1)

            def gelus(b, par):
                wait(act, eo_ps, b - 1)
                for e in range(TOPK):
                    act.wait_ge(h_ps, 2 * b + e + 1)
                    act.activation(hidden[par][:, e, :], (s_ps, e_ps)[par][e][:, :], ACT.Gelu).then_inc(h_act, 1)

            def pick_experts(b, par):
                for e in range(TOPK):
                    expert = act.value_load(taken_i[0:1, bass.ds(b * 8 + e, 1)], min_val=0, max_val=NE - 1)
                    act.activation(w1s[par][:, e, :], w1[:, bass.ds(expert, 1), :].rearrange("p o f -> p (o f)"), ACT.Copy).then_inc(w1_picked, 1)

            act.wait_ge(w_in, 32)
            act.wait_ge(routed, 64)
            for par in range(2):
                pick_experts(par, par)
            for par in range(2):
                gelus(par, par)
                pick_experts(par + 2, par)
            with act.Fori(1, NB // 2 - 1) as g:
                for par in range(2):
                    gelus(2 * g + par, par)
                    pick_experts(2 * g + par + 2, par)
            for par in range(2):
                gelus(NB - 2 + par, par)

        @block.vector
        def _(dve):
            def maxima(k, kind, off, h):
                i = place(kind, k, off)
                if h % HALF == 0:
                    wait(dve, shift_made, 4 * i + 2 * (h // HALF) - 2)
                dve.wait_ge(s_ready, 16 * i + h + 1)
                dve.tensor_reduce(rowmax[:, h // HALF, :, h % HALF:h % HALF + 1], s_ps[h % 2][:, :].rearrange("p (q n) -> p q n", q=QT),
                                  AX_X, ALU.max).then_inc(s_max, 1)

            def make_shift(k, kind, off, half):
                i = place(kind, k, off)
                dve.wait_ge(s_max, 16 * i + HALF * (half + 1))
                wait(dve, shift_ps, 2 * i + half - 1)
                hi, lo = shift[:, half, :, 0:HALF], shift[:, half, :, HALF:2 * HALF]
                dve.tensor_scalar(hi, rowmax[:, half, :, :], -1.0, None, ALU.mult).then_inc(shift_made, 1)
                dve.wait_ge(shift_made, 4 * i + 2 * half + 1)
                dve.scalar_tensor_tensor(out=lo, in0=rowmax[:, half, :, :], scalar=-1.0, in1=hi, op0=ALU.mult,
                                         op1=ALU.subtract).then_inc(shift_made, 1)

            def invert_sums(k, kind, off, half):
                i = place(kind, k, off)
                dve.wait_ge(o_ps_t, 2 * i + half + 1)
                wait(dve, ctx_done, 4 * i + 2 * half - 2)
                sums = misc["X"][:, :].rearrange("p (q s c) -> p q s c", q=QT, c=VW)[:, :, :, KD]
                dve.reciprocal(inv[:, half, :, :], sums).then_inc(ctx_done, 1)

            def normalise(k, kind, off, half):
                i = place(kind, k, off)
                dve.wait_ge(ctx_done, 4 * i + 2 * half + 1)
                if (last := before(kind, k, off)) and half == 0:
                    b = k + last[1]
                    if last[0] == "A":
                        dve.wait_ge(an, NA * b + 7)
                    else:
                        dve.wait_ge(ct_ps, 2 * b + KINDS.index(last[0]))
                heads = misc["X"][:, :].rearrange("p (q s c) -> p q s c", q=QT, c=VW)[:, :, :, 0:KD]
                dst = context[:, :, half * 64:(half + 1) * 64].rearrange("p q (s d) -> p q s d", d=KD)
                dve.tensor_tensor(dst, heads, inv[:, half, :, :].unsqueeze(3).to_broadcast([128, QT, HALF, KD]),
                                  ALU.mult).then_inc(ctx_done, 1)

            def stats(sem_, base, done, src, s):
                wait(dve, sem_, base + done)
                alone(dve, passed["dve"])
                for q in range(QT):
                    dve.bn_stats(st[s][0][:, q, :], src(q)).then_inc(sem_, 1)

            def aggregate(sem_, base, done, s):
                dve.wait_ge(sem_, base + done)
                alone(dve, passed["dve"])
                for q in range(QT):
                    dve.bn_aggr(st[s][1][:, q, :], st[s][0][:, q, :]).then_inc(sem_, 1)

            def add_eps(sem_, base, done, s, eps):
                dve.wait_ge(sem_, base + done)
                dve.tensor_scalar(var_eps[s][:, :], st[s][1][:, :, 1], eps, None, ALU.add).then_inc(sem_, 1)

            def scale_to(sem_, b, s, dst, src):
                dve.wait_ge(inv_std[s], b + 1)
                for q in range(QT):
                    dve.tensor_scalar(dst(q), src(q), st[s][1][:, q, 0:1], st[s][2][:, q:q + 1], ALU.subtract, ALU.mult).then_inc(sem_, 1)

            def tile_of(buf):
                return lambda q: buf[:, q * 128:(q + 1) * 128]

            def tile_at(buf, b):
                return lambda q: buf[:, bass.ds(b * T + q * 128, 128)]

            def norm_x(k, off, part):
                b = k + off
                if part == 0:
                    if known(k):
                        dve.wait_ge(x_in[(b > 0) + (b > 2)], 16)
                    stats(xn, NX * b, 0, tile_at(xs, b), "x")
                elif part == 1:
                    aggregate(xn, NX * b, 2, "x")
                elif part == 2:
                    add_eps(xn, NX * b, 4, "x", EPS_OUTER)
                else:
                    wait(dve, xt_ps, b)
                    scale_to(xn, b, "x", tile_of(u0), tile_at(xs, b))

            def first_block(k, off, part):
                b = k + off
                base = NA * b
                if part == 0:
                    dve.wait_ge(ctx_done, 4 * place("A", k, off) + 4)
                    stats(an, base, 0, lambda q: context[:, q, :], "a")
                elif part == 1:
                    aggregate(an, base, 2, "a")
                elif part == 2:
                    add_eps(an, base, 4, "a", EPS_OUTER)
                elif part == 3:
                    scale_to(an, b, "a", tile_of(t1), lambda q: context[:, q, :])
                elif part == 4:
                    dve.wait_ge(an, base + 7)
                    x_b = xs[:, bass.ds(b * T, T)]
                    dve.tensor_tensor(x_b, t1[:, :], x_b, ALU.add).then_inc(an, 1)
                elif part == 5:
                    stats(an, base, 8, tile_at(xs, b), "y")
                elif part == 6:
                    aggregate(an, base, 10, "y")
                elif part == 7:
                    add_eps(an, base, 12, "y", EPS_OUTER)
                elif part == 8:
                    scale_to(an, b, "y", tile_at(ys, b), tile_at(xs, b))
                elif part == 9:
                    dve.wait_ge(an, base + 15)
                    dve.tensor_tensor(r2[:, 0:QT], st["y"][1][:, :, 1], st["y"][2][:, :], ALU.mult).then_inc(an, 1)
                elif part == 10:
                    dve.wait_ge(an, base + 16)
                    dve.tensor_tensor(r2[:, QT:2 * QT], r2[:, 0:QT], st["y"][2][:, :], ALU.mult).then_inc(an, 1)
                elif part == 11:
                    dve.wait_ge(an, base + 17)
                    dve.tensor_scalar(var_eps["n"][:, :], r2[:, QT:2 * QT], EPS_INNER, None, ALU.add).then_inc(an, 1)
                else:
                    dve.wait_ge(inv_std["n"], b + 1)
                    wait(dve, n1_ps, b)
                    for q in range(QT):
                        dve.tensor_scalar(tile_of(u1)(q), tile_at(ys, b)(q), r3[:, q:q + 1], None, ALU.mult).then_inc(an, 1)

            def second_block(k, off, part):
                b = k + off
                base = NZ * b
                if part < 2:
                    if part == 0:
                        dve.wait_ge(mix_ps, b + 1)
                        dve.wait_ge(an, NA * b + 15)
                        dve.wait_ge(route_v, NR * b + 6)
                    else:
                        dve.wait_ge(zn, base + 1)
                    y_b = ys[:, bass.ds(b * T, T)]
                    dve.scalar_tensor_tensor(out=y_b, in0=misc["X"][:, part * T:(part + 1) * T], scalar=mixp[:, bass.ds(b * NM + part, 1)],
                                             in1=y_b, op0=ALU.mult, op1=ALU.add).then_inc(zn, 1)
                elif part == 2:
                    stats(zn, base, 2, tile_at(ys, b), "z")
                elif part == 3:
                    aggregate(zn, base, 4, "z")
                elif part == 4:
                    add_eps(zn, base, 6, "z", EPS_INNER)
                else:
                    wait(dve, n2_ps, b)
                    scale_to(zn, b, "z", tile_of(u2), tile_at(ys, b))

            def route(k, off, part):
                b = k + off
                dve.wait_ge(*((route_ps, b + 1) if part == 0 else (route_v, NR * b + part)))
                if part == 0:
                    wait(dve, route_v, NR * b)
                    op = dve.scalar_tensor_tensor(out=lg[:, 0:2], in0=misc["Y"][:, 0:NM], scalar=1.0 / T, in1=rbb[:, :], op0=ALU.mult, op1=ALU.add)
                elif part == 1:
                    op = dve.tensor_reduce(lg[:, 2:3], lg[:, 0:2], AX_X, ALU.max)
                elif part == 2:
                    wait(dve, route_e, b)
                    op = dve.tensor_scalar(lg[:, 4:6], lg[:, 0:2], lg[:, 2:3], None, ALU.subtract)
                elif part == 3:
                    dve.wait_ge(route_e, b + 1)
                    op = dve.tensor_reduce(lg[:, 8:9], lg[:, 6:8], AX_X, ALU.add)
                elif part == 4:
                    op = dve.reciprocal(lg[:, 9:10], lg[:, 8:9])
                else:
                    op = dve.tensor_scalar(mixp[:, bass.ds(b * NM, NM)], lg[:, 6:8], lg[:, 9:10], None, ALU.mult)
                op.then_inc(route_v, 1)

            WORK = {
                "project A": [],
                "maxima A0": [(8, make_shift, "A", 0, 0), (15, make_shift, "A", 0, 1)],
                "attend A0": [(h, norm_x, 3, n) for n, h in enumerate((1, 2, 3, 5))]
                + [(8, make_shift, "A", 1, 0), (15, make_shift, "A", 1, 1), (15, invert_sums, "A", 0, 0)],
                "attend A1": [(0, normalise, "A", 0, 0), (7, invert_sums, "A", 0, 1), (8, normalise, "A", 0, 1), (8, make_shift, "A", 2, 0)]
                + [(h, first_block, 0, n) for n, h in enumerate((9, 10, 10, 12, 13, 13, 14, 14))]
                + [(15, make_shift, "A", 2, 1), (15, invert_sums, "A", 1, 0)],
                "attend A2": [(0, first_block, 0, n) for n in (8, 9, 10, 11)] + [(0, normalise, "A", 1, 0), (1, first_block, 0, 12)]
                + [(7, invert_sums, "A", 1, 1), (8, normalise, "A", 1, 1)] + [(8, first_block, 1, n) for n in range(9)]
                + [(15, invert_sums, "A", 2, 0)],
                "turn to B": [(0, first_block, 1, n) for n in range(9, 13)] + [(0, route, 0, n) for n in range(6)],
                "maxima B0": [(8, make_shift, "B0", 0, 0), (15, make_shift, "B0", 0, 1)],
                "B0": [(0, normalise, "A", 2, 0), (7, invert_sums, "A", 2, 1), (8, normalise, "A", 2, 1), (8, make_shift, "B1", 0, 0),
                       (15, make_shift, "B1", 0, 1), (15, invert_sums, "B0", 0, 0)]
                + [(h, second_block, -1, n) for n, h in enumerate((3, 4, 5, 6, 7, 10))]
                + [(h, first_block, 2, n) for n, h in enumerate((9, 10, 11, 13, 14))]
                + [(8 + n, route, 1, n) for n in range(3)] + [(13 + n, route, 1, 3 + n) for n in range(3)],
                "B1": [(0, normalise, "B0", 0, 0), (7, invert_sums, "B0", 0, 1), (8, normalise, "B0", 0, 1), (8, make_shift, "A", 3, 0),
                       (15, make_shift, "A", 3, 1), (15, invert_sums, "B1", 0, 0)]
                + [(h, first_block, 2, 5 + n) for n, h in enumerate((1, 2, 3, 5, 6, 7, 8, 11))]
                + [(h, norm_x, 4, n) for n, h in enumerate((9, 10, 11, 14))],
                "A": [(0, normalise, "B1", 0, 0), (7, invert_sums, "B1", 0, 1), (8, normalise, "B1", 0, 1), (8, make_shift, "B0", 1, 0),
                      (15, make_shift, "B0", 1, 1), (15, invert_sums, "A", 3, 0)],
            }

            def step(k):
                for slot in SLOTS:
                    run_slot(k, *slot)

            def run_slot(k, name, attend, of, _last):
                for h in heads_of(attend, of):
                    if of and real(k, of[1]):
                        maxima(k, *of, h)
                    for when, what, *args in WORK[name]:
                        if when == h and real(k, args[1] if isinstance(args[0], str) else args[0]):
                            what(k, *args)

            for b in range(3):
                dve.memset(qs[b][:, :, :].bitcast(U32), 0).then_inc(zeroed, 1)
                norm_x(0, b, 0)
                norm_x(0, b, 1)
                norm_x(0, b, 2)
                dve.memset(ks[b][:, :, :].bitcast(U32), 0).then_inc(zeroed, 1)
                norm_x(0, b, 3)
            for slot in START:
                if slot[0] == "turn to B":
                    dve.wait_ge(const_in, 16 * 7)
                run_slot(0, *slot)
            run_steps(dve, step)

            dve.wait_ge(fr_ps, 1)
            dve.scalar_tensor_tensor(out=fr[:, 0:8], in0=misc["X"][0:NB, 0:NE], scalar=1.0 / T, in1=frb[:, :], op0=ALU.mult,
                                     op1=ALU.add).then_inc(fr_v, 1)
            dve.wait_ge(fr_v, 1)
            dve.tensor_reduce(fr[:, 8:9], fr[:, 0:8], AX_X, ALU.max).then_inc(fr_v, 1)
            dve.wait_ge(fr_v, 2)
            dve.tensor_scalar(fr[:, 16:24], fr[:, 0:8], fr[:, 8:9], None, ALU.subtract).then_inc(fr_v, 1)
            dve.wait_ge(fr_e, 1)
            dve.tensor_reduce(fr[:, 9:10], fr[:, 24:32], AX_X, ALU.add).then_inc(fr_v, 1)
            dve.wait_ge(fr_v, 4)
            dve.reciprocal(fr[:, 10:11], fr[:, 9:10]).then_inc(fr_v, 1)
            dve.wait_ge(fr_v, 5)
            dve.tensor_scalar(fr[:, 32:40], fr[:, 24:32], fr[:, 10:11], None, ALU.mult).then_inc(fr_v, 1)
            dve.wait_ge(fr_v, 6)
            dve.max(top[:, :], fr[:, 32:40]).then_inc(fr_v, 1)
            dve.wait_ge(fr_v, 7)
            dve.max_index(topi[:, :], top[:, :], fr[:, 32:40]).then_inc(fr_v, 1)
            dve.tensor_reduce(fr[:, 11:12], top[:, 0:TOPK], AX_X, ALU.add).then_inc(fr_v, 1)
            dve.wait_ge(fr_v, 9)
            dve.reciprocal(fr[:, 12:13], fr[:, 11:12]).then_inc(fr_v, 1)
            dve.wait_ge(fr_v, 10)
            dve.tensor_scalar(fr[:, 40:42], top[:, 0:TOPK], fr[:, 12:13], None, ALU.mult).then_inc(fr_v, 1)
            dve.wait_ge(routed, 64)

            def scale_experts(b, par):
                for e in range(TOPK):
                    expert = dve.value_load(taken_i[0:1, bass.ds(b * 8 + e, 1)], min_val=0, max_val=NE - 1)
                    dve.tensor_scalar(w2s[par][:, e, :], w2[:, bass.ds(expert, 1), :].rearrange("p o n -> p (o n)"),
                                      taken_p[:, bass.ds(b * TOPK + e, 1)], None, ALU.mult).then_inc(w2_scaled, 1)

            def last_norm(b, par):
                dve.wait_ge(inv_std["f"], b + 1)
                wait(dve, finished, b - 1)
                alone(dve, passed["dve"])
                for q in range(QT):
                    dve.tensor_scalar(tile_of(normed[par])(q), tile_of(z[par])(q), st[f"f{par}"][1][:, q, 0:1],
                                      st[f"f{par}"][2][:, q:q + 1], ALU.subtract, ALU.mult).then_inc(fn, 1)

            def finish(b, par, scale):
                base = NF * b
                dve.wait_ge(eo_ps, b + 1)
                wait(dve, fn, 2 * (b - 1))
                alone(dve, passed["dve"])
                dve.tensor_tensor(z[par][:, :], o_ps[par][:, 0:T], ys[:, bass.ds(b * T, T)], ALU.add).then_inc(fz, 1)
                if not (known(b) and b == 0):
                    last_norm(b - 1, 1 - par)
                stats(fz, base, 1, tile_of(z[par]), f"f{par}")
                if scale:
                    scale_experts(b + 2, par)
                aggregate(fz, base, 3, f"f{par}")
                add_eps(fz, base, 5, f"f{par}", EPS_OUTER)

            dve.wait_ge(w_in, 32)
            for par in range(2):
                scale_experts(par, par)
            for par in range(2):
                finish(par, par, True)
            with dve.Fori(1, NB // 2 - 1) as g:
                for par in range(2):
                    finish(2 * g + par, par, True)
            for par in range(2):
                finish(NB - 2 + par, par, False)
            last_norm(NB - 1, 1)


def kernel(L0_attn_x, L0_attn_Wq, L0_attn_Wk, L0_attn_Wv, L0_ffn_ln1_g, L0_ffn_ln1_b, L0_ffn_ln2_g, L0_ffn_ln2_b,
           L0_ffn_mha_wq, L0_ffn_mha_bq, L0_ffn_mha_wk, L0_ffn_mha_bk, L0_ffn_mha_wv, L0_ffn_mha_bv, L0_ffn_mha_wo,
           L0_ffn_mha_bo, L0_ffn_mha_rw, L0_ffn_mha_rb, L0_ffn_ffn_rw, L0_ffn_ffn_rb, L0_ffn_fw1, L0_ffn_fw2):
    import numpy as np
    import concourse.bacc as bacc
    from concourse.bass_utils import run_bass_kernel_spmd

    def heads_last(w):
        return np.asarray(w).reshape(-1, H, KD).swapaxes(1, 2).reshape(-1, D)

    wq, wk, wv, wo = (np.asarray(w) for w in (L0_ffn_mha_wq, L0_ffn_mha_wk, L0_ffn_mha_wv, L0_ffn_mha_wo))
    w_proj = np.concatenate([heads_last(np.asarray(L0_attn_Wq).T), heads_last(np.asarray(L0_attn_Wk).T), np.asarray(L0_attn_Wv).T]
                            + [w for m in range(NM) for w in (heads_last(wq[m]), heads_last(wk[m]), wv[m].reshape(D, D))], axis=1)
    cols = np.concatenate([heads_last(L0_ffn_mha_bq).T, heads_last(L0_ffn_mha_bk).T, np.asarray(L0_ffn_mha_bv).reshape(NM, D).T]
                          + [np.asarray(v).reshape(D, 1) for v in (L0_ffn_ln1_g, L0_ffn_ln1_b, L0_ffn_ln2_g, L0_ffn_ln2_b)]
                          + [np.asarray(L0_ffn_mha_rw)], axis=1)
    rows = np.concatenate([np.asarray(L0_ffn_mha_bo).reshape(1, NM * D), np.asarray(L0_ffn_mha_rb).reshape(1, NM)], axis=1)
    arrays = {
        "x": np.asarray(L0_attn_x), "w_proj": w_proj, "w_out": wo.reshape(NM, D, D), "cols": cols, "rows": rows,
        "ffn_rw": np.asarray(L0_ffn_ffn_rw), "ffn_rb": np.asarray(L0_ffn_ffn_rb).reshape(1, NE),
        "fw1": np.asarray(L0_ffn_fw1), "fw2": np.asarray(L0_ffn_fw2),
    }
    arrays = {name: np.ascontiguousarray(a) for name, a in arrays.items()}
    nc = bacc.Bacc("TRN2", target_bir_lowering=False, num_devices=1)
    args = [nc.dram_tensor(name, a.shape, F32, kind="ExternalInput").ap() for name, a in arrays.items()]
    out = nc.dram_tensor("out", (NB, T, D), F32, kind="ExternalOutput").ap()
    sandwich_kernel(nc, *args, out)
    return run_bass_kernel_spmd(nc, [arrays], core_ids=[0]).results[0]["out"]
```

```python
from contextlib import ExitStack

import concourse.bass as bass
from concourse import mybir

ALU = mybir.AluOpType
ACT = mybir.ActivationFunctionType
F32 = mybir.dt.float32
BF16 = mybir.dt.bfloat16
U32 = mybir.dt.uint32
AX_X = mybir.AxisListType.X

NB, T, D = 16, 256, 128
H, KD = 16, 8
QT = T // 128
F, NE, TOPK, NM = 256, 8, 2, 2
FC = F // 128
EPS_OUTER, EPS_INNER = 1e-5, 1e-6
HALF = H // 2
VW, VSTEP, ODD = 32, 36, 16
HEAD_ORDER = [half + 2 * g + odd for half in (0, HALF) for odd in range(2) for g in range(4)]
SHIFT = 126
RUNS = ((0, 1), (1, 2), (3, 3))

KINDS = ("A", "B0", "B1")
TAIL_STEP = 13
LOOP_STEPS = (1, 11)

INSTANCES = [("A", 0), ("A", 1), ("A", 2)]
for _k in range(NB):
    INSTANCES += [("B0", _k), ("B1", _k)] + ([("A", _k + 3)] if _k + 3 < NB else [])
PLACE = {inst: n for n, inst in enumerate(INSTANCES)}

START = (("project A", None, None, None), ("maxima A0", None, ("A", 0), None), ("attend A0", ("A", 0), ("A", 1), None),
         ("attend A1", ("A", 1), ("A", 2), ("A", 0)), ("attend A2", ("A", 2), None, ("A", 1)), ("turn to B", None, None, None),
         ("maxima B0", None, ("B0", 0), None))
SLOTS = (("B0", ("B0", 0), ("B1", 0), ("A", 2)), ("B1", ("B1", 0), ("A", 3), ("B0", 0)), ("A", ("A", 3), ("B0", 1), ("B1", 0)))

TAIL = (("first B0", ("B0", 0), ("B1", 0), ("A", 2)), ("first B1", ("B1", 0), ("B0", 1), ("B0", 0)),
        ("second B0", ("B0", 1), ("B1", 1), ("B1", 0)), ("second B1", ("B1", 1), ("B0", 2), ("B0", 1)),
        ("last B0", ("B0", 2), ("B1", 2), ("B1", 1)), ("last B1", ("B1", 2), None, ("B0", 2)))
GROUPS = ((0, NB - 2), (NB - 2, 2))

TENSOR_WORK = {
    "project A": [(0, "norm_x", "A", 0, "X"), (0, "project", "A", 0, "Y"), (0, "values", "A", 0, "Y"),
                  (0, "norm_x", "A", 1, "X"), (0, "project", "A", 1, "Y"), (0, "values", "A", 1, "Y"),
                  (0, "norm_x", "A", 2, "X")],
    "maxima A0": [(7, "project", "A", 2, "Y"), (7, "values", "A", 2, "Y"), (10, "shift0", "A", 0, "Y")],
    "attend A0": [(1, "shift1", "A", 0, "Y"), (7, "norm_x", "A", 3, "X"), (10, "shift0", "A", 1, "Y"),
                  (14, "turn0", "A", 0, "X")],
    "attend A1": [(1, "shift1", "A", 1, "Y"), (6, "turn1", "A", 0, "X"), (12, "shift0", "A", 2, "Y"),
                  (15, "turn0", "A", 1, "X")],
    "attend A2": [(0, "shift1", "A", 2, "Y"), (2, "norm1", "A", 0, "Y"), (4, "project", "B0", 0, "Y"),
                  (6, "turn1", "A", 1, "X"), (8, "values", "B0", 0, "Y"), (12, "project", "B1", 0, "Y"),
                  (14, "turn0", "A", 2, "X")],
    "turn to B": [(0, "values", "B1", 0, "Y")],
    "maxima B0": [(1, "norm1", "A", 1, "Y"), (3, "project", "A", 3, "Y"), (5, "route", "A", 0, "Y"),
                  (10, "shift0", "B0", 0, "Y"), (12, "project", "B0", 1, "Y")],
    "first B1": [(2, "shift1", "B1", 0, "Y"), (4, "project", "B1", 1, "Y"), (6, "turn1", "B0", 0, "X"),
                 (8, "values", "B0", 1, "Y"), (9, "values", "B1", 1, "Y"), (9, "norm2", "B", -1, "X"),
                 (10, "shift0", "B0", 1, "Y"), (11, "context", "B0", 0, "X"), (14, "turn0", "B1", 0, "X"),
                 (15, "norm1", "A", 2, "Y"), (15, "project", "B0", 2, "Y")],
    "second B0": [(2, "route", "A", 2, "Y"), (3, "shift1", "B0", 1, "Y"), (4, "turn1", "B1", 0, "X"),
                  (9, "context", "B1", 0, "X"), (10, "shift0", "B1", 1, "Y"), (11, "mix", "B", 0, "X"),
                  (14, "turn0", "B0", 1, "X")],
    "second B1": [(2, "shift1", "B1", 1, "Y"), (4, "norm2", "B", 0, "X"), (4, "project", "B1", 2, "Y"),
                  (6, "turn1", "B0", 1, "X"), (8, "values", "B0", 2, "Y"), (9, "values", "B1", 2, "Y"),
                  (10, "shift0", "B0", 2, "Y"), (11, "context", "B0", 1, "X"), (14, "turn0", "B1", 1, "X")],
    "last B0": [(2, "shift1", "B0", 2, "Y"), (4, "experts", "B", 0, "Y"), (7, "turn1", "B1", 1, "X"),
                (8, "context", "B1", 1, "X"), (10, "shift0", "B1", 2, "Y"), (12, "mix", "B", 1, "X"),
                (14, "turn0", "B0", 2, "X")],
    "last B1": [(2, "shift1", "B1", 2, "Y"), (3, "norm2", "B", 1, "X"), (6, "turn1", "B0", 2, "X"),
                (11, "context", "B0", 2, "X"), (14, "turn0", "B1", 2, "X")],
    "B0": [(2, "shift1", "B0", 0, "Y"), (2, "mix", "B", -1, "X"), (4, "route", "A", 1, "Y"), (6, "turn1", "A", 2, "X"),
           (8, "values", "A", 3, "Y"), (11, "shift0", "B1", 0, "Y"), (14, "turn0", "B0", 0, "X")],
    "B1": [(2, "shift1", "B1", 0, "Y"), (4, "project", "B1", 1, "Y"), (6, "turn1", "B0", 0, "X"),
           (7, "values", "B0", 1, "Y"), (9, "norm2", "B", -1, "X"), (10, "shift0", "A", 3, "Y"),
           (11, "context", "B0", 0, "X"), (15, "turn0", "B1", 0, "X")],
    "A": [(2, "shift1", "A", 3, "Y"), (2, "norm_x", "A", 4, "X"), (6, "project", "A", 4, "Y"),
          (6, "turn1", "B1", 0, "X"), (7, "values", "B1", 1, "Y"), (10, "shift0", "B0", 1, "Y"),
          (11, "norm1", "A", 2, "Y"), (12, "context", "B1", 0, "X"), (14, "project", "B0", 2, "Y"),
          (14, "turn0", "A", 3, "X")],
}
TENSOR_WORK["first B0"] = TENSOR_WORK["B0"]


def known(k):
    return isinstance(k, int)


def real(k, off):
    return not known(k) or 0 <= k + off < NB


def place(kind, k, off):
    if known(k):
        return PLACE[(kind, k + off)]
    return 3 * k + 3 * off + {"A": -4, "B0": 3, "B1": 4}[kind]


def ring3(kind, k, off):
    return PLACE[(kind, k + off)] % 3 if known(k) else {"A": 2, "B0": 0, "B1": 1}[kind]


def turn3(kind, k, off):
    return PLACE[(kind, k + off)] // 3 if known(k) else k + off + {"A": -2, "B0": 1, "B1": 1}[kind]


def before(kind, k, off):
    if not known(k):
        return {"A": ("B1", off - 3), "B0": ("A", off + 2), "B1": ("B0", off)}[kind]
    n = PLACE[(kind, k + off)]
    return (INSTANCES[n - 1][0], INSTANCES[n - 1][1] - k) if n else None


def wait(eng, sem, value):
    if not (known(value) and value <= 0):
        eng.wait_ge(sem, value)


def alone(eng, passed):
    eng.sem_inc(passed, 1)


def heads_of(attend, maxima, last):
    return range(H if attend or maxima or last else 1)


def run_steps(eng, step):
    for k in range(LOOP_STEPS[0]):
        step(k)
    with eng.Fori(*LOOP_STEPS) as k:
        step(k)
    for k in range(LOOP_STEPS[1], TAIL_STEP):
        step(k)


def sandwich_kernel(nc, x, w_proj, w_out, cols, rows, ffn_rw, ffn_rb, fw1, fw2, out):
    ctx = ExitStack()
    with ctx:
        def sb(name, shape, dt=F32):
            return ctx.enter_context(nc.sbuf_tensor(name, shape, dt))

        def sem(name):
            return ctx.enter_context(nc.semaphore(name))

        xs = sb("xs", [128, NB * T])
        ys = sb("ys", [128, NB * T])
        n2t = sb("n2t", [128, NB * T])
        n2sum = sb("n2sum", [128, NB])
        mixp = sb("mixp", [128, NB * NM])
        wp = sb("wp", [128, 9, 128])
        wo = sb("wo", [128, NM, 128])
        col = sb("col", [128, 12])
        qbias = sb("qbias", [128, NM])
        row = sb("row", [1, NM * 128])
        rbb = sb("rbb", [128, NM])
        frw = sb("frw", [128, NE])
        frb = sb("frb", [NB, NE])
        ident = sb("ident", [128, 128])
        identb = sb("identb", [128, 128], BF16)
        ones3 = sb("ones3", [3, 128], BF16)
        row_parts = sb("row_parts", [1, 3, NM * 128], BF16)
        row_rest = sb("row_rest", [1, NM * 128])
        row3 = sb("row3", [3, NM * 128], BF16)
        onerow = sb("onerow", [2, H * T], BF16)
        BQ, BK, BV, G1, B1, G2, B2, RW = 0, 2, 4, 6, 7, 8, 9, 10

        qs = [sb(f"qs{i}", [128, H, T], BF16) for i in range(3)]
        ks = [sb(f"ks{i}", [128, H, T], BF16) for i in range(3)]
        vext = [sb(f"vext{i}", [128, QT * H * VSTEP]) for i in range(3)]
        probs = sb("probs", [128, H, QT * T])
        qk = sb("qk", [128, 2 * T])
        parts = [sb(f"parts{i}", [128, 6, T], BF16) for i in range(3)]
        rest = sb("rest", [128, 2 * T])
        rowmax = sb("rowmax", [128, 2, QT, HALF])
        shift = sb("shift", [128, 2, QT, 2 * HALF], BF16)
        shiftrow = sb("shiftrow", [2 * HALF, 2, T], BF16)
        heads_out = sb("heads_out", [128, 2, T])
        inv = sb("inv", [128, 2, QT, HALF])
        context = sb("context", [128, QT, 128])
        ct = [sb(f"ct{m}", [128, T]) for m in range(NM)]
        nta = sb("nta", [128, T])
        n1t = sb("n1t", [128, T])
        n1sum = sb("n1sum", [128, 1])
        n1sumb = sb("n1sumb", [128, 128])
        u0 = sb("u0", [128, T])
        u1 = sb("u1", [128, T])
        u2 = sb("u2", [128, T])
        t1 = sb("t1", [128, T])
        st = {s: (sb(f"st{s}", [128, QT, 6]), sb(f"mv{s}", [128, QT, 2]), sb(f"rs{s}", [128, QT])) for s in (*"xayz", "f0", "f1")}
        var_eps = {s: sb(f"var_eps{s}", [128, QT]) for s in (*"xaynz", "f0", "f1")}
        minus_half = sb("minus_half", [128, QT])
        r2 = sb("r2", [128, 2 * QT])
        r3 = sb("r3", [128, QT])
        lg = sb("lg", [128, 10])

        s_ps = [ctx.enter_context(nc.psum_tensor(f"s_ps{i}", [128, 512], F32)) for i in range(2)]
        e_ps = [ctx.enter_context(nc.psum_tensor(f"e_ps{i}", [128, 512], F32)) for i in range(2)]
        o_ps = [ctx.enter_context(nc.psum_tensor(f"o_ps{i}", [128, 512], F32)) for i in range(2)]
        misc = {b: ctx.enter_context(nc.psum_tensor(f"misc{b}", [128, 512], F32)) for b in "XY"}

        scratch = nc.dram_tensor("part_scratch", (3, 6, KD, H, T), BF16, kind="Internal").ap()

        def part(r, p):
            return parts[r][:, p:6 - p:5 - 2 * p, :]

        def both(buf):
            return buf[:, :].rearrange("p (j n) -> p j n", j=2)

        inv_std = {s: sem(f"inv_std_{s}") for s in "xaynzf"}
        const_in = sem("const_in")
        row_split = sem("row_split")
        row3_in = sem("row3_in")
        wp_a_in = sem("wp_a_in")
        x_in = [sem(f"x_in{i}") for i in range(3)]
        passed = {e: sem(f"passed_{e}") for e in ("dve", "pool", "sp")}
        zeroed = sem("zeroed")
        ones_in = sem("ones_in")
        pool_const = sem("pool_const")
        xn = sem("xn")
        xt_ps = sem("xt_ps")
        xt_done = sem("xt_done")
        qk_ps = sem("qk_ps")
        qk_out = sem("qk_out")
        onerow_set = sem("onerow_set")
        qbias_set = sem("qbias_set")
        split = sem("split")
        parts_out = [sem(f"parts_out{i}") for i in range(3)]
        stacked = [sem(f"stacked{i}") for i in range(3)]
        v_ps = sem("v_ps")
        v_out = sem("v_out")
        s_ready = sem("s_ready")
        s_max = sem("s_max")
        shift_made = sem("shift_made")
        shift_ps = sem("shift_ps")
        shift_out = sem("shift_out")
        shift_in = [sem(f"shift_in{i}") for i in range(2)]
        e_ready = sem("e_ready")
        e_done = sem("e_done")
        pv = sem("pv")
        o_saved = sem("o_saved")
        o_ps_t = sem("o_ps_t")
        ctx_done = sem("ctx_done")
        an = sem("an")
        n1_ps = sem("n1_ps")
        n1_out = sem("n1_out")
        n1sum_b = sem("n1sum_b")
        route_ps = sem("route_ps")
        route_v = sem("route_v")
        route_e = sem("route_e")
        ct_ps = sem("ct_ps")
        ct_out = sem("ct_out")
        mix_ps = sem("mix_ps")
        zn = sem("zn")
        n2_ps = sem("n2_ps")
        n2_out = sem("n2_out")

        NX, NA, NZ, NR = 7, 20, 9, 6

        fr = [sb(f"fr{g}", [n, 48]) for g, (_b, n) in enumerate(GROUPS)]
        top = [sb(f"top{g}", [n, 8]) for g, (_b, n) in enumerate(GROUPS)]
        topi = [sb(f"topi{g}", [n, 8], U32) for g, (_b, n) in enumerate(GROUPS)]
        taken_p = sb("taken_p", [128, NB * TOPK])
        taken_i = sb("taken_i", [1, NB * 8], U32)
        w1 = sb("w1", [128, NE, F])
        w2 = sb("w2", [128, NE, FC * D])
        hidden = [probs[:, i * TOPK:(i + 1) * TOPK, :] for i in range(2)]
        w1s = [probs[:, 2 * TOPK + i, :].rearrange("p (e f) -> p e f", e=TOPK) for i in range(2)]
        w2s = [probs[:, 3 * TOPK + i, :].rearrange("p (e n) -> p e n", e=TOPK) for i in range(2)]
        z = [probs[:, 4 * TOPK, i * T:(i + 1) * T] for i in range(2)]
        normed = [probs[:, 4 * TOPK + 1, i * T:(i + 1) * T] for i in range(2)]
        result = [sb(f"result{i}", [128, T]) for i in range(2)]
        p_scratch = nc.dram_tensor("p_scratch", (NB, TOPK), F32, kind="Internal").ap()
        i_scratch = nc.dram_tensor("i_scratch", (NB, 8), U32, kind="Internal").ap()
        fr_ps = sem("fr_ps")
        fr_v = sem("fr_v")
        fr_e = sem("fr_e")
        routed = [sem(f"routed{g}") for g in range(2)]
        w_in = sem("w_in")
        w1_picked = sem("w1_picked")
        w2_scaled = sem("w2_scaled")
        h_ps = sem("h_ps")
        h_act = sem("h_act")
        eo_ps = sem("eo_ps")
        fz = sem("fz")
        fn = sem("fn")
        finished = sem("finished")
        stored = [sem(f"stored{i}") for i in range(2)]
        NF = 6

        def split_step(eng, eng_passed, k, kind, off, step):
            i, r = place(kind, k, off), ring3(kind, k, off)
            if step == 0:
                wait(eng, qk_out, 3 * i + 3)
                wait(eng, split, 3 * i)
                eng.tensor_tensor(both(rest), both(qk), part(r, 0), ALU.subtract).then_inc(split, 1)
            elif step == 1:
                eng.wait_ge(split, 3 * i + 1)
                wait(eng, parts_out[r], 16 * turn3(kind, k, off))
                alone(eng, eng_passed)
                eng.tensor_copy(part(r, 1), both(rest)).then_inc(split, 1)
            else:
                eng.wait_ge(split, 3 * i + 2)
                eng.tensor_tensor(part(r, 2), both(rest), part(r, 1), ALU.subtract).then_inc(split, 1)

        block = ctx.enter_context(nc.Block())

        @block.sync
        def _(sp):
            def load_x(i, first, last):
                sp.dma_start(xs[:, :].rearrange("p (b q d) -> p b q d", b=NB, q=QT)[:, first:last],
                             x.rearrange("b (q p) d -> p b q d", p=128)[:, first:last]).then_inc(x_in[i], 16)

            load_x(0, 0, 1)
            sp.dma_start(wp[:, 0:3, :].rearrange("p c n -> p (c n)"), w_proj[:, 0:3 * D]).then_inc(wp_a_in, 16)
            load_x(1, 1, 3)
            for dst, src in ((col[:, :], cols), (wp[:, 3:9, :].rearrange("p c n -> p (c n)"), w_proj[:, 3 * D:9 * D]),
                             (wo[:, :, :], w_out.rearrange("m p n -> p m n")),
                             (row[:, :], rows[0:1, 0:NM * 128]), (frw[:, :], ffn_rw),
                             (rbb[:, :], rows[0:1, NM * 128:NM * 128 + NM].to_broadcast([128, NM])),
                             (frb[:, :], ffn_rb.to_broadcast([NB, NE]))):
                sp.dma_start(dst, src).then_inc(const_in, 16)
            load_x(2, 3, NB)

            def ones_rows(i):
                sp.dma_start(ks[i][SHIFT:SHIFT + 2, :, :], onerow[:, :].rearrange("p (h n) -> p h n", h=H)).then_inc(ones_in, 16)

            def shift_rows(k, kind, off, half):
                i = place(kind, k, off)
                wait(sp, shift_out, 2 * i + half + 1)
                for part in range(2):
                    sp.dma_start(qs[ring3(kind, k, off)][SHIFT + part:SHIFT + part + 1, half * HALF:(half + 1) * HALF, :],
                                 shiftrow[part * HALF:(part + 1) * HALF, half, :]).then_inc(shift_in[half], 16)

            def store_parts(k, kind, off):
                i, r = place(kind, k, off), ring3(kind, k, off)
                wait(sp, split, 3 * i + 3)
                alone(sp, passed["sp"])
                wait(sp, stacked[r], 96 * turn3(kind, k, off))
                sp.dma_start(scratch[r].rearrange("c d h n -> (d h) c n"), parts[r][:, :, :]).then_inc(parts_out[r], 16)

            def stack_heads(k, kind, off):
                i, r = place(kind, k, off), ring3(kind, k, off)
                wait(sp, parts_out[r], 16 * (turn3(kind, k, off) + 1))
                alone(sp, passed["sp"])
                wait(sp, e_ready, 16 * (i - 2))
                for c, n in RUNS:
                    for dst, first in ((qs, 0), (ks, 6 - n)):
                        sp.dma_start(dst[r][KD * c:KD * (c + n), :, :],
                                     scratch[r, first:first + n].rearrange("c d h n -> (c d) h n")).then_inc(stacked[r], 16)

            def step(k):
                for slot in SLOTS:
                    run_slot(k, slot)

            def run_slot(k, slot):
                name, attend, maxima, _last = slot
                bring = NEXT.get(name)
                if attend and real(k, attend[1]):
                    shift_rows(k, *attend, 1)
                if name in ("A", "B1"):
                    if maxima and real(k, maxima[1]):
                        shift_rows(k, *maxima, 0)
                    if real(k, bring[1]):
                        store_parts(k, *bring)
                        stack_heads(k, *bring)
                elif name in ("B0", "first B1", "second B1"):
                    if real(k, bring[1]):
                        store_parts(k, *bring)
                    shift_rows(k, *maxima, 0)
                    if real(k, bring[1]):
                        stack_heads(k, *bring)
                else:
                    if bring:
                        store_parts(k, *bring)
                        stack_heads(k, *bring)
                    if maxima:
                        shift_rows(k, *maxima, 0)

            NEXT = {"B0": ("B0", 1), "B1": ("B1", 1), "A": ("A", 4), "first B0": ("B0", 1), "first B1": ("B1", 1),
                    "second B0": ("B0", 2), "second B1": ("B1", 2)}

            for b in range(2):
                store_parts(0, "A", b)
                sp.wait_ge(zeroed, 2 * b + 2)
                stack_heads(0, "A", b)
            sp.wait_ge(onerow_set, 1)
            sp.wait_ge(zeroed, 6)
            for i in range(3):
                ones_rows(i)
            shift_rows(0, "A", 0, 0)
            store_parts(0, "A", 2)
            shift_rows(0, "A", 0, 1)
            stack_heads(0, "A", 2)
            shift_rows(0, "A", 1, 0)
            shift_rows(0, "A", 1, 1)
            shift_rows(0, "A", 2, 0)
            shift_rows(0, "A", 2, 1)
            for p in range(3):
                sp.wait_ge(row_split, 4)
                sp.dma_start(row3[p:p + 1, :], row_parts[:, p, :]).then_inc(row3_in, 16)
            sp.dma_start(w1[:, :, :], fw1.rearrange("e p f -> p e f")).then_inc(w_in, 16)
            sp.dma_start(w2[:, :, :].rearrange("p e (c n) -> p e c n", c=FC), fw2.rearrange("e (c p) n -> p e c n", p=128)).then_inc(w_in, 16)
            for kind in ("B0", "B1"):
                store_parts(0, kind, 0)
                stack_heads(0, kind, 0)
            shift_rows(0, "B0", 0, 0)
            store_parts(0, "A", 3)
            stack_heads(0, "A", 3)
            run_steps(sp, step)
            def put_choice(g):
                b, n = GROUPS[g]
                sp.wait_ge(fr_v, 11 * (g + 1))
                sp.dma_start(p_scratch[b:b + n, :], fr[g][:, 40:40 + TOPK]).then_inc(routed[g], 16)
                sp.dma_start(i_scratch[b:b + n, :], topi[g][:, :]).then_inc(routed[g], 16)

            def get_choice(g):
                b, n = GROUPS[g]
                sp.wait_ge(routed[g], 32)
                sp.dma_start(taken_p[:, b * TOPK:(b + n) * TOPK],
                             p_scratch[b:b + n, :].rearrange("(o b) e -> o (b e)", o=1).to_broadcast([128, n * TOPK])).then_inc(routed[g], 16)
                sp.dma_start(taken_i[:, b * 8:(b + n) * 8], i_scratch[b:b + n, :].rearrange("(o b) e -> o (b e)", o=1)).then_inc(routed[g], 16)

            for slot in TAIL:
                run_slot(TAIL_STEP, slot)
                if slot[0] == "last B0":
                    put_choice(0)
            get_choice(0)

            def store_result(b, par):
                sp.wait_ge(finished, b + 1)
                sp.dma_start(out[bass.ds(b, 1), :, :].rearrange("o (q p) d -> p (o q) d", p=128),
                             result[par][:, :].rearrange("p (q d) -> p q d", q=QT)).then_inc(stored[par], 16)

            for par in range(2):
                store_result(par, par)
            put_choice(1)
            get_choice(1)
            with sp.Fori(1, NB // 2) as g:
                for par in range(2):
                    store_result(2 * g + par, par)
            for par in range(2):
                sp.wait_ge(stored[par], 16 * (NB // 2))

        @block.gpsimd
        def _(pool):
            pool.memset(ident[:, :], 0.0).then_inc(pool_const, 1)
            pool.memset(identb[:, :], 0.0).then_inc(pool_const, 1)
            pool.memset(ones3[:, :], 1.0).then_inc(pool_const, 1)
            pool.wait_ge(pool_const, 3)
            for m in (ident, identb):
                pool.affine_select(out=m[:, :], in_=m[:, :], compare_op=ALU.not_equal, fill=1.0, base=0,
                                   pattern=[[-1, 128]], channel_multiplier=1).then_inc(pool_const, 1)
            pool.memset(minus_half[:, :], -0.5).then_inc(pool_const, 1)
            def split_parts(k, kind, off, step):
                split_step(pool, passed["pool"], k, kind, off, step)

            STD = {"x": (xn, NX, 4, EPS_OUTER), "a": (an, NA, 4, EPS_OUTER), "y": (an, NA, 12, EPS_OUTER), "z": (zn, NZ, 6, EPS_INNER)}

            def invert_std(k, s, off):
                b = k + off
                sem_, per, done, eps = STD[s]
                pool.wait_ge(sem_, per * b + done)
                wait(pool, inv_std[s], b)
                alone(pool, passed["pool"])
                pool.tensor_scalar(var_eps[s][:, :], st[s][1][:, :, 1], eps, None, ALU.add).then_inc(sem_, 1)
                pool.wait_ge(sem_, per * b + done + 1)
                pool.tensor_tensor(st[s][2][:, :], var_eps[s][:, :], minus_half[:, :], ALU.pow).then_inc(inv_std[s], 1)

            def invert_inner_std(k, off):
                base = NA * (k + off)
                mv, rs = st["y"][1], st["y"][2]
                pool.wait_ge(an, base + 15)
                pool.tensor_tensor(r2[:, 0:QT], mv[:, :, 1], rs[:, :], ALU.mult).then_inc(an, 1)
                pool.wait_ge(an, base + 16)
                pool.tensor_tensor(r2[:, QT:2 * QT], r2[:, 0:QT], rs[:, :], ALU.mult).then_inc(an, 1)
                pool.wait_ge(an, base + 17)
                alone(pool, passed["pool"])
                pool.tensor_scalar(var_eps["n"][:, :], r2[:, QT:2 * QT], EPS_INNER, None, ALU.add).then_inc(an, 1)
                pool.wait_ge(an, base + 18)
                pool.tensor_tensor(r3[:, :], var_eps["n"][:, :], minus_half[:, :], ALU.pow).then_inc(inv_std["n"], 1)

            def add_to_x(k, off):
                b = k + off
                pool.wait_ge(an, NA * b + 7)
                alone(pool, passed["pool"])
                x_b = xs[:, bass.ds(b * T, T)]
                pool.tensor_tensor(x_b, t1[:, :], x_b, ALU.add).then_inc(an, 1)

            def spread_sum(k, kind, off):
                b = k + off
                wait(pool, n1_out, b + 1)
                wait(pool, route_ps, b)
                alone(pool, passed["pool"])
                pool.tensor_copy(n1sumb[:, :], n1sum[:, 0:1].to_broadcast([128, 128])).then_inc(n1sum_b, 1)

            def step(k):
                for what, *args in WORK:
                    if real(k, args[1] if isinstance(args[0], str) else args[0]):
                        what(k, *args)

            WORK = [(split_parts, "B0", 1, 0), (split_parts, "B0", 1, 1), (split_parts, "B0", 1, 2), (invert_std, "a", 2), (add_to_x, 2), (invert_std, "z", -1),
                    (split_parts, "B1", 1, 0), (split_parts, "B1", 1, 1), (split_parts, "B1", 1, 2), (invert_std, "y", 2),
                    (invert_inner_std, 2), (invert_std, "x", 5), (split_parts, "A", 4, 0), (split_parts, "A", 4, 1), (split_parts, "A", 4, 2),
                    (spread_sum, "A", 2)]
            def start(*work):
                for what, *args in work:
                    what(0, *args)

            start((invert_std, "x", 0))
            for i in range(3):
                pool.memset(vext[i][:, :], 0.0).then_inc(pool_const, 1)
            pool.wait_ge(pool_const, 9)
            for i in range(3):
                pool.memset(vext[i][:, :].rearrange("p (c d) -> p c d", d=VSTEP)[:, :, KD:KD + 1], 1.0).then_inc(pool_const, 1)
            start((invert_std, "x", 1))
            pool.memset(onerow[:, :], 1.0).then_inc(onerow_set, 1)
            pool.wait_ge(const_in, 16 * 7)
            pool.tensor_scalar(qbias[:, :], col[:, BQ:BQ + NM], KD ** -0.5, None, ALU.mult).then_inc(qbias_set, 1)
            start((invert_std, "x", 2), *((split_parts, "A", b, n) for b in (1, 2) for n in range(3)), (invert_std, "x", 3),
                  (invert_std, "a", 0), (add_to_x, 0), (invert_std, "y", 0), (invert_inner_std, 0), (spread_sum, "A", 0),
                  (invert_std, "a", 1), (add_to_x, 1), (invert_std, "y", 1), (invert_inner_std, 1), (invert_std, "x", 4),
                  *((split_parts, "B1", 0, n) for n in range(3)), (spread_sum, "A", 1), *((split_parts, "A", 3, n) for n in range(3)))
            run_steps(pool, step)
            step(TAIL_STEP)
            for what, *args in (*((split_parts, "B0", 2, n) for n in range(3)), (invert_std, "z", 0),
                                *((split_parts, "B1", 2, n) for n in range(3)), (invert_std, "z", 1)):
                what(TAIL_STEP, *args)

            def last_std(b, par):
                pool.wait_ge(fz, NF * (b + 1))
                pool.tensor_tensor(st[f"f{par}"][2][:, :], var_eps[f"f{par}"][:, :], minus_half[:, :], ALU.pow).then_inc(inv_std["f"], 1)

            def add_result(b, par, half_count):
                pool.wait_ge(fn, 2 * b + 2)
                wait(pool, stored[par], 16 * (half_count - 1))
                alone(pool, passed["pool"])
                pool.tensor_tensor(result[par][:, :], normed[par][:, :], xs[:, bass.ds(b * T, T)], ALU.add).then_inc(finished, 1)

            last_std(0, 0)
            invert_std(TAIL_STEP, "z", 2)
            add_result(0, 0, 1)
            last_std(1, 1)
            with pool.Fori(1, NB // 2) as g:
                add_result(2 * g - 1, 1, g)
                last_std(2 * g, 0)
                add_result(2 * g, 0, g + 1)
                last_std(2 * g + 1, 1)
            add_result(NB - 1, 1, NB // 2)

        @block.tensor
        def _(pe):
            pe.wait_ge(pool_const, 5)
            pe.wait_ge(wp_a_in, 16)
            at = {"X": None, "Y": None}

            def read(stage, kind, k, off):
                b = k + off
                if kind == "B":
                    return {"mix": (zn, NZ * b + 2), "norm2": (n2_out, b + 1), "experts": (fr_v, 11 * off + 1)}[stage]
                i = place(kind, k, off)
                return {"shift0": (shift_out, 2 * i + 1), "shift1": (shift_out, 2 * i + 2), "project": (qk_out, 3 * i + 2),
                        "turn0": (ctx_done, 4 * i + 2), "turn1": (ctx_done, 4 * i + 4), "route": (route_v, NR * b + 1),
                        "values": (v_out, i + 1), "context": (ct_out, 2 * b + KINDS.index(kind)),
                        "norm_x": (xt_done, b + 1), "norm1": (n1_out, b + 1)}[stage]

            def take(bank, stage, kind, k, off):
                if at[bank]:
                    pe.wait_ge(*read(at[bank][0], at[bank][1], k, at[bank][2]))
                at[bank] = (stage, kind, off)
                return misc[bank]

            def turn_tiles(dst, src, done):
                for q in range(QT):
                    last = pe.transpose(dst[:, q * 128:(q + 1) * 128], src[:, q * 128:(q + 1) * 128], ident[:, :])
                last.then_inc(done, 1)

            def work(k, stage, kind, off, bank):
                b = k + off
                i = place(kind, k, off) if kind != "B" else None
                m = KINDS.index(kind) - 1 if kind != "B" else None
                if stage in ("shift0", "shift1"):
                    half = int(stage[-1])
                    pe.wait_ge(shift_made, 4 * i + 2 * half + 2)
                    ps = take(bank, stage, kind, k, off)[:, :].bitcast(BF16)
                    for q in range(QT):
                        last = pe.transpose(ps[0:2 * HALF, q * 128:(q + 1) * 128], shift[:, half, q, :], identb[:, :])
                    last.then_inc(shift_ps, 1)
                elif stage in ("turn0", "turn1"):
                    half = int(stage[-1])
                    pe.wait_ge(o_saved, 2 * i + half + 1)
                    turn_tiles(take(bank, stage, kind, k, off), heads_out[:, half, :], o_ps_t)
                elif stage == "project":
                    if kind == "A":
                        pe.wait_ge(xt_done, b + 1)
                    else:
                        pe.wait_ge(n1_out, b + 1)
                    ps = take(bank, stage, kind, k, off)
                    for j in range(2):
                        last = pe.matmul(ps[:, j * T:(j + 1) * T], wp[:, 3 * (m + 1) + j, :], (nta if kind == "A" else n1t)[:, :],
                                         start=True, stop=True)
                    last.then_inc(qk_ps, 1)
                elif stage == "values":
                    ps = take(bank, stage, kind, k, off)
                    for q in range(QT):
                        last = pe.matmul(ps[:, q * 128:(q + 1) * 128], (nta if kind == "A" else n1t)[:, q * 128:(q + 1) * 128],
                                         wp[:, 3 * (m + 1) + 2, :], start=True, stop=True)
                    last.then_inc(v_ps, 1)
                elif stage == "norm_x":
                    pe.wait_ge(xn, NX * b + 7)
                    turn_tiles(take(bank, stage, kind, k, off), u0, xt_ps)
                elif stage == "norm1":
                    pe.wait_ge(an, NA * b + 20)
                    turn_tiles(take(bank, stage, kind, k, off), u1, n1_ps)
                elif stage == "norm2":
                    pe.wait_ge(zn, NZ * b + 9)
                    turn_tiles(take(bank, stage, kind, k, off), u2, n2_ps)
                elif stage == "route":
                    pe.wait_ge(n1sum_b, b + 1)
                    ps = take(bank, stage, kind, k, off)
                    pe.matmul(ps[:, 0:NM], n1sumb[:, :], col[:, RW:RW + NM], start=True, stop=True).then_inc(route_ps, 1)
                elif stage == "experts":
                    first, n = GROUPS[off]
                    pe.wait_ge(n2_out, first + n)
                    ps = take(bank, stage, kind, k, off)
                    pe.matmul(ps[0:n, 0:NE], n2sum[:, first:first + n], frw[:, :], start=True, stop=True).then_inc(fr_ps, 1)
                elif stage == "context":
                    pe.wait_ge(ctx_done, 4 * i + 4)
                    ps = take(bank, stage, kind, k, off)
                    for q in range(QT):
                        last = pe.transpose(ps[:, q * 128:(q + 1) * 128], context[:, q, :], ident[:, :])
                    last.then_inc(ct_ps, 1)
                elif stage == "mix":
                    pe.wait_ge(ct_out, 2 * b + 2)
                    ps = take(bank, stage, kind, k, off)
                    for q in range(QT):
                        o = ps[:, :].rearrange("p (e q n) -> p q e n", e=NM, q=QT)[:, q]
                        pe.matmul(o, ones3[:, :], row3[:, :].rearrange("p (e n) -> p e n", e=NM), start=True, stop=False)
                        for e in range(NM):
                            last = pe.matmul(o[:, e], ct[e][:, q * 128:(q + 1) * 128], wo[:, e, :], start=False, stop=(e == NM - 1))
                    last.then_inc(mix_ps, 1)

            def scores(k, kind, off, h):
                i, r = place(kind, k, off), ring3(kind, k, off)
                if h == 0:
                    pe.wait_ge(stacked[r], 96 * (turn3(kind, k, off) + 1))
                wait(pe, s_max, 16 * i + h - 1)
                for q in range(QT):
                    last = pe.matmul(s_ps[h % 2][:, q * T:(q + 1) * T], qs[r][0:SHIFT, h, q * 128:(q + 1) * 128],
                                     ks[r][0:SHIFT, h, :], start=True, stop=True)
                last.then_inc(s_ready, 1)

            def shifted_scores(k, kind, off, h):
                i, r = place(kind, k, off), ring3(kind, k, off)
                if h % HALF == 0:
                    pe.wait_ge(shift_in[h // HALF], 32 * (i + 1))
                wait(pe, e_done, 16 * i + h - 1)
                for q in range(QT):
                    last = pe.matmul(e_ps[h % 2][:, q * T:(q + 1) * T], ks[r][:, h, q * 128:(q + 1) * 128],
                                     qs[r][:, h, :], start=True, stop=True)
                last.then_inc(e_ready, 1)

            def probs_v(k, kind, off, quad, q):
                i, r = place(kind, k, off), ring3(kind, k, off)
                if q == 0:
                    pe.wait_ge(e_done, 16 * i + 4 * quad + 4)
                    if quad == 0:
                        pe.wait_ge(v_out, i + 1)
                    if quad % 2 == 0:
                        wait(pe, o_saved, 2 * i + quad // 2 - 1)
                o = o_ps[quad // 2]
                odd = quad % 2
                for g in range(4):
                    h = 4 * quad + g
                    tile = (q * H + h) * VSTEP - ODD * odd
                    last = pe.matmul(o[VW * g:VW * (g + 1), 0:T], vext[r][:, tile:tile + VW], probs[:, h, q * T:(q + 1) * T],
                                     start=(odd == 0 and q == 0), stop=(odd == 1 and q == QT - 1))
                if q == QT - 1:
                    last.then_inc(pv, 1)

            def step(k):
                for slot in SLOTS:
                    run_slot(k, *slot)
                for bank in at:
                    if at[bank]:
                        at[bank] = at[bank][:2] + (at[bank][2] - 1,)

            def run_slot(k, name, attend, maxima, last):
                for h in heads_of(attend, maxima, last):
                    if attend and real(k, attend[1]):
                        shifted_scores(k, *attend, h)
                    if maxima and real(k, maxima[1]):
                        scores(k, *maxima, h)
                    if h in (1, 3) and last and real(k, last[1]):
                        probs_v(k, *last, 3, h // 2)
                    if h % 2 and h >= 5 and attend and real(k, attend[1]):
                        probs_v(k, *attend, (h - 5) // 4, (h - 5) // 2 % 2)
                    for when, stage, kind, off, bank in TENSOR_WORK[name]:
                        if when == h and real(k, off):
                            work(k, stage, kind, off, bank)

            for slot in START:
                if slot[0] == "turn to B":
                    pe.wait_ge(row3_in, 16 * 3)
                if slot[0] == "maxima A0":
                    pe.wait_ge(zeroed, 6)
                if slot[0] == "attend A0":
                    pe.wait_ge(ones_in, 16 * 3)
                    pe.wait_ge(const_in, 16 * 7)
                run_slot(0, *slot)
            run_steps(pe, step)
            for slot in TAIL:
                run_slot(TAIL_STEP, *slot)

            def up(b, par):
                wait(pe, h_act, 2 * b - 2)
                for e in range(TOPK):
                    pe.wait_ge(w1_picked, 2 * b + e + 1)
                    for c in range(FC):
                        last = pe.matmul((s_ps, e_ps)[par][e][:, c * T:(c + 1) * T],
                                         w1s[par][:, e, c * 128:(c + 1) * 128],
                                         n2t[:, bass.ds(b * T, T)], start=True, stop=True)
                    last.then_inc(h_ps, 1)

            def down(b, par):
                pe.wait_ge(h_act, 2 * b + 2)
                pe.wait_ge(w2_scaled, 2 * b + 2)
                wait(pe, fz, NF * (b - 2) + 1)
                for q in range(QT):
                    for e in range(TOPK):
                        for c in range(FC):
                            last = pe.matmul(o_ps[par][:, q * 128:(q + 1) * 128],
                                             hidden[par][:, e, c * T + q * 128:c * T + (q + 1) * 128], w2s[par][:, e, c * D:(c + 1) * D],
                                             start=(e == 0 and c == 0), stop=(e == TOPK - 1 and c == FC - 1))
                last.then_inc(eo_ps, 1)

            end = TAIL_STEP
            probs_v(end, "B1", 2, 3, 0)
            probs_v(end, "B1", 2, 3, 1)
            pe.wait_ge(s_max, 16 * len(INSTANCES))
            up(0, 0)
            work(end, "turn1", "B1", 2, "X")
            pe.wait_ge(e_done, 16 * len(INSTANCES))
            up(1, 1)
            work(end, "context", "B1", 2, "X")
            pe.wait_ge(o_saved, 2 * len(INSTANCES))
            down(0, 0)
            work(end, "mix", "B", 2, "X")
            up(2, 0)
            down(1, 1)
            up(3, 1)
            work(end, "norm2", "B", 2, "X")
            down(2, 0)
            up(4, 0)
            work(end, "experts", "B", 1, "Y")
            down(3, 1)
            with pe.Fori(2, NB // 2 - 1) as g:
                up(2 * g + 1, 1)
                down(2 * g, 0)
                up(2 * g + 2, 0)
                down(2 * g + 1, 1)
            up(NB - 1, 1)
            down(NB - 2, 0)
            down(NB - 1, 1)

        @block.scalar
        def _(act):

            def exps(k, kind, off, h):
                i = place(kind, k, off)
                if h % 4 == 0:
                    wait(act, pv, 4 * i + h // 4 - 3)
                act.wait_ge(e_ready, 16 * i + h + 1)
                act.activation(probs[:, h, :], e_ps[h % 2][:, :], ACT.Exp).then_inc(e_done, 1)

            def save_heads(k, kind, off, half):
                i = place(kind, k, off)
                act.wait_ge(pv, 4 * i + 2 * half + 2)
                wait(act, o_ps_t, 2 * i + half - 1)
                act.activation(heads_out[:, half, :], o_ps[half][:, 0:T], ACT.Copy).then_inc(o_saved, 1)

            def save_shift(k, kind, off, half):
                i = place(kind, k, off)
                act.wait_ge(shift_ps, 2 * i + half + 1)
                wait(act, shift_in[half], 32 * i)
                ps = misc["Y"][:, :].bitcast(BF16)
                act.activation(shiftrow[:, half, :], ps[0:2 * HALF, 0:T], ACT.Copy).then_inc(shift_out, 1)

            def save_qk(k, kind, off, step):
                i, r, m = place(kind, k, off), ring3(kind, k, off), KINDS.index(kind) - 1
                if step == 0:
                    act.wait_ge(qk_ps, i + 1)
                    wait(act, split, 3 * i - 2)
                    if kind == "A":
                        op = act.activation(qk[:, 0:T], misc["Y"][:, 0:T], ACT.Copy, scale=D ** -0.5)
                    else:
                        op = act.activation(qk[:, 0:T], misc["Y"][:, 0:T], ACT.Identity, bias=qbias[:, m:m + 1], scale=KD ** -0.5)
                elif step == 1:
                    if kind == "A":
                        op = act.activation(qk[:, T:2 * T], misc["Y"][:, T:2 * T], ACT.Copy)
                    else:
                        op = act.activation(qk[:, T:2 * T], misc["Y"][:, T:2 * T], ACT.Identity, bias=col[:, BK + m:BK + m + 1])
                else:
                    act.wait_ge(qk_out, 3 * i + 2)
                    wait(act, parts_out[r], 16 * turn3(kind, k, off))
                    op = act.activation(part(r, 0), both(qk), ACT.Copy)
                op.then_inc(qk_out, 1)

            def save_v(k, kind, off):
                i, r = place(kind, k, off), ring3(kind, k, off)
                act.wait_ge(v_ps, i + 1)
                if known(k):
                    act.wait_ge(pool_const, 12)
                wait(act, pv, 4 * (i - 2))
                act.activation(vext[r][:, :].rearrange("p (c d) -> p c d", d=VSTEP)[:, :, 0:KD], misc["Y"][:, 0:T].rearrange("p (c d) -> p c d", d=KD), ACT.Copy).then_inc(v_out, 1)

            def save_norm_x(k, off):
                b = k + off
                act.wait_ge(xt_ps, b + 1)
                if real(k, off - 1):
                    act.wait_ge(v_ps, place("A", k, off - 1) + 1)
                act.activation(nta[:, :], misc["X"][:, 0:T], ACT.Copy).then_inc(xt_done, 1)

            def scale_inner(k, off):
                b = k + off
                act.wait_ge(inv_std["n"], b + 1)
                wait(act, n1_ps, b)
                for q in range(QT):
                    act.activation(u1[:, q * 128:(q + 1) * 128], ys[:, bass.ds(b * T + q * 128, 128)], ACT.Copy,
                                   scale=r3[:, q:q + 1]).then_inc(an, 1)

            def save_norm1(k, off):
                b = k + off
                act.wait_ge(n1_ps, b + 1)
                if real(k, off - 1):
                    act.wait_ge(v_ps, place("B1", k, off - 1) + 1)
                    act.wait_ge(n1sum_b, b)
                act.activation(n1t[:, :], misc["Y"][:, 0:T], ACT.Identity, bias=col[:, B1:B1 + 1], scale=col[:, G1:G1 + 1],
                               accum_out=n1sum[:, 0:1]).then_inc(n1_out, 1)

            def save_norm2(k, off):
                b = k + off
                act.wait_ge(n2_ps, b + 1)
                act.activation(n2t[:, bass.ds(b * T, T)], misc["X"][:, 0:T], ACT.Identity, bias=col[:, B2:B2 + 1],
                               scale=col[:, G2:G2 + 1], accum_out=n2sum[:, bass.ds(b, 1)]).then_inc(n2_out, 1)

            def save_context(k, kind, off):
                b, m = k + off, KINDS.index(kind) - 1
                act.wait_ge(ct_ps, 2 * b + m + 1)
                wait(act, mix_ps, b)
                act.activation(ct[m][:, :], misc["X"][:, 0:T], ACT.Identity, bias=col[:, BV + m:BV + m + 1]).then_inc(ct_out, 1)

            def route_exp(k, off):
                b = k + off
                act.wait_ge(route_v, NR * b + 3)
                act.activation(lg[:, 6:8], lg[:, 4:6], ACT.Exp).then_inc(route_e, 1)

            def expert_exp(k, g):
                act.wait_ge(fr_v, 11 * g + 3)
                act.activation(fr[g][:, 24:32], fr[g][:, 16:24], ACT.Exp).then_inc(fr_e, 1)

            WORK = {
                "project A": [(0, save_norm_x, 0), (0, save_qk, "A", 0, 0), (0, save_qk, "A", 0, 1),
                              (0, save_qk, "A", 0, 2), (0, save_v, "A", 0), (0, save_norm_x, 1),
                              (0, save_qk, "A", 1, 0), (0, save_qk, "A", 1, 1), (0, save_qk, "A", 1, 2),
                              (0, save_v, "A", 1), (0, save_norm_x, 2)],
                "maxima A0": [(8, save_qk, "A", 2, 0), (8, save_qk, "A", 2, 1), (8, save_qk, "A", 2, 2),
                              (8, save_v, "A", 2), (12, save_shift, "A", 0, 0)],
                "attend A0": [(2, save_shift, "A", 0, 1), (8, save_norm_x, 3), (9, save_heads, "A", 0, 0),
                              (11, save_shift, "A", 1, 0)],
                "attend A1": [(2, save_shift, "A", 1, 1), (4, save_heads, "A", 0, 1), (12, save_heads, "A", 1, 0),
                              (13, save_shift, "A", 2, 0)],
                "attend A2": [(1, save_shift, "A", 2, 1), (1, scale_inner, 0), (3, save_norm1, 0),
                              (4, save_heads, "A", 1, 1), (5, save_qk, "B0", 0, 0), (5, save_qk, "B0", 0, 1),
                              (5, save_qk, "B0", 0, 2), (9, save_v, "B0", 0), (12, save_heads, "A", 2, 0),
                              (13, save_qk, "B1", 0, 0), (13, save_qk, "B1", 0, 1), (13, save_qk, "B1", 0, 2)],
                "turn to B": [(0, save_v, "B1", 0), (0, scale_inner, 1)],
                "maxima B0": [(2, save_norm1, 1), (4, save_qk, "A", 3, 0), (4, save_qk, "A", 3, 1),
                              (7, save_qk, "A", 3, 2), (9, route_exp, 0), (11, save_shift, "B0", 0, 0),
                              (12, save_qk, "B0", 1, 0), (13, save_qk, "B0", 1, 1), (13, save_qk, "B0", 1, 2)],
                "first B1": [(3, save_shift, "B1", 0, 1), (4, save_heads, "B0", 0, 1), (5, save_qk, "B1", 1, 0),
                             (5, save_qk, "B1", 1, 1), (5, save_qk, "B1", 1, 2), (9, save_v, "B0", 1),
                             (10, save_v, "B1", 1), (10, save_norm2, -1), (11, save_shift, "B0", 1, 0),
                             (12, save_context, "B0", 0), (12, save_heads, "B1", 0, 0), (13, scale_inner, 2),
                             (15, save_norm1, 2)],
                "second B0": [(0, save_qk, "B0", 2, 0), (0, save_qk, "B0", 2, 1), (0, save_qk, "B0", 2, 2),
                              (3, save_shift, "B0", 1, 1), (4, save_heads, "B1", 0, 1), (10, save_context, "B1", 0),
                              (10, route_exp, 2), (11, save_shift, "B1", 1, 0), (12, save_heads, "B0", 1, 0)],
                "second B1": [(3, save_shift, "B1", 1, 1), (4, save_heads, "B0", 1, 1), (5, save_norm2, 0),
                              (5, save_qk, "B1", 2, 0), (5, save_qk, "B1", 2, 1), (5, save_qk, "B1", 2, 2),
                              (9, save_v, "B0", 2), (10, save_v, "B1", 2), (11, save_shift, "B0", 2, 0),
                              (12, save_context, "B0", 1), (13, save_heads, "B1", 1, 0)],
                "last B0": [(3, save_shift, "B0", 2, 1), (4, save_heads, "B1", 1, 1), (5, expert_exp, 0),
                            (10, save_context, "B1", 1), (11, save_shift, "B1", 2, 0), (12, save_heads, "B0", 2, 0)],
                "last B1": [(1, save_heads, "B0", 2, 1), (3, save_shift, "B1", 2, 1), (5, save_norm2, 1),
                            (12, save_context, "B0", 2), (12, save_heads, "B1", 2, 0)],
                "B0": [(2, save_shift, "B0", 0, 1), (5, save_heads, "A", 2, 1), (10, save_v, "A", 3),
                       (11, save_shift, "B1", 0, 0), (11, save_heads, "B0", 0, 0), (12, route_exp, 1)],
                "B1": [(2, save_shift, "B1", 0, 1), (2, save_heads, "B0", 0, 1), (5, save_qk, "B1", 1, 0),
                       (5, save_qk, "B1", 1, 1), (6, save_qk, "B1", 1, 2), (7, save_v, "B0", 1), (10, save_norm2, -1),
                       (11, save_shift, "A", 3, 0), (12, save_context, "B0", 0), (12, save_heads, "B1", 0, 0)],
                "A": [(3, save_shift, "A", 3, 1), (3, save_norm_x, 4), (4, save_heads, "B1", 0, 1), (6, scale_inner, 2),
                      (6, save_qk, "A", 4, 0), (6, save_qk, "A", 4, 1), (7, save_qk, "A", 4, 2), (9, save_v, "B1", 1),
                      (10, save_shift, "B0", 1, 0), (12, save_norm1, 2), (12, save_heads, "A", 3, 0),
                      (13, save_context, "B1", 0), (14, save_qk, "B0", 2, 0), (14, save_qk, "B0", 2, 1),
                      (15, save_qk, "B0", 2, 2)],
            }
            WORK["first B0"] = WORK["B0"]

            def step(k):
                for slot in SLOTS:
                    run_slot(k, *slot)

            def run_slot(k, name, attend, maxima, last):
                for h in heads_of(attend, maxima, last):
                    if attend and real(k, attend[1]):
                        exps(k, *attend, h)
                    for when, what, *args in WORK[name]:
                        if when == h and real(k, args[1] if isinstance(args[0], str) else args[0]):
                            what(k, *args)

            act.wait_ge(pool_const, 6)
            act.activation(lg[:, 0:1], minus_half[:, 0:1], ACT.Exp)
            for slot in START:
                if slot[0] == "attend A2":
                    act.wait_ge(const_in, 16 * 7)
                    act.wait_ge(qbias_set, 1)
                run_slot(0, *slot)
            run_steps(act, step)
            for slot in TAIL:
                run_slot(TAIL_STEP, *slot)

            def gelus(b, par):
                wait(act, eo_ps, b - 1)
                for e in range(TOPK):
                    act.wait_ge(h_ps, 2 * b + e + 1)
                    act.activation(hidden[par][:, e, :], (s_ps, e_ps)[par][e][:, :], ACT.Gelu).then_inc(h_act, 1)

            def pick_experts(b, par):
                for e in range(TOPK):
                    expert = act.value_load(taken_i[0:1, bass.ds(b * 8 + e, 1)], min_val=0, max_val=NE - 1)
                    act.activation(w1s[par][:, e, :], w1[:, bass.ds(expert, 1), :].rearrange("p o f -> p (o f)"), ACT.Copy).then_inc(w1_picked, 1)

            act.wait_ge(w_in, 32)
            act.wait_ge(routed[0], 64)
            act.wait_ge(pv, 4 * len(INSTANCES) - 2)
            pick_experts(0, 0)
            pick_experts(1, 1)
            end = TAIL_STEP
            save_heads(end, "B1", 2, 1)
            gelus(0, 0)
            pick_experts(2, 0)
            gelus(1, 1)
            save_context(end, "B1", 2)
            pick_experts(3, 1)
            gelus(2, 0)
            pick_experts(4, 0)
            gelus(3, 1)
            pick_experts(5, 1)
            save_norm2(end, 2)
            gelus(4, 0)
            pick_experts(6, 0)
            expert_exp(end, 1)
            gelus(5, 1)
            pick_experts(7, 1)
            with act.Fori(3, NB // 2 - 2) as g:
                for par in range(2):
                    gelus(2 * g + par, par)
                    pick_experts(2 * g + par + 2, par)
            act.wait_ge(routed[1], 64)
            for par in range(2):
                gelus(NB - 4 + par, par)
                pick_experts(NB - 2 + par, par)
            for par in range(2):
                gelus(NB - 2 + par, par)

        @block.vector
        def _(dve):
            def maxima(k, kind, off, h):
                i = place(kind, k, off)
                if h % HALF == 0:
                    wait(dve, shift_made, 4 * i + 2 * (h // HALF) - 2)
                dve.wait_ge(s_ready, 16 * i + h + 1)
                dve.tensor_reduce(rowmax[:, h // HALF, :, h % HALF:h % HALF + 1], s_ps[h % 2][:, :].rearrange("p (q n) -> p q n", q=QT),
                                  AX_X, ALU.max).then_inc(s_max, 1)

            def split_parts(k, kind, off, step):
                split_step(dve, passed["dve"], k, kind, off, step)

            def make_shift(k, kind, off, half, part):
                i = place(kind, k, off)
                hi, lo = shift[:, half, :, 0:HALF], shift[:, half, :, HALF:2 * HALF]
                if part == 0:
                    dve.wait_ge(s_max, 16 * i + HALF * (half + 1))
                    wait(dve, shift_ps, 2 * i + half - 1)
                    dve.tensor_scalar(hi, rowmax[:, half, :, :], -1.0, None, ALU.mult).then_inc(shift_made, 1)
                else:
                    dve.wait_ge(shift_made, 4 * i + 2 * half + 1)
                    dve.scalar_tensor_tensor(out=lo, in0=rowmax[:, half, :, :], scalar=-1.0, in1=hi, op0=ALU.mult,
                                             op1=ALU.subtract).then_inc(shift_made, 1)

            def invert_sums(k, kind, off, half):
                i = place(kind, k, off)
                dve.wait_ge(o_ps_t, 2 * i + half + 1)
                wait(dve, ctx_done, 4 * i + 2 * half - 2)
                sums = misc["X"][:, 0:T].rearrange("p (q s c) -> p q s c", q=QT, c=ODD)[:, :, :, KD]
                dve.reciprocal(inv[:, half, :, :], sums).then_inc(ctx_done, 1)

            def normalise(k, kind, off, half):
                i = place(kind, k, off)
                dve.wait_ge(ctx_done, 4 * i + 2 * half + 1)
                if (last := before(kind, k, off)) and half == 0:
                    b = k + last[1]
                    if last[0] == "A":
                        dve.wait_ge(an, NA * b + 7)
                    else:
                        dve.wait_ge(ct_ps, 2 * b + KINDS.index(last[0]))
                heads = misc["X"][:, 0:T].rearrange("p (q s c) -> p q s c", q=QT, c=ODD)[:, :, :, 0:KD]
                dst = context[:, :, half * 64:(half + 1) * 64].rearrange("p q (s d) -> p q s d", d=KD)
                dve.tensor_tensor(dst, heads, inv[:, half, :, :].unsqueeze(3).to_broadcast([128, QT, HALF, KD]),
                                  ALU.mult).then_inc(ctx_done, 1)

            def stats(sem_, base, done, src, s):
                wait(dve, sem_, base + done)
                alone(dve, passed["dve"])
                for q in range(QT):
                    dve.bn_stats(st[s][0][:, q, :], src(q)).then_inc(sem_, 1)

            def aggregate(sem_, base, done, s):
                dve.wait_ge(sem_, base + done)
                alone(dve, passed["dve"])
                for q in range(QT):
                    dve.bn_aggr(st[s][1][:, q, :], st[s][0][:, q, :]).then_inc(sem_, 1)

            def add_eps(sem_, base, done, s, eps):
                dve.wait_ge(sem_, base + done)
                dve.tensor_scalar(var_eps[s][:, :], st[s][1][:, :, 1], eps, None, ALU.add).then_inc(sem_, 1)

            def scale_to(sem_, b, s, dst, src):
                dve.wait_ge(inv_std[s], b + 1)
                for q in range(QT):
                    dve.tensor_scalar(dst(q), src(q), st[s][1][:, q, 0:1], st[s][2][:, q:q + 1], ALU.subtract, ALU.mult).then_inc(sem_, 1)

            def tile_of(buf):
                return lambda q: buf[:, q * 128:(q + 1) * 128]

            def tile_at(buf, b):
                return lambda q: buf[:, bass.ds(b * T + q * 128, 128)]

            def norm_x(k, off, part):
                b = k + off
                if part == 0:
                    if known(k):
                        dve.wait_ge(x_in[(b > 0) + (b > 2)], 16)
                    stats(xn, NX * b, 0, tile_at(xs, b), "x")
                elif part == 1:
                    aggregate(xn, NX * b, 2, "x")
                else:
                    wait(dve, xt_ps, b)
                    scale_to(xn, b, "x", tile_of(u0), tile_at(xs, b))

            def first_block(k, off, part):
                b = k + off
                base = NA * b
                if part == 0:
                    dve.wait_ge(ctx_done, 4 * place("A", k, off) + 4)
                    stats(an, base, 0, lambda q: context[:, q, :], "a")
                elif part == 1:
                    aggregate(an, base, 2, "a")
                elif part == 2:
                    scale_to(an, b, "a", tile_of(t1), lambda q: context[:, q, :])
                elif part == 3:
                    stats(an, base, 8, tile_at(xs, b), "y")
                elif part == 4:
                    wait(dve, inv_std["n"], b)
                    aggregate(an, base, 10, "y")
                else:
                    scale_to(an, b, "y", tile_at(ys, b), tile_at(xs, b))

            def second_block(k, off, part):
                b = k + off
                base = NZ * b
                if part < 2:
                    if part == 0:
                        dve.wait_ge(mix_ps, b + 1)
                        dve.wait_ge(an, NA * b + 20)
                        dve.wait_ge(route_v, NR * b + 6)
                    else:
                        dve.wait_ge(zn, base + 1)
                    y_b = ys[:, bass.ds(b * T, T)]
                    dve.scalar_tensor_tensor(out=y_b, in0=misc["X"][:, part * T:(part + 1) * T], scalar=mixp[:, bass.ds(b * NM + part, 1)],
                                             in1=y_b, op0=ALU.mult, op1=ALU.add).then_inc(zn, 1)
                elif part == 2:
                    stats(zn, base, 2, tile_at(ys, b), "z")
                elif part == 3:
                    aggregate(zn, base, 4, "z")
                else:
                    wait(dve, n2_ps, b)
                    scale_to(zn, b, "z", tile_of(u2), tile_at(ys, b))

            def route(k, off, part):
                b = k + off
                dve.wait_ge(*((route_ps, b + 1) if part == 0 else (route_v, NR * b + part)))
                if part == 0:
                    wait(dve, route_v, NR * b)
                    op = dve.scalar_tensor_tensor(out=lg[:, 0:2], in0=misc["Y"][:, 0:NM], scalar=1.0 / T, in1=rbb[:, :], op0=ALU.mult, op1=ALU.add)
                elif part == 1:
                    op = dve.tensor_reduce(lg[:, 2:3], lg[:, 0:2], AX_X, ALU.max)
                elif part == 2:
                    wait(dve, route_e, b)
                    op = dve.tensor_scalar(lg[:, 4:6], lg[:, 0:2], lg[:, 2:3], None, ALU.subtract)
                elif part == 3:
                    dve.wait_ge(route_e, b + 1)
                    op = dve.tensor_reduce(lg[:, 8:9], lg[:, 6:8], AX_X, ALU.add)
                elif part == 4:
                    op = dve.reciprocal(lg[:, 9:10], lg[:, 8:9])
                else:
                    op = dve.tensor_scalar(mixp[:, bass.ds(b * NM, NM)], lg[:, 6:8], lg[:, 9:10], None, ALU.mult)
                op.then_inc(route_v, 1)

            def choose(k, g, part):
                n = GROUPS[g][1]
                f = fr[g]
                dve.wait_ge(*((fr_ps, g + 1) if part == 0 else (fr_v, 11 * g + (7 if part == 8 else part))))
                if part == 0:
                    op = dve.scalar_tensor_tensor(out=f[:, 0:8], in0=misc["Y"][0:n, 0:NE], scalar=1.0 / T, in1=frb[0:n, :],
                                                  op0=ALU.mult, op1=ALU.add)
                elif part == 1:
                    op = dve.tensor_reduce(f[:, 8:9], f[:, 0:8], AX_X, ALU.max)
                elif part == 2:
                    op = dve.tensor_scalar(f[:, 16:24], f[:, 0:8], f[:, 8:9], None, ALU.subtract)
                elif part == 3:
                    dve.wait_ge(fr_e, g + 1)
                    op = dve.tensor_reduce(f[:, 9:10], f[:, 24:32], AX_X, ALU.add)
                elif part == 4:
                    op = dve.reciprocal(f[:, 10:11], f[:, 9:10])
                elif part == 5:
                    op = dve.tensor_scalar(f[:, 32:40], f[:, 24:32], f[:, 10:11], None, ALU.mult)
                elif part == 6:
                    op = dve.max(top[g][:, :], f[:, 32:40])
                elif part == 7:
                    op = dve.max_index(topi[g][:, :], top[g][:, :], f[:, 32:40])
                elif part == 8:
                    op = dve.tensor_reduce(f[:, 11:12], top[g][:, 0:TOPK], AX_X, ALU.add)
                elif part == 9:
                    op = dve.reciprocal(f[:, 12:13], f[:, 11:12])
                else:
                    op = dve.tensor_scalar(f[:, 40:42], top[g][:, 0:TOPK], f[:, 12:13], None, ALU.mult)
                op.then_inc(fr_v, 1)

            WORK = {
                "project A": [],
                "maxima A0": [(7, make_shift, "A", 0, 0, 0), (8, make_shift, "A", 0, 0, 1), (15, make_shift, "A", 0, 1, 0), (15, make_shift, "A", 0, 1, 1)],
                "attend A0": [(h, norm_x, 3, n) for n, h in enumerate((1, 2, 5))]
                + [(8, make_shift, "A", 1, 0, 0), (9, make_shift, "A", 1, 0, 1), (15, make_shift, "A", 1, 1, 0), (15, make_shift, "A", 1, 1, 1), (15, invert_sums, "A", 0, 0)],
                "attend A1": [(0, normalise, "A", 0, 0), (7, invert_sums, "A", 0, 1), (8, normalise, "A", 0, 1), (8, make_shift, "A", 2, 0, 0), (8, make_shift, "A", 2, 0, 1)]
                + [(h, first_block, 0, n) for n, h in enumerate((8, 8, 9, 11, 11, 12))]
                + [(15, make_shift, "A", 2, 1, 0), (15, make_shift, "A", 2, 1, 1), (15, invert_sums, "A", 1, 0)],
                "attend A2": [(0, normalise, "A", 1, 0)] + [(2, split_parts, "B0", 0, n) for n in range(3)]
                + [(7, invert_sums, "A", 1, 1), (8, normalise, "A", 1, 1)] + [(8, first_block, 1, n) for n in range(6)]
                + [(15, invert_sums, "A", 2, 0)],
                "turn to B": [(0, norm_x, 4, n) for n in range(2)] + [(0, norm_x, 4, 2)],
                "maxima B0": [(h, route, 0, n) for n, h in enumerate((6, 7, 7, 11, 11, 12))]
                + [(8, make_shift, "B0", 0, 0, 0), (8, make_shift, "B0", 0, 0, 1), (15, make_shift, "B0", 0, 1, 0)],
                "first B1": [(0, make_shift, "B1", 0, 1, 1), (0, normalise, "B0", 0, 0), (7, invert_sums, "B0", 0, 1), (8, make_shift, "B0", 1, 0, 0),
                       (8, normalise, "B0", 0, 1), (8, make_shift, "B0", 1, 0, 1), (15, invert_sums, "B1", 0, 0), (15, make_shift, "B0", 1, 1, 0)]
                + [(h, second_block, -1, 2 + n) for n, h in enumerate((1, 1, 4))]
                + [(h, first_block, 2, 3 + n) for n, h in enumerate((5, 6, 10))],
                "second B0": [(0, make_shift, "B0", 1, 1, 1), (0, normalise, "B1", 0, 0), (7, invert_sums, "B1", 0, 1), (8, make_shift, "B1", 1, 0, 0),
                       (8, normalise, "B1", 0, 1), (8, make_shift, "B1", 1, 0, 1), (15, invert_sums, "B0", 1, 0), (15, make_shift, "B1", 1, 1, 0)]
                + [(h, second_block, 0, n) for n, h in enumerate((12, 13, 13, 15))]
                + [(3 + n, route, 2, n) for n in range(3)] + [(10 + n, route, 2, 3 + n) for n in range(3)],
                "second B1": [(0, make_shift, "B1", 1, 1, 1), (0, normalise, "B0", 1, 0), (7, invert_sums, "B0", 1, 1), (8, make_shift, "B0", 2, 0, 0),
                       (8, normalise, "B0", 1, 1), (8, make_shift, "B0", 2, 0, 1), (15, invert_sums, "B1", 1, 0), (15, make_shift, "B0", 2, 1, 0)]
                + [(1, second_block, 0, 4)],
                "last B0": [(h, choose, 0, n) for n, h in enumerate((3, 4, 6, 7, 7, 8, 8, 9, 9, 10, 10))] + [(0, make_shift, "B0", 2, 1, 1), (0, normalise, "B1", 1, 0), (7, invert_sums, "B1", 1, 1), (8, make_shift, "B1", 2, 0, 0),
                       (7, normalise, "B1", 1, 1), (8, make_shift, "B1", 2, 0, 1), (15, invert_sums, "B0", 2, 0), (15, make_shift, "B1", 2, 1, 0)]
                + [(h, second_block, 1, n) for n, h in enumerate((12, 13, 13, 14))],
                "last B1": [(1, make_shift, "B1", 2, 1, 1), (0, normalise, "B0", 2, 0), (0, second_block, 1, 4), (7, invert_sums, "B0", 2, 1),
                            (8, normalise, "B0", 2, 1), (15, invert_sums, "B1", 2, 0)],
                "B0": [(0, make_shift, "B0", 0, 1, 1), (0, normalise, "A", 2, 0), (7, invert_sums, "A", 2, 1), (7, make_shift, "B1", 0, 0, 0),
                       (8, normalise, "A", 2, 1), (8, make_shift, "B1", 0, 0, 1), (15, invert_sums, "B0", 0, 0), (15, make_shift, "B1", 0, 1, 0)]
                + [(6 + n, route, 1, n) for n in range(3)] + [(13 + n, route, 1, 3 + n) for n in range(3)]
                + [(h, second_block, -1, n) for n, h in enumerate((3, 4))]
                + [(h, first_block, 2, n) for n, h in enumerate((9, 11, 13))],
                "B1": [(0, make_shift, "B1", 0, 1, 1), (2, normalise, "B0", 0, 0), (6, invert_sums, "B0", 0, 1), (7, make_shift, "A", 3, 0, 0),
                       (7, normalise, "B0", 0, 1), (7, make_shift, "A", 3, 0, 1), (15, invert_sums, "B1", 0, 0), (15, make_shift, "A", 3, 1, 0)]
                + [(h, second_block, -1, 2 + n) for n, h in enumerate((1, 3, 6))]
                + [(h, first_block, 2, 3 + n) for n, h in enumerate((9, 10, 14))],
                "A": [(0, make_shift, "A", 3, 1, 1), (0, normalise, "B1", 0, 0), (7, invert_sums, "B1", 0, 1), (8, make_shift, "B0", 1, 0, 0),
                      (7, normalise, "B1", 0, 1), (8, make_shift, "B0", 1, 0, 1), (15, invert_sums, "A", 3, 0), (15, make_shift, "B0", 1, 1, 0)]
                + [(h, norm_x, 5, n) for n, h in enumerate((2, 4, 10))],
            }
            WORK["first B0"] = WORK["B0"]

            def step(k):
                for slot in SLOTS:
                    run_slot(k, *slot)

            def run_slot(k, name, attend, of, last):
                for h in heads_of(attend, of, last):
                    if of and real(k, of[1]):
                        maxima(k, *of, h)
                    for when, what, *args in WORK[name]:
                        if when == h and real(k, args[1] if isinstance(args[0], str) else args[0]):
                            what(k, *args)

            def clear(stack):
                dve.memset(stack[:, :, :].bitcast(U32), 0).then_inc(zeroed, 1)

            for b in range(3):
                if b == 0:
                    clear(qs[b])
                norm_x(0, b, 0)
                norm_x(0, b, 1)
                if b > 0:
                    clear(qs[b])
                norm_x(0, b, 2)
                if b == 1:
                    for n in range(3):
                        split_parts(0, "A", 0, n)
                clear(ks[b])
            for slot in START:
                if slot[0] == "attend A1":
                    dve.wait_ge(const_in, 16 * 7)
                    dve.tensor_copy(row_parts[:, 0, :], row[:, :]).then_inc(row_split, 1)
                    dve.wait_ge(row_split, 1)
                    dve.tensor_tensor(row_rest[:, :], row[:, :], row_parts[:, 0, :], ALU.subtract).then_inc(row_split, 1)
                    dve.wait_ge(row_split, 2)
                    dve.tensor_copy(row_parts[:, 1, :], row_rest[:, :]).then_inc(row_split, 1)
                    dve.wait_ge(row_split, 3)
                    dve.tensor_tensor(row_parts[:, 2, :], row_rest[:, :], row_parts[:, 1, :], ALU.subtract).then_inc(row_split, 1)
                run_slot(0, *slot)
            run_steps(dve, step)
            for slot in TAIL:
                run_slot(TAIL_STEP, *slot)

            def scale_experts(b, par):
                for e in range(TOPK):
                    expert = dve.value_load(taken_i[0:1, bass.ds(b * 8 + e, 1)], min_val=0, max_val=NE - 1)
                    dve.tensor_scalar(w2s[par][:, e, :], w2[:, bass.ds(expert, 1), :].rearrange("p o n -> p (o n)"),
                                      taken_p[:, bass.ds(b * TOPK + e, 1)], None, ALU.mult).then_inc(w2_scaled, 1)

            def last_norm(b, par):
                dve.wait_ge(inv_std["f"], b + 1)
                wait(dve, finished, b - 1)
                alone(dve, passed["dve"])
                for q in range(QT):
                    dve.tensor_scalar(tile_of(normed[par])(q), tile_of(z[par])(q), st[f"f{par}"][1][:, q, 0:1],
                                      st[f"f{par}"][2][:, q:q + 1], ALU.subtract, ALU.mult).then_inc(fn, 1)

            def finish(b, par, scale):
                base = NF * b
                dve.wait_ge(eo_ps, b + 1)
                wait(dve, fn, 2 * (b - 1))
                alone(dve, passed["dve"])
                dve.tensor_tensor(z[par][:, :], o_ps[par][:, 0:T], ys[:, bass.ds(b * T, T)], ALU.add).then_inc(fz, 1)
                if not (known(b) and b == 0):
                    last_norm(b - 1, 1 - par)
                stats(fz, base, 1, tile_of(z[par]), f"f{par}")
                if scale:
                    scale_experts(b + 2, par)
                aggregate(fz, base, 3, f"f{par}")
                add_eps(fz, base, 5, f"f{par}", EPS_OUTER)

            dve.wait_ge(w_in, 32)
            dve.wait_ge(routed[0], 64)
            dve.wait_ge(pv, 4 * len(INSTANCES) - 2)
            for par in range(2):
                scale_experts(par, par)
            end = TAIL_STEP
            normalise(end, "B1", 2, 0)
            invert_sums(end, "B1", 2, 1)
            normalise(end, "B1", 2, 1)
            finish(0, 0, True)
            for part in range(4):
                second_block(end, 2, part)
            finish(1, 1, True)
            second_block(end, 2, 4)
            finish(2, 0, True)
            for part in range(3):
                choose(end, 1, part)
            finish(3, 1, True)
            for part in range(3, 11):
                choose(end, 1, part)
            with dve.Fori(2, NB // 2 - 2) as g:
                for par in range(2):
                    finish(2 * g + par, par, True)
            dve.wait_ge(routed[1], 64)
            for par in range(2):
                finish(NB - 4 + par, par, True)
            for par in range(2):
                finish(NB - 2 + par, par, False)
            last_norm(NB - 1, 1)


def kernel(L0_attn_x, L0_attn_Wq, L0_attn_Wk, L0_attn_Wv, L0_ffn_ln1_g, L0_ffn_ln1_b, L0_ffn_ln2_g, L0_ffn_ln2_b,
           L0_ffn_mha_wq, L0_ffn_mha_bq, L0_ffn_mha_wk, L0_ffn_mha_bk, L0_ffn_mha_wv, L0_ffn_mha_bv, L0_ffn_mha_wo,
           L0_ffn_mha_bo, L0_ffn_mha_rw, L0_ffn_mha_rb, L0_ffn_ffn_rw, L0_ffn_ffn_rb, L0_ffn_fw1, L0_ffn_fw2):
    import numpy as np
    import concourse.bacc as bacc
    from concourse.bass_utils import run_bass_kernel_spmd

    def in_order(w):
        return np.asarray(w).reshape(-1, H, KD)[:, HEAD_ORDER].reshape(-1, D)

    def heads_last(w):
        return np.asarray(w).reshape(-1, H, KD)[:, HEAD_ORDER].swapaxes(1, 2).reshape(-1, D)

    wq, wk, wv, wo = (np.asarray(w) for w in (L0_ffn_mha_wq, L0_ffn_mha_wk, L0_ffn_mha_wv, L0_ffn_mha_wo))
    w_proj = np.concatenate([heads_last(np.asarray(L0_attn_Wq).T), heads_last(np.asarray(L0_attn_Wk).T),
                             in_order(np.asarray(L0_attn_Wv).T)]
                            + [w for m in range(NM) for w in (heads_last(wq[m]), heads_last(wk[m]), in_order(wv[m]))], axis=1)
    cols = np.concatenate([heads_last(L0_ffn_mha_bq).T, heads_last(L0_ffn_mha_bk).T, np.asarray(L0_ffn_mha_bv).reshape(NM, D).T]
                          + [np.asarray(v).reshape(D, 1) for v in (L0_ffn_ln1_g, L0_ffn_ln1_b, L0_ffn_ln2_g, L0_ffn_ln2_b)]
                          + [np.asarray(L0_ffn_mha_rw)], axis=1)
    rows = np.concatenate([np.asarray(L0_ffn_mha_bo).reshape(1, NM * D), np.asarray(L0_ffn_mha_rb).reshape(1, NM)], axis=1)
    arrays = {
        "x": np.asarray(L0_attn_x), "w_proj": w_proj, "w_out": wo.reshape(NM, D, D), "cols": cols, "rows": rows,
        "ffn_rw": np.asarray(L0_ffn_ffn_rw), "ffn_rb": np.asarray(L0_ffn_ffn_rb).reshape(1, NE),
        "fw1": np.asarray(L0_ffn_fw1), "fw2": np.asarray(L0_ffn_fw2),
    }
    arrays = {name: np.ascontiguousarray(a) for name, a in arrays.items()}
    nc = bacc.Bacc("TRN2", target_bir_lowering=False, num_devices=1)
    args = [nc.dram_tensor(name, a.shape, F32, kind="ExternalInput").ap() for name, a in arrays.items()]
    out = nc.dram_tensor("out", (NB, T, D), F32, kind="ExternalOutput").ap()
    sandwich_kernel(nc, *args, out)
    return run_bass_kernel_spmd(nc, [arrays], core_ids=[0]).results[0]["out"]
```
